# Optimizing a Trainium2 kernel written in Bass

```python
import numpy as np
import jax
import jax.numpy as jnp

def _softmax(x, axis=-1):
    return jax.nn.softmax(x, axis=axis)

def _gelu(x):
    return jax.nn.gelu(x, approximate=True)

def _silu(x):
    return jax.nn.silu(x)

def _sigmoid(x):
    return jax.nn.sigmoid(x)

def _layernorm(x, axis=-1, eps=1e-05):
    m = jnp.mean(x, axis=axis, keepdims=True)
    v = jnp.var(x, axis=axis, keepdims=True)
    return (x - m) / jnp.sqrt(v + eps)

def _scatter_add(tgt, idx, src, axis=0):
    return tgt.at[idx].add(src)

def _segment_sum(src, seg, n):
    return jax.ops.segment_sum(src, seg, n)
kernel_name = 'mk_decoder_postln_d2_seqx_r4_119c61'

def setup_inputs(seed: int=0):
    np.random.seed(seed)
    _w = jnp.asarray

    def _rec_inputs():
        import jax
        import jax.numpy as jnp
        _rk = jax.random.key(seed)
        x = 7.22e-05 + 1 * jax.random.normal(jax.random.fold_in(_rk, 1), (2, 512, 512), jnp.float32)
        _lenS = 512 - jax.random.randint(jax.random.fold_in(_rk, 7), (2,), 0, max(1, 512 // 4) + 1, jnp.int32)
        _lenS2 = 1024 - jax.random.randint(jax.random.fold_in(_rk, 8), (2,), 0, max(1, 1024 // 4) + 1, jnp.int32)
        _ctx_2048P = jax.random.normal(jax.random.fold_in(_rk, 11), (2, 16, 512), jnp.float32)
        _ctx_2048c = jax.random.dirichlet(jax.random.fold_in(_rk, 511), 0.3 * jnp.ones((16,), jnp.float32), (2, 1024))
        _ctx_2048t = jnp.einsum('bsk,bkd->bsd', _ctx_2048c, _ctx_2048P)
        _ctx_2048t = _ctx_2048t * jax.lax.rsqrt(jnp.mean(jnp.square(_ctx_2048t)) + 1e-12) * 0.953939
        ctx_2048 = -0.000514642 + 1.00011 * (_ctx_2048t + 0.3 * jax.random.normal(jax.random.fold_in(_rk, 611), (2, 1024, 512), jnp.float32))
        _validS = jnp.arange(512)[None, :] < _lenS[:, None]
        _validS2 = jnp.arange(1024)[None, :] < _lenS2[:, None]
        _causal = jnp.tril(jnp.ones((512, 512), dtype=bool))
        mask_BxS2_bk0 = jnp.logical_not(jnp.broadcast_to(_validS2[:, :], (2, 1024)))
        return (x, ctx_2048, mask_BxS2_bk0)
    x, ctx_2048, mask_BxS2_bk0 = _rec_inputs()

    def _L0_attn_setup():
        import jax, jax.numpy as jnp
        import numpy as np
        D_MODEL = 512
        NUM_HEADS = 16
        HEAD_DIM = D_MODEL // NUM_HEADS
        SCALE = HEAD_DIM ** (-0.5)
        ALPHA = 1.0
        key = jax.random.key(seed)
        ks = jax.random.split(key, 9)
        B, T = (2, 512)
        s = 0.02
        w = lambda k: jax.random.normal(k, (D_MODEL, D_MODEL), jnp.float32) * s
        b = lambda k: jax.random.normal(k, (D_MODEL,), jnp.float32) * s
        return {'x': jax.random.normal(ks[0], (B, T, D_MODEL), jnp.float32), 'q_w': w(ks[1]), 'q_b': b(ks[2]), 'k_w': w(ks[3]), 'k_b': b(ks[4]), 'v_w': w(ks[5]), 'v_b': b(ks[6]), 'o_w': w(ks[7]), 'o_b': b(ks[8])}
    _L0_attn_all = _L0_attn_setup()
    _L0_attn_in = {k: v for k, v in _L0_attn_all.items() if k in ('q_w', 'q_b', 'k_w', 'k_b', 'v_w', 'v_b', 'o_w', 'o_b')}
    del _L0_attn_all

    def _L0_xattn_setup():
        import jax, jax.numpy as jnp
        import numpy as np
        D_MODEL = 512
        NUM_HEADS = 16
        HEAD_DIM = D_MODEL // NUM_HEADS

        def _fq_sym(x, axis):
            s = jnp.max(jnp.abs(x), axis=axis, keepdims=True) / 127.0
            s = jnp.maximum(s, 1e-08)
            q = jnp.clip(jnp.round(x / s), -127.0, 127.0) * s
            return x + jax.lax.stop_gradient(q - x)

        def _fq_unsigned(x, axis):
            s = jnp.max(x, axis=axis, keepdims=True) / 255.0
            s = jnp.maximum(s, 1e-08)
            q = jnp.clip(jnp.round(x / s), 0.0, 255.0) * s
            return x + jax.lax.stop_gradient(q - x)
        key = jax.random.key(seed)
        ks = jax.random.split(key, 8)
        B, N, M, C = (2, 512, 128, D_MODEL)
        return {'x': jax.random.normal(ks[0], (B, N, C), jnp.float32), 'cond': jax.random.normal(ks[1], (B, M, C), jnp.float32), 'Wq': jax.random.normal(ks[2], (C, C), jnp.float32) * 0.02, 'bq': jnp.zeros((C,), jnp.float32), 'Wkv': jax.random.normal(ks[3], (C, 2 * C), jnp.float32) * 0.02, 'bkv': jnp.zeros((2 * C,), jnp.float32), 'Wp': jax.random.normal(ks[4], (C, C), jnp.float32) * 0.02, 'bp': jnp.zeros((C,), jnp.float32)}
    _L0_xattn_all = _L0_xattn_setup()
    _L0_xattn_in = {k: v for k, v in _L0_xattn_all.items() if k in ('Wq', 'bq', 'Wkv', 'bkv', 'Wp', 'bp')}
    del _L0_xattn_all

    def _L0_ffn_setup():
        import jax, jax.numpy as jnp
        import numpy as np
        TOPK = 4
        key = jax.random.key(seed)
        k_x, k_a, k_b, k_w, k_bias = jax.random.split(key, 5)
        b, s, h, j, a, r = (4, 512, 512, 512, 64, 16)
        x = jax.random.normal(k_x, (b, s, h), dtype=jnp.float32)
        A = jax.random.normal(k_a, (a, r, h), dtype=jnp.float32) * 0.02
        B = jax.random.normal(k_b, (a, j, r), dtype=jnp.float32) * 0.02
        W = jax.random.normal(k_w, (j, h), dtype=jnp.float32) * 0.02
        bias = jax.random.normal(k_bias, (j,), dtype=jnp.float32) * 0.02
        return {'x': x, 'A': A, 'B': B, 'W': W, 'bias': bias}
    _L0_ffn_all = _L0_ffn_setup()
    _L0_ffn_in = {k: v for k, v in _L0_ffn_all.items() if k in ('A', 'B', 'W', 'bias')}
    del _L0_ffn_all

    def _L1_attn_setup():
        import jax, jax.numpy as jnp
        import numpy as np
        B, L, D, DI = (4, 1024, 512, 64)
        LN_EPS = 1e-05

        def _scan_dir(z, Wp):
            d = z.shape[-1]
            o = jnp.einsum('bld,de->ble', z, Wp)
            delta = jax.nn.sigmoid(o[..., :d])
            gate = o[..., d:] * z

            def step(h, dg):
                dlt, g = dg
                h = h * dlt + g
                return (h, h)
            h0 = jnp.zeros_like(z[:, 0])
            _, hs = jax.lax.scan(step, h0, (jnp.swapaxes(delta, 0, 1), jnp.swapaxes(gate, 0, 1)))
            return jnp.swapaxes(hs, 0, 1)
        key = jax.random.key(seed)
        ks = jax.random.split(key, 5)
        x = jax.random.normal(ks[0], (B, L, D), jnp.float32)
        W_in = jax.random.normal(ks[1], (D, DI), jnp.float32) * np.float32(1.0 / np.sqrt(D))
        W_fwd = jax.random.normal(ks[2], (DI, 2 * DI), jnp.float32) * np.float32(0.01)
        W_bwd = jax.random.normal(ks[3], (DI, 2 * DI), jnp.float32) * np.float32(0.01)
        W_out = jax.random.normal(ks[4], (2 * DI, D), jnp.float32) * np.float32(1.0 / np.sqrt(2 * DI))
        gamma = jnp.ones((D,), jnp.float32)
        beta = jnp.zeros((D,), jnp.float32)
        return {'x': x, 'W_in': W_in, 'W_fwd': W_fwd, 'W_bwd': W_bwd, 'W_out': W_out, 'gamma': gamma, 'beta': beta}
    _L1_attn_all = _L1_attn_setup()
    _L1_attn_in = {k: v for k, v in _L1_attn_all.items() if k in ('W_in', 'W_fwd', 'W_bwd', 'W_out', 'gamma', 'beta')}
    del _L1_attn_all

    def _L1_xattn_setup():
        import jax, jax.numpy as jnp
        import numpy as np
        H = 512
        NH = 16
        HD = H // NH
        EPS = 1e-06

        def rmsnorm(x, w, eps=EPS):
            var = jnp.mean(x * x, axis=-1, keepdims=True)
            return x * jax.lax.rsqrt(var + eps) * w
        key = jax.random.key(seed)
        ks = jax.random.split(key, 9)
        B, L, M = (4, 1024, 64)
        s = 1.0 / np.sqrt(H)
        return {'hidden_states': jax.random.normal(ks[0], (B, L, H), dtype=jnp.float32), 'memory_tokens': jax.random.normal(ks[1], (B, M, H), dtype=jnp.float32), 'memory_mask': jax.random.randint(ks[2], (B, M), 0, 2).astype(bool), 'norm_w': jnp.ones((H,), dtype=jnp.float32), 'wq': jax.random.normal(ks[3], (H, H), dtype=jnp.float32) * s, 'wk': jax.random.normal(ks[4], (H, H), dtype=jnp.float32) * s, 'wv': jax.random.normal(ks[5], (H, H), dtype=jnp.float32) * s, 'wo': jax.random.normal(ks[6], (H, H), dtype=jnp.float32) * s, 'wg': jax.random.normal(ks[7], (H, H), dtype=jnp.float32) * s}
    _L1_xattn_all = _L1_xattn_setup()
    _L1_xattn_in = {k: v for k, v in _L1_xattn_all.items() if k in ('norm_w', 'wq', 'wk', 'wv', 'wo', 'wg')}
    del _L1_xattn_all

    def _L1_ffn_setup():
        import jax, jax.numpy as jnp
        import numpy as np
        B, S, EMB = (4, 512, 512)
        LAT, HID = (128, 256)
        E, K = (16, 8)
        SCALE = 2.5

        def _w(key, shape, fan_in):
            return jax.random.normal(key, shape, jnp.float32) * fan_in ** (-0.5)

        def _sqrelu(x):
            return jnp.square(jax.nn.relu(x))
        key = jax.random.key(seed)
        ks = jax.random.split(key, 11)
        return {'x': jax.random.normal(ks[0], (B, S, EMB), jnp.float32), 'sw1': _w(ks[1], (HID, EMB), EMB), 'swg': _w(ks[2], (HID, EMB), EMB), 'sw2': _w(ks[3], (EMB, HID), HID), 'rw1': _w(ks[4], (E, HID, LAT), LAT), 'rwg': _w(ks[5], (E, HID, LAT), LAT), 'rw2': _w(ks[6], (E, LAT, HID), HID), 'Wg': _w(ks[7], (E, EMB), EMB), 'Wdown': _w(ks[8], (LAT, EMB), EMB), 'Wup': _w(ks[9], (EMB, LAT), LAT), 'biases': jnp.zeros((E,), jnp.float32)}
    _L1_ffn_all = _L1_ffn_setup()
    _L1_ffn_in = {k: v for k, v in _L1_ffn_all.items() if k in ('sw1', 'swg', 'sw2', 'rw1', 'rwg', 'rw2', 'Wg', 'Wdown', 'Wup', 'biases')}
    del _L1_ffn_all
    return {'x': x, 'ctx_2048': ctx_2048, 'mask_BxS2_bk0': mask_BxS2_bk0, 'L0_attn_q_w': _L0_attn_in['q_w'], 'L0_attn_q_b': _L0_attn_in['q_b'], 'L0_attn_k_w': _L0_attn_in['k_w'], 'L0_attn_k_b': _L0_attn_in['k_b'], 'L0_attn_v_w': _L0_attn_in['v_w'], 'L0_attn_v_b': _L0_attn_in['v_b'], 'L0_attn_o_w': _L0_attn_in['o_w'], 'L0_attn_o_b': _L0_attn_in['o_b'], 'L0_xattn_Wq': _L0_xattn_in['Wq'], 'L0_xattn_bq': _L0_xattn_in['bq'], 'L0_xattn_Wkv': _L0_xattn_in['Wkv'], 'L0_xattn_bkv': _L0_xattn_in['bkv'], 'L0_xattn_Wp': _L0_xattn_in['Wp'], 'L0_xattn_bp': _L0_xattn_in['bp'], 'L0_ffn_A': _L0_ffn_in['A'], 'L0_ffn_B': _L0_ffn_in['B'], 'L0_ffn_W': _L0_ffn_in['W'], 'L0_ffn_bias': _L0_ffn_in['bias'], 'L1_attn_W_in': _L1_attn_in['W_in'], 'L1_attn_W_fwd': _L1_attn_in['W_fwd'], 'L1_attn_W_bwd': _L1_attn_in['W_bwd'], 'L1_attn_W_out': _L1_attn_in['W_out'], 'L1_attn_gamma': _L1_attn_in['gamma'], 'L1_attn_beta': _L1_attn_in['beta'], 'L1_xattn_norm_w': _L1_xattn_in['norm_w'], 'L1_xattn_wq': _L1_xattn_in['wq'], 'L1_xattn_wk': _L1_xattn_in['wk'], 'L1_xattn_wv': _L1_xattn_in['wv'], 'L1_xattn_wo': _L1_xattn_in['wo'], 'L1_xattn_wg': _L1_xattn_in['wg'], 'L1_ffn_sw1': _L1_ffn_in['sw1'], 'L1_ffn_swg': _L1_ffn_in['swg'], 'L1_ffn_sw2': _L1_ffn_in['sw2'], 'L1_ffn_rw1': _L1_ffn_in['rw1'], 'L1_ffn_rwg': _L1_ffn_in['rwg'], 'L1_ffn_rw2': _L1_ffn_in['rw2'], 'L1_ffn_Wg': _L1_ffn_in['Wg'], 'L1_ffn_Wdown': _L1_ffn_in['Wdown'], 'L1_ffn_Wup': _L1_ffn_in['Wup'], 'L1_ffn_biases': _L1_ffn_in['biases']}

def reference(x, ctx_2048, mask_BxS2_bk0, L0_attn_q_w, L0_attn_q_b, L0_attn_k_w, L0_attn_k_b, L0_attn_v_w, L0_attn_v_b, L0_attn_o_w, L0_attn_o_b, L0_xattn_Wq, L0_xattn_bq, L0_xattn_Wkv, L0_xattn_bkv, L0_xattn_Wp, L0_xattn_bp, L0_ffn_A, L0_ffn_B, L0_ffn_W, L0_ffn_bias, L1_attn_W_in, L1_attn_W_fwd, L1_attn_W_bwd, L1_attn_W_out, L1_attn_gamma, L1_attn_beta, L1_xattn_norm_w, L1_xattn_wq, L1_xattn_wk, L1_xattn_wv, L1_xattn_wo, L1_xattn_wg, L1_ffn_sw1, L1_ffn_swg, L1_ffn_sw2, L1_ffn_rw1, L1_ffn_rwg, L1_ffn_rw2, L1_ffn_Wg, L1_ffn_Wdown, L1_ffn_Wup, L1_ffn_biases):
    import jax
    import jax.numpy as jnp

    def _L0_attn_ref(x, q_w, q_b, k_w, k_b, v_w, v_b, o_w, o_b):
        import jax, jax.numpy as jnp
        import numpy as np
        D_MODEL = 512
        NUM_HEADS = 16
        HEAD_DIM = D_MODEL // NUM_HEADS
        SCALE = HEAD_DIM ** (-0.5)
        ALPHA = 1.0
        B, T, D = x.shape
        H, HD = (NUM_HEADS, HEAD_DIM)

        def proj_split(w, bias):
            y = x @ w.T + bias
            return y.reshape(B, T, H, HD).transpose(0, 2, 1, 3).reshape(B * H, T, HD)
        Q = proj_split(q_w, q_b)
        K = proj_split(k_w, k_b)
        V = proj_split(v_w, v_b)
        S = jnp.einsum('hid,hjd->hij', K, Q) * SCALE
        idx = jnp.arange(T)
        delta = idx[:, None] - idx[None, :]
        decay = jnp.where(delta < 0, 0.0, -delta.astype(jnp.float32) ** ALPHA)
        S = jnp.where(delta < 0, -jnp.inf, S) + decay
        C = jax.nn.softmax(S, axis=-1)
        attn = jnp.einsum('hij,hjd->hid', C, V)
        attn = attn.reshape(B, H, T, HD).transpose(0, 2, 1, 3).reshape(B, T, D)
        return attn @ o_w.T + o_b

    def _L0_xattn_ref(x, cond, Wq, bq, Wkv, bkv, Wp, bp):
        import jax, jax.numpy as jnp
        import numpy as np
        D_MODEL = 512
        NUM_HEADS = 16
        HEAD_DIM = D_MODEL // NUM_HEADS

        def _fq_sym(x, axis):
            s = jnp.max(jnp.abs(x), axis=axis, keepdims=True) / 127.0
            s = jnp.maximum(s, 1e-08)
            q = jnp.clip(jnp.round(x / s), -127.0, 127.0) * s
            return x + jax.lax.stop_gradient(q - x)

        def _fq_unsigned(x, axis):
            s = jnp.max(x, axis=axis, keepdims=True) / 255.0
            s = jnp.maximum(s, 1e-08)
            q = jnp.clip(jnp.round(x / s), 0.0, 255.0) * s
            return x + jax.lax.stop_gradient(q - x)
        B, N, C = x.shape
        H, hd = (NUM_HEADS, HEAD_DIM)
        q = (x @ Wq + bq).reshape(1, B * N, H, hd)
        kv = (cond @ Wkv + bkv).reshape(1, -1, 2, H, hd)
        k, v = (kv[:, :, 0], kv[:, :, 1])
        scale = 1.0 / np.sqrt(hd).astype(np.float32)
        q = jnp.transpose(q * scale, (0, 2, 1, 3))
        k = jnp.transpose(k, (0, 2, 1, 3))
        v = jnp.transpose(v, (0, 2, 1, 3))
        q = _fq_sym(q, axis=-1)
        k = _fq_sym(k, axis=-1)
        v = _fq_sym(v, axis=2)
        attn = jnp.einsum('bhqd,bhkd->bhqk', q, k)
        attn = jax.nn.softmax(attn.astype(jnp.float32), axis=-1)
        attn = _fq_unsigned(attn, axis=-1)
        out = jnp.einsum('bhqk,bhkd->bhqd', attn, v)
        out = jnp.transpose(out, (0, 2, 1, 3)).reshape(B, N, C)
        return out @ Wp + bp

    def _L0_ffn_ref(x, A, B, W, bias):
        import jax, jax.numpy as jnp
        import numpy as np
        TOPK = 4
        vecs = jnp.einsum('arh,bsh->bsar', A, x)
        arrows = jnp.linalg.norm(vecs, axis=-1)
        _, idx = jax.lax.top_k(arrows, TOPK)
        routes = jax.nn.one_hot(idx, arrows.shape[-1], dtype=x.dtype).sum(-2) / TOPK
        v = jnp.einsum('bsa,bsar->bsr', routes, vecs)
        delta = jnp.einsum('bsa,ajr,bsr->bsj', routes, B, v)
        base = jnp.einsum('bsh,jh->bsj', x, W) + bias
        return base + delta

    def _L1_attn_ref(x, W_in, W_fwd, W_bwd, W_out, gamma, beta):
        import jax, jax.numpy as jnp
        import numpy as np
        B, L, D, DI = (4, 1024, 512, 64)
        LN_EPS = 1e-05

        def _scan_dir(z, Wp):
            d = z.shape[-1]
            o = jnp.einsum('bld,de->ble', z, Wp)
            delta = jax.nn.sigmoid(o[..., :d])
            gate = o[..., d:] * z

            def step(h, dg):
                dlt, g = dg
                h = h * dlt + g
                return (h, h)
            h0 = jnp.zeros_like(z[:, 0])
            _, hs = jax.lax.scan(step, h0, (jnp.swapaxes(delta, 0, 1), jnp.swapaxes(gate, 0, 1)))
            return jnp.swapaxes(hs, 0, 1)
        z = jnp.einsum('bld,de->ble', x, W_in)
        h_fwd = _scan_dir(z, W_fwd)
        h_bwd = _scan_dir(z[:, ::-1], W_bwd)[:, ::-1]
        out = jnp.einsum('ble,ed->bld', jnp.concatenate([h_fwd, h_bwd], axis=-1), W_out)
        y = out + x
        mu = jnp.mean(y, axis=-1, keepdims=True)
        var = jnp.var(y, axis=-1, keepdims=True)
        return (y - mu) * jax.lax.rsqrt(var + LN_EPS) * gamma + beta

    def _L1_xattn_ref(hidden_states, memory_tokens, memory_mask, norm_w, wq, wk, wv, wo, wg):
        import jax, jax.numpy as jnp
        import numpy as np
        H = 512
        NH = 16
        HD = H // NH
        EPS = 1e-06

        def rmsnorm(x, w, eps=EPS):
            var = jnp.mean(x * x, axis=-1, keepdims=True)
            return x * jax.lax.rsqrt(var + eps) * w
        B, L, C = hidden_states.shape
        M = memory_tokens.shape[1]
        scale = HD ** (-0.5)
        x = rmsnorm(hidden_states, norm_w)
        q = (x @ wq.T).reshape(B, L, NH, HD)
        k = (memory_tokens @ wk.T).reshape(B, M, NH, HD)
        v = (memory_tokens @ wv.T).reshape(B, M, NH, HD)
        attn = jnp.einsum('blhd,bmhd->bhlm', q, k) * scale
        attn = jnp.where(memory_mask[:, None, None, :], attn, -jnp.inf)
        attn = jax.nn.softmax(attn, axis=-1)
        attn = jnp.nan_to_num(attn, nan=0.0)
        out = jnp.einsum('bhlm,bmhd->blhd', attn, v).reshape(B, L, C)
        out = out @ wo.T
        gate = jax.nn.sigmoid(x @ wg.T)
        return gate * out

    def _L1_ffn_ref(x, sw1, swg, sw2, rw1, rwg, rw2, Wg, Wdown, Wup, biases):
        import jax, jax.numpy as jnp
        import numpy as np
        B, S, EMB = (4, 512, 512)
        LAT, HID = (128, 256)
        E, K = (16, 8)
        SCALE = 2.5

        def _w(key, shape, fan_in):
            return jax.random.normal(key, shape, jnp.float32) * fan_in ** (-0.5)

        def _sqrelu(x):
            return jnp.square(jax.nn.relu(x))
        b, s, d = x.shape
        x2 = x.reshape(-1, d)
        shared = x2 @ sw1.T * _sqrelu(x2 @ swg.T) @ sw2.T
        xl = x2 @ Wdown.T
        probas = jax.nn.sigmoid(x2 @ Wg.T)
        _, idx = jax.lax.top_k(probas + biases, K)
        p = jnp.take_along_axis(probas, idx, axis=-1)
        p = p / p.sum(-1, keepdims=True) * SCALE
        T = x2.shape[0]
        w_dense = jnp.zeros((T, E), x2.dtype).at[jnp.arange(T)[:, None], idx].add(p)
        acc = jnp.zeros_like(xl)
        for e in range(E):
            ye = xl @ rw1[e].T * _sqrelu(xl @ rwg[e].T) @ rw2[e].T
            acc = acc + w_dense[:, e:e + 1] * ye
        out = shared + acc @ Wup.T
        return out.reshape(b, s, d)
    x = _layernorm(x + _L0_attn_ref(x, L0_attn_q_w, L0_attn_q_b, L0_attn_k_w, L0_attn_k_b, L0_attn_v_w, L0_attn_v_b, L0_attn_o_w, L0_attn_o_b), axis=-1)
    x = _layernorm(x + _L0_xattn_ref(x, ctx_2048, L0_xattn_Wq, L0_xattn_bq, L0_xattn_Wkv, L0_xattn_bkv, L0_xattn_Wp, L0_xattn_bp), axis=-1)
    x = _layernorm(x + _L0_ffn_ref(x, L0_ffn_A, L0_ffn_B, L0_ffn_W, L0_ffn_bias), axis=-1)
    x = _layernorm(x + _L1_attn_ref(x, L1_attn_W_in, L1_attn_W_fwd, L1_attn_W_bwd, L1_attn_W_out, L1_attn_gamma, L1_attn_beta), axis=-1)
    x = _layernorm(x + _L1_xattn_ref(x, ctx_2048, mask_BxS2_bk0, L1_xattn_norm_w, L1_xattn_wq, L1_xattn_wk, L1_xattn_wv, L1_xattn_wo, L1_xattn_wg), axis=-1)
    x = _layernorm(x + _L1_ffn_ref(x, L1_ffn_sw1, L1_ffn_swg, L1_ffn_sw2, L1_ffn_rw1, L1_ffn_rwg, L1_ffn_rw2, L1_ffn_Wg, L1_ffn_Wdown, L1_ffn_Wup, L1_ffn_biases), axis=-1)
    return x

_drawn_inputs = setup_inputs


def setup_inputs(seed=0):
    import zlib

    import numpy as np

    out = dict(_drawn_inputs(seed))
    spreads = {'L0_xattn_bq': (0.0, 0.522),
     'L0_xattn_bkv': (0.0, 0.1),
     'L0_xattn_bp': (0.0, 0.1),
     'L1_attn_gamma': (1.0, 0.2),
     'L1_attn_beta': (0.0, 0.1),
     'L1_xattn_norm_w': (1.0, 0.2),
     'L1_ffn_biases': (0.0, 0.1)}
    factors = {'L0_attn_q_b': 8.0, 'L0_attn_k_b': 8.0}
    for name, (base, spread) in spreads.items():
        noise = np.random.default_rng([zlib.crc32(name.encode()), seed]).standard_normal(out[name].shape)
        drawn = base * np.exp(spread * noise) if base else spread * noise
        out[name] = jnp.asarray(drawn.astype(out[name].dtype))
    for name, factor in factors.items():
        out[name] = (out[name] * factor).astype(out[name].dtype)
    return out
```

```python
from contextlib import ExitStack

import concourse.bass as bass
from concourse import mybir

F32 = mybir.dt.float32
BF16 = mybir.dt.bfloat16
U8 = mybir.dt.uint8
ALU = mybir.AluOpType
ACT = mybir.ActivationFunctionType
AX_X = mybir.AxisListType.X

P = 128
BATCH, SEQ, CTX, D, HEADS = 2, 512, 1024, 512, 16
HD = D // HEADS
FT = D // P
TOK = BATCH * SEQ
TT = TOK // P
TB = SEQ // P
KEYS = BATCH * CTX
KT = KEYS // P
KB = CTX // P
HALF = TOK // 512
ARROWS, RANK = 64, 16
EXPERTS, LAT, HID, TOPK = 16, 128, 256, 8
DI = 64
SCALE = float(HD) ** -0.5
ROUND = 1.5 * 2.0 ** 23
LN255 = 5.541263545158426
MASKED = -1.0e30
LN_EPS = 1e-5
RMS_EPS = 1e-6
KIB = 1024


def decoder_program(nc, dram, out, stop=6):
    with ExitStack() as ctx:
        base = (nc.sbuf_base + 255) // 256 * 256
        ctx.enter_context(nc.sbuf_tensor("arena", [P, base - nc.sbuf_base + 206 * KIB], U8))

        def at(name, kib, shape, dt=F32):
            return nc.alloc_sbuf_tensor_at(name, shape, dt, offset=base + int(kib * KIB))

        def sem(name):
            return ctx.enter_context(nc.semaphore(name))

        x_tok = at("x_tok", 0, [P, TT, D])
        x_feat = at("x_feat", 16, [P, FT, TOK])
        WA, WB, CONST, BC, R = 32, 72, 112, 118, 134
        ident = at("ident", CONST, [P, P])
        ident_bf = at("ident_bf", CONST + 0.5, [P, P], BF16)
        decay = at("decay", CONST + 0.75, [P, SEQ])
        ln255 = at("ln255", CONST + 2.75, [P, 1])
        eps_ln = at("eps_ln", CONST + 2.8125, [P, 1])
        eps_rms = at("eps_rms", CONST + 2.875, [P, 1])
        stats = at("stats", CONST + 3, [P, TT, 6])
        meanvar = at("meanvar", CONST + 3.25, [P, TT, 2])
        std = at("std", CONST + 3.5, [P, TT])
        rstd = at("rstd", CONST + 3.625, [P, TT])
        ones_f = at("ones_f", CONST + 3.75, [P, HD])
        ones_bf = at("ones_bf", CONST + 4, [P, P], BF16)
        q_bias = at("q_bias", CONST + 4.25, [P, FT])
        k_bias = at("k_bias", CONST + 4.375, [P, FT])
        v_bias2 = at("v_bias2", CONST + 4.5, [P, FT])

        psum = ctx.enter_context(nc.psum_tensor("psum", [P, 8, 512], F32))

        def bank(i):
            return psum[:, i, :]

        SUB = 7
        y_made = [sem(f"y_made{i}") for i in range(SUB)]
        y_added = [sem(f"y_added{i}") for i in range(SUB)]
        var_made = [sem(f"var_made{i}") for i in range(SUB)]
        std_made = [sem(f"std_made{i}") for i in range(SUB)]
        x_normed = [sem(f"x_normed{i}") for i in range(SUB)]
        x_turned = [sem(f"x_turned{i}") for i in range(SUB)]
        xf_made = [sem(f"xf_made{i}") for i in range(SUB)]
        bias_in = [sem(f"bias_in{i}") for i in range(SUB)]
        dve_step = sem("dve_step")
        act_step = sem("act_step")
        pool_step = sem("pool_step")
        consts_in = sem("consts_in")
        consts_set = sem("consts_set")
        out_done = sem("out_done")
        Y0, XT0 = 4, 6

        def pe_turn_x(pe, i, src=x_tok):
            for t in range(TT):
                pe.wait_ge(x_normed[i], t + 1)
                if t >= 2:
                    pe.wait_ge(xf_made[i], t - 1)
                for f in range(FT):
                    ins = nc.tensor.transpose(bank(XT0 + t % 2)[:, f * P:(f + 1) * P],
                                              src[:, t, f * P:(f + 1) * P], ident[:, :])
                ins.then_inc(x_turned[i], 1)

        def act_copy_x(act, i):
            for t in range(TT):
                act.wait_ge(x_turned[i], t + 1)
                nc.scalar.copy(x_feat[:, :, t * P:(t + 1) * P],
                               bank(XT0 + t % 2).rearrange("p (f t) -> p f t", f=FT)
                               ).then_inc(xf_made[i], 1)

        def act_std(act, i):
            for half in range(2):
                act.wait_ge(var_made[i], half + 1)
                nc.scalar.activation(std[:, half * TB:(half + 1) * TB],
                                     meanvar[:, half * TB:(half + 1) * TB, 1], ACT.Sqrt,
                                     bias=eps_ln[:, :]).then_inc(std_made[i], 1)

        sa_wq = at("sa_wq", WA, [P, FT, D])
        sa_wk = at("sa_wk", WA + 8, [P, FT, D])
        sa_wv = at("sa_wv", WA + 16, [P, FT, D])
        sa_wo = at("sa_wo", WA + 32, [P, FT, D])
        sa_vb = at("sa_vb", BC, [P, D])
        sa_ob = at("sa_ob", BC + 2, [P, D])
        sa_q = at("sa_q", R, [P, FT, TOK])
        sa_k = at("sa_k", R + 16, [P, FT, TOK])
        sa_v = at("sa_v", R + 32, [P, TT, D])
        sa_s = at("sa_s", R + 48, [P, 3, SEQ])
        sa_p = at("sa_p", R + 54, [P, 3, SEQ])
        sa_pt = at("sa_pt", R + 60, [P, 3, SEQ])
        sa_nm = at("sa_nm", R + 66, [P, P])
        sa_sum = at("sa_sum", R + 66.5, [P, P])
        sa_rs = at("sa_rs", R + 67, [P, P])
        sa_o = x_feat[:, :, :].rearrange("p f t -> p (f t)").rearrange("p (t d) -> p t d", t=TT)
        sa_of = sa_q
        sa_qkv_in, sa_wo_in, x_in = sem("sa_qkv_in"), sem("sa_wo_in"), sem("x_in")
        sa_lin, sa_lin_out = sem("sa_lin"), sem("sa_lin_out")
        sa_scored, sa_nm_made, sa_p_made = sem("sa_scored"), sem("sa_nm_made"), sem("sa_p_made")
        sa_turned, sa_pt_made, sa_pv = sem("sa_turned"), sem("sa_pt_made"), sem("sa_pv")
        sa_o_made, sa_o_turned, sa_of_made = sem("sa_o_made"), sem("sa_o_turned"), sem("sa_of_made")
        sa_rs_made = sem("sa_rs_made")
        SA_LIN = 3 * 8
        SA_JOBS = BATCH * HEADS * TB

        def sa_unit(n):
            b, h, t = n // (HEADS * TB), n // TB % HEADS, n % TB
            return b, h, t, (t + 1) * P

        qa_ctx = at("qa_ctx", WA, [P, FT, KEYS])
        qa_wp = at("qa_wp", WB, [P, FT, D])
        qa_wq = at("qa_wq", WB + 8, [P, FT, D])
        qa_wkv = at("qa_wkv", WB + 16, [P, FT, 2 * D])
        qa_qb = at("qa_qb", BC + 4, [P, D])
        qa_kb = at("qa_kb", BC + 6, [P, D])
        qa_pb = at("qa_pb", BC + 8, [P, D])
        qa_load, qa_ctx_in = sem("qa_load"), sem("qa_ctx_in")
        REP = HD + 3
        KR = 3 * REP
        qa_kint = at("qa_kint", R, [P, KT, HEADS, REP], BF16)
        qa_v = at("qa_v", R + 18, [P, KT, D], BF16)
        qa_qint = at("qa_qint", R + 34, [P, TT, D], BF16)
        qa_qa = at("qa_qa", R + 42, [3 * HD, TOK], BF16)
        qa_ka = at("qa_ka", R + 44, [3 * HD, KEYS], BF16)
        qa_kb2 = at("qa_kb2", R + 48, [KR, 2, KEYS], BF16)
        qa_qb2 = at("qa_qb2", R + 56, [KR, 2, TOK], BF16)
        qa_e = at("qa_e", R + 60, [P, 4, 512])
        qa_r = at("qa_r", R + 68, [P, 4, 512], BF16)
        qa_vf = at("qa_vf", R + 42, [P, 2, KEYS])
        qa_x1 = at("qa_x1", R + 58, [P, 2, D])
        qa_x2 = at("qa_x2", R + 62, [P, 2, D])
        qa_vint = x_feat[:, :, :].bitcast(BF16)
        qa_of = x_feat
        qa_kt = at("qa_kt", WA + 8, [P, KT, 3, HD], BF16)
        qa_qt = at("qa_qt", WA + 11, [P, TT, 3, REP], BF16)
        qa_krep = at("qa_krep", WA + 36, [P, KT, 3, REP], BF16)
        qa_qrep = at("qa_qrep", BC, [P, TT, 3, HD], BF16)
        qa_t1 = at("qa_t1", WA + 13, [P, KT, HD])
        qa_t2 = at("qa_t2", WA + 15, [P, KT, HD])
        qa_t3 = at("qa_t3", WA + 17, [P, TT, HD])
        qa_t4 = at("qa_t4", WA + 18, [P, TT, HD])
        qa_os = at("qa_os", WA + 19, [P, HALF, 512])
        qa_zs = at("qa_zs", WA + 23, [P, HALF, 512])
        qa_rz = at("qa_rz", WA + 27, [P, HALF, 512])
        qa_mx8 = at("qa_mx8", WA + 31, [P, TT, 4])
        qa_m = at("qa_m", WA + 31.25, [P, 4, TT])
        qa_sq = at("qa_sq", WA + 32, [P, TT, HEADS])
        qa_sk = at("qa_sk", WA + 32.5, [P, KT, HEADS])
        qa_rk = at("qa_rk", WA + 33.5, [P, KT, HEADS])
        qa_rk1 = at("qa_rk1", WA + 34.5, [P, KT, HEADS])
        qa_sv = at("qa_sv", WA + 35.5, [P, FT])
        qa_rv = at("qa_rv", WA + 35.5625, [P, FT])
        qa_sm = at("qa_sm", WA + 35.625, [P, 2, HEADS])
        qa_q, qa_q_out = sem("qa_q"), sem("qa_q_out")
        qa_k, qa_k_out = sem("qa_k"), sem("qa_k_out")
        qa_vl, qa_vl_out = sem("qa_vl"), sem("qa_vl_out")
        qa_v_q, qa_vt, qa_v_made = sem("qa_v_q"), sem("qa_vt"), sem("qa_v_made")
        qa_ints, qa_qt_zero = sem("qa_ints"), sem("qa_qt_zero")
        qa_krep_made, qa_qrep_made = sem("qa_krep_made"), sem("qa_qrep_made")
        qa_kt_made, qa_qt_made, qa_m_made = sem("qa_kt_made"), sem("qa_qt_made"), sem("qa_m_made")
        qa_turned, qa_stack = sem("qa_turned"), sem("qa_stack")
        qa_s, qa_max, qa_st, qa_exp, qa_rnd = sem("qa_s"), sem("qa_max"), sem("qa_st"), sem("qa_exp"), sem("qa_rnd")
        qa_pv, qa_oz, qa_grp = sem("qa_pv"), sem("qa_oz"), sem("qa_grp")
        SU = TT * 4
        EU = HALF * KT
        TURNS = 6

        ff_a = at("ff_a", WB + 8, [P, FT, ARROWS * RANK])
        ff_b = at("ff_b", WB + 24, [P, TT, D])
        ff_w = at("ff_w", WA, [P, FT, D])
        ff_bias = at("ff_bias", BC + 10, [P, D])
        ff_load = sem("ff_load")
        ff_vec = at("ff_vec", R, [P, 2, ARROWS, RANK])
        ff_sq = at("ff_sq", R + 8, [P, ARROWS, RANK])
        ff_rv = at("ff_rv", R + 12, [P, 2, ARROWS * RANK])
        ff_rvt = at("ff_rvt", R + 20, [P, 2, TT, P])
        ff_norm = at("ff_norm", R + 28, [P, ARROWS + 4])
        ff_rep = at("ff_rep", R + 28.5, [P, ARROWS + 4])
        ff_route = at("ff_route", R + 29, [P, ARROWS])
        ff_top = at("ff_top", R + 29.25, [P, 8])
        ff_v = at("ff_v", R + 29.5, [P, RANK])
        ff_vecs, ff_vec_out, ff_rv_made = sem("ff_vecs"), sem("ff_vec_out"), sem("ff_rv_made")
        ff_turned, ff_rvt_made = sem("ff_turned"), sem("ff_rvt_made")

        rc_win = at("rc_win", R + 60, [P, FT, P])
        rc_wd = at("rc_wd", R + 62, [P, P])
        rc_wg = at("rc_wg", R + 62.5, [P, P])
        rc_wout = at("rc_wout", R + 63, [P, D])
        rc_gamma = at("rc_gamma", BC + 12, [P, D])
        rc_beta = at("rc_beta", BC + 14, [P, D])
        rc_load, rc_set = sem("rc_load"), sem("rc_set")
        rc_z = at("rc_z", R, [P, TOK])
        rc_d = at("rc_d", R + 4, [P, TOK])
        rc_g = at("rc_g", R + 8, [P, TOK])
        rc_h = at("rc_h", R + 12, [P, TOK])
        rc_y = at("rc_y", R + 16, [P, TT, D])
        rc_n = at("rc_n", R + 32, [P, TT, D])
        rc_zl, rc_z_out, rc_gl, rc_d_out, rc_h_made = (sem(f"rc_{n}") for n in ("zl", "z_out", "gl", "d_out", "h_made"))
        rc_g_out, rc_yn = sem("rc_g_out"), sem("rc_yn")

        ca_wk = at("ca_wk", WA + 8, [P, FT, D])
        ca_wv = at("ca_wv", WA + 16, [P, FT, D])
        ca_wq = at("ca_wq", WA + 24, [P, FT, D])
        ca_wg = at("ca_wg", WA + 32, [P, FT, D])
        ca_wo = at("ca_wo", WA, [P, FT, D])
        ca_nw = at("ca_nw", BC, [P, D])
        ca_load, ca_ctx_in = sem("ca_load"), sem("ca_ctx_in")
        ca_ctx = at("ca_ctx", WB, [P, FT, CTX])
        ca_k = at("ca_k", WB + 16, [P, FT, CTX])
        ca_q = at("ca_q", WB + 32, [P, FT, SEQ])
        ca_v = at("ca_v", R, [P, KB, HEADS // 2, 3 * HD])
        ca_gate = at("ca_gate", R + 24, [P, TB, D])
        ca_e = at("ca_e", R + 32, [P, 4, 512])
        ca_xn = at("ca_xn", R + 32, [P, TT, D])
        ca_os = at("ca_os", R + 48, [P, 512])
        ca_zs = at("ca_zs", R + 50, [P, 512])
        ca_rz = at("ca_rz", R + 52, [P, 512])
        ca_mrow = at("ca_mrow", R + 54, [P, 2, 512], BF16)
        ca_mb = at("ca_mb", R + 56, [P, 2, 3, TB], BF16)
        ca_m = at("ca_m", R + 56.25, [P, 4, TB])
        ca_mx = at("ca_mx", R + 56.5, [P, TB, 2])
        ca_mask8 = at("ca_mask8", R + 57, [P, KT], U8)
        ca_mask = at("ca_mask", R + 57.0625, [P, KT])
        ca_row8 = at("ca_row8", R + 58, [P, KEYS], U8)
        ca_row = at("ca_row", R + 66, [P, KEYS], BF16)
        ca_tmp = at("ca_tmp", R + 44, [P, 2, D])
        ca_ss = at("ca_ss", R + 57.5, [P, TT])
        ca_rr = at("ca_rr", R + 57.625, [P, TT])
        ca_mask_in, ca_mask_set = sem("ca_mask_in"), sem("ca_mask_set")
        ca_ss_made, ca_rr_made, ca_xn_made = sem("ca_ss_made"), sem("ca_rr_made"), sem("ca_xn_made")
        ca_lin = sem("ca_lin")
        ca_lin_out = sem("ca_lin_out")
        ca_v_out = sem("ca_v_out")
        ca_s, ca_max, ca_m_made, ca_mt, ca_mrow_made = (sem(f"ca_{n}") for n in ("s", "max", "m_made", "mt", "mrow_made"))
        ca_st, ca_exp, ca_pv, ca_oz, ca_grp = (sem(f"ca_{n}") for n in ("st", "exp", "pv", "oz", "grp"))
        CU = TB * 2
        CE = KB

        me_w1 = at("me_w1", WA, [P, EXPERTS, HID])
        me_wg = at("me_wg", WA + 16, [P, EXPERTS, HID])
        me_w2 = at("me_w2", WB, [P, EXPERTS * 2, LAT])
        me_s1 = at("me_s1", WB + 16, [P, FT, HID])
        me_sg = at("me_sg", WB + 20, [P, FT, HID])
        me_s2 = at("me_s2", WB + 24, [P, 2, D])
        me_wd = at("me_wd", WB + 28, [P, FT, LAT])
        me_wu = at("me_wu", WB + 30, [P, D])
        me_wr = at("me_wr", WB + 32, [P, FT, EXPERTS])
        me_bias = at("me_bias", BC + 2, [P, EXPERTS])
        me_load, me_load2 = sem("me_load"), sem("me_load2")
        me_xl = at("me_xl", R, [P, TOK])
        me_us = at("me_us", R + 4, [P, 2, TOK])
        me_u = at("me_u", R + 12, [P, 2, 2, TOK])
        me_rl = at("me_rl", R + 28, [P, 4, 512])
        me_rq = at("me_rq", R + 36, [P, 4, 512])
        me_acc = at("me_acc", R + 44, [P, TT, LAT])
        me_acct = at("me_acct", R + 48, [P, TT, LAT])
        me_pr = at("me_pr", R + 52, [P, TT, EXPERTS])
        me_pb = at("me_pb", R + 52.5, [P, TT, EXPERTS])
        me_rep = at("me_rep", R + 53, [P, TT, EXPERTS])
        me_w = at("me_w", R + 53.5, [P, TT, EXPERTS])
        me_top = at("me_top", R + 54, [P, TT, 8])
        me_sum = at("me_sum", R + 54.25, [P, TT])
        me_rsum = at("me_rsum", R + 54.375, [P, TT])
        me_l, me_l_out, me_r, me_pr_made, me_w_made = (sem(f"me_{n}") for n in ("l", "l_out", "r", "pr_made", "w_made"))
        me_h, me_relu, me_sqr, me_u_made = (sem(f"me_{n}") for n in ("h", "relu", "sqr", "u_made"))
        me_y, me_y_out, me_at, me_at_out = (sem(f"me_{n}") for n in ("y", "y_out", "at", "at_out"))
        ME_UNITS = 4 * (EXPERTS + 1)

        block = ctx.enter_context(nc.Block())

        @block.sync
        def _(sp):
            def load(dst, name, s):
                sp.dma_start(dst, dram[name]).then_inc(s, 16)

            load(x_feat[:, :, :], "x_feat", sa_qkv_in)
            load(sa_wq[:, :, :], "sa_wq", sa_qkv_in)
            load(sa_wk[:, :, :], "sa_wk", sa_qkv_in)
            load(sa_wv[:, :, :], "sa_wv", sa_qkv_in)
            load(q_bias[:, :], "q_b", consts_in)
            load(k_bias[:, :], "k_b", consts_in)
            load(v_bias2[:, :], "qa_vb", consts_in)
            load(ident[:, :], "ident", consts_in)
            load(decay[:, :], "decay", consts_in)
            for dst, name in ((sa_vb, "sa_vb"), (sa_ob, "sa_ob"), (qa_qb, "qa_qb"), (qa_kb, "qa_kb"),
                              (qa_pb, "qa_pb"), (ff_bias, "ff_bias"), (rc_gamma, "rc_gamma"),
                              (rc_beta, "rc_beta")):
                sp.dma_start(dst[:, :], dram[name].partition_broadcast(P)).then_inc(consts_in, 16)
            load(x_tok[:, :, :], "x_tok", x_in)
            load(sa_wo[:, :, :], "sa_wo", sa_wo_in)
            load(qa_wq[:, :, :], "qa_wq", qa_load)
            load(qa_wkv[:, :, :], "qa_wkv", qa_load)
            load(qa_wp[:, :, :], "qa_wp", qa_load)
            sp.wait_ge(sa_lin, SA_LIN)
            load(qa_ctx[:, :, :], "ctx", qa_ctx_in)
            if stop >= 2:
                sp.wait_ge(qa_vl, 16)
                sp.wait_ge(qa_k, KT)
                sp.wait_ge(qa_q, TT)
                load(ff_w[:, :, :], "ff_w", ff_load)
                load(ff_a[:, :, :], "ff_a", ff_load)
                load(ff_b[:, :, :], "ff_b", ff_load)
                sp.wait_ge(y_made[1], TT)
                sp.wait_ge(qa_grp, 2 * HEADS // 4)
                sp.wait_ge(qa_rnd, HEADS * EU)
                sp.wait_ge(rc_set, 1)
                load(rc_win[:, :, 0:DI], "rc_win", rc_load)
                load(rc_win[:, :, DI:P], "rc_win", rc_load)
                load(rc_wd[0:DI, 0:DI], "rc_wf_d", rc_load)
                load(rc_wd[DI:P, DI:P], "rc_wb_d", rc_load)
                load(rc_wg[0:DI, 0:DI], "rc_wf_g", rc_load)
                load(rc_wg[DI:P, DI:P], "rc_wb_g", rc_load)
                load(rc_wout[:, :], "rc_wout", rc_load)
                load(ca_wk[:, :, :], "ca_wk", ca_load)
                load(ca_wv[:, :, :], "ca_wv", ca_load)
                load(ca_wq[:, :, :], "ca_wq", ca_load)
                load(ca_wg[:, :, :], "ca_wg", ca_load)
            if stop >= 3:
                sp.wait_ge(y_made[2], TT)
                load(ca_wo[:, :, :], "ca_wo", ca_load)
                load(ca_ctx[:, :, :], "ctx0", ca_ctx_in)
                sp.dma_start(ca_nw[:, :], dram["ca_nw"].partition_broadcast(P)).then_inc(ca_load, 16)
                sp.dma_start(me_bias[:, :], dram["me_bias"].partition_broadcast(P)).then_inc(ca_load, 16)
            if stop >= 5:
                sp.wait_ge(y_made[3], TT)
                load(ca_mask8[:, :], "mask_tok", ca_mask_in)
                sp.dma_start(ca_row8[:, :], dram["mask_row"].partition_broadcast(P)).then_inc(ca_mask_in, 16)
                sp.wait_ge(ca_lin, 16)
                load(ca_ctx[:, :, :], "ctx1", ca_ctx_in)
            if stop >= 6:
                sp.wait_ge(y_made[5], TT)
                load(me_wd[:, :, :], "me_wd", me_load)
                load(me_wr[:, :, :], "me_wr", me_load)
                load(me_s1[:, :, :], "me_s1", me_load)
                load(me_sg[:, :, :], "me_sg", me_load)
                load(me_w1[:, :, :], "me_w1", me_load2)
                load(me_wg[:, :, :], "me_wg", me_load2)
                load(me_w2[:, :, :], "me_w2", me_load2)
                load(me_s2[:, :, :], "me_s2", me_load2)
                load(me_wu[:, :], "me_wu", me_load2)
            last = {1: 0, 2: 1, 3: 2, 4: 4, 5: 5, 6: 6}[stop]
            for t in range(TT):
                sp.wait_ge(x_normed[last], t + 1)
                sp.dma_start(out[t * P:(t + 1) * P, :], x_tok[:, t, :]).then_inc(out_done, 16)
            sp.wait_ge(out_done, 16 * TT)

        @block.tensor
        def _(pe):
            mm = nc.tensor.matmul

            def linear(o, lhs, rhs):
                for i, (a, b) in enumerate(zip(lhs, rhs)):
                    ins = mm(o, a, b, start=(i == 0), stop=(i == len(lhs) - 1))
                return ins

            def cols(w, a, b):
                return [w[:, k, a:b] for k in range(w.shape[1])]

            def y_bank(i, t):
                if t >= 2:
                    pe.wait_ge(y_added[i], t - 1)
                return bank(Y0 + t % 2)

            pe.wait_ge(sa_qkv_in, 64)
            g = 0
            for w in (sa_wq, sa_wk):
                for m in range(FT):
                    for c in range(HALF):
                        if g >= 4:
                            pe.wait_ge(sa_lin_out, g - 3)
                        linear(bank(g % 4), cols(w, m * P, (m + 1) * P),
                               cols(x_feat, c * 512, (c + 1) * 512)).then_inc(sa_lin, 1)
                        g += 1
            for t in range(TT):
                pe.wait_ge(sa_lin_out, g - 3)
                linear(bank(g % 4), cols(x_feat, t * P, (t + 1) * P), cols(sa_wv, 0, D)).then_inc(sa_lin, 1)
                g += 1
            pe.wait_ge(sa_lin_out, SA_LIN)
            pe.wait_ge(consts_in, 13 * 16)

            def sa_scores(n):
                b, h, t, seen = sa_unit(n)
                r = slice(h % 4 * HD, h % 4 * HD + HD)
                if n >= 3:
                    pe.wait_ge(sa_nm_made, n - 2)
                mm(bank(n % 3)[:, 0:seen], sa_k[r, h // 4, b * SEQ + t * P:b * SEQ + (t + 1) * P],
                   sa_q[r, h // 4, b * SEQ:b * SEQ + seen], start=True, stop=True).then_inc(sa_scored, 1)

            def sa_turn(n):
                b, h, t, seen = sa_unit(n)
                pe.wait_ge(sa_p_made, n + 1)
                if n >= 3:
                    pe.wait_ge(sa_pt_made, n - 2)
                for j in range(t + 1):
                    ins = nc.tensor.transpose(bank(3 + n % 3)[:, j * P:(j + 1) * P],
                                              sa_p[:, n % 3, j * P:(j + 1) * P], ident[:, :])
                ins.then_inc(sa_turned, 1)

            def sa_values(n):
                b, h, t, seen = sa_unit(n)
                u = n // TB
                pe.wait_ge(sa_pt_made, n + 1)
                if t == 0 and u >= 2:
                    pe.wait_ge(sa_o_made, u - 1)
                for j in range(t + 1):
                    ins = mm(bank(6 + u % 2)[:, t * HD:(t + 1) * HD], sa_pt[:, n % 3, j * P:(j + 1) * P],
                             sa_v[:, b * TB + j, h * HD:(h + 1) * HD], start=(j == 0), stop=(j == t))
                ins.then_inc(sa_pv, 1)

            for n in range(SA_JOBS + 4):
                if n < SA_JOBS:
                    sa_scores(n)
                if 2 <= n < SA_JOBS + 2:
                    sa_turn(n - 2)
                if n >= 4:
                    sa_values(n - 4)
            pe.wait_ge(sa_wo_in, 16)
            pe.wait_ge(sa_o_made, BATCH * HEADS)
            for t in range(TT + 1):
                if t < TT:
                    if t >= 3:
                        pe.wait_ge(sa_of_made, t - 2)
                    for f in range(FT):
                        ins = nc.tensor.transpose(bank(t % 3)[:, f * P:(f + 1) * P],
                                                  sa_o[:, t, f * P:(f + 1) * P], ident[:, :])
                    ins.then_inc(sa_o_turned, 1)
                if t >= 1:
                    pe.wait_ge(sa_of_made, t)
                    linear(y_bank(0, t - 1), cols(sa_of, (t - 1) * P, t * P), cols(sa_wo, 0, D)
                           ).then_inc(y_made[0], 1)
            pe_turn_x(pe, 0)
            if stop == 1:
                return

            pe.wait_ge(qa_load, 48)
            for t in range(TT):
                pe.wait_ge(xf_made[0], t + 1)
                if t >= 2:
                    pe.wait_ge(qa_q_out, t - 1)
                linear(bank(t % 2), cols(x_feat, t * P, (t + 1) * P), cols(qa_wq, 0, D)).then_inc(qa_q, 1)
            pe.wait_ge(qa_ctx_in, 16)
            pe.wait_ge(qa_q_out, TT)
            for g in range(16):
                m, c = g // 4, g % 4
                if g >= 2:
                    pe.wait_ge(qa_vl_out, g - 1)
                linear(bank(2 + g % 2), cols(qa_wkv, D + m * P, D + (m + 1) * P),
                       cols(qa_ctx, c * 512, (c + 1) * 512)).then_inc(qa_vl, 1)
            for t in range(KT):
                if t >= 2:
                    pe.wait_ge(qa_k_out, t - 1)
                linear(bank(t % 2), cols(qa_ctx, t * P, (t + 1) * P), cols(qa_wkv, 0, D)).then_inc(qa_k, 1)
            for t in range(KT):
                pe.wait_ge(qa_v_q, FT)
                if t >= 2:
                    pe.wait_ge(qa_v_made, t - 1)
                for m in range(FT):
                    ins = nc.tensor.transpose(bank(6 + t % 2).bitcast(BF16)[:, m * P:(m + 1) * P],
                                              qa_vint[:, m, t * P:(t + 1) * P], ident_bf[:, :])
                ins.then_inc(qa_vt, 1)
            pe.wait_ge(qa_ints, 1)
            pe.wait_ge(qa_v_made, KT)

            turn_bank = bank(6).bitcast(BF16)
            fills = [0]

            def fill(rows, blocks):
                if fills[0]:
                    pe.wait_ge(qa_stack, fills[0])
                for j, src in enumerate(blocks):
                    ins = nc.tensor.transpose(turn_bank[0:rows, j * P:(j + 1) * P], src, ident_bf[:, :])
                ins.then_inc(qa_turned, 1)
                fills[0] += 1

            def fill_qa(h):
                pe.wait_ge(qa_qrep_made, h + 1)
                fill(3 * HD, [qa_qrep[:, t, :, :].rearrange("p a b -> p (a b)") for t in range(TT)])

            def fill_ka(h, half):
                pe.wait_ge(qa_kt_made, h + 1)
                fill(3 * HD, [qa_kt[:, half * 8 + t, :, :].rearrange("p a b -> p (a b)") for t in range(8)])

            def fill_kb(h, half):
                pe.wait_ge(qa_krep_made, h + 1)
                fill(KR, [qa_krep[:, half * 8 + t, :, :].rearrange("p a b -> p (a b)") for t in range(8)])

            def fill_qb(h):
                pe.wait_ge(qa_qt_made, h + 1)
                pe.wait_ge(qa_m_made, h + 1)
                fill(KR, [qa_qt[:, t, :, :].rearrange("p a b -> p (a b)") for t in range(TT)])

            def qa_scores(h, i):
                n = h * SU + i
                t, c = i // 4, i % 4
                if i == 0:
                    pe.wait_ge(qa_stack, 3 if h == 0 else TURNS * h + 3)
                if n >= 2:
                    pe.wait_ge(qa_max, n - 1)
                mm(bank(n % 2), qa_qa[:, t * P:(t + 1) * P], qa_ka[:, c * 512:(c + 1) * 512],
                   start=True, stop=True).then_inc(qa_s, 1)

            def qa_scores_t(h, i):
                n = h * EU + i
                c, k = i // KT, i % KT
                if i == 0:
                    pe.wait_ge(qa_stack, TURNS * (h + 1))
                if n >= 3:
                    pe.wait_ge(qa_exp, n - 2)
                mm(bank(2 + n % 3), qa_kb2[:, h % 2, k * P:(k + 1) * P],
                   qa_qb2[:, h % 2, c * 512:(c + 1) * 512], start=True, stop=True).then_inc(qa_st, 1)

            def qa_values(h, i):
                n = h * EU + i
                c, k = i // KT, i % KT
                r = slice(h % 4 * HD, h % 4 * HD + HD)
                if k == 0 and n > 0:
                    pe.wait_ge(qa_oz, h * HALF + c)
                pe.wait_ge(qa_exp, n + 1)
                mm(bank(7)[r, :], ones_f[:, :], qa_e[:, n % 4, :], start=(k == 0), stop=(k == KT - 1))
                pe.wait_ge(qa_rnd, n + 1)
                mm(bank(5)[r, :], qa_v[:, k, h * HD:(h + 1) * HD], qa_r[:, n % 4, :],
                   start=(k == 0), stop=(k == KT - 1)).then_inc(qa_pv, 1)

            fill_qa(0)
            fill_ka(0, 0)
            fill_ka(0, 1)
            for i in range(SU):
                qa_scores(0, i)
            fill_kb(0, 0)
            fill_kb(0, 1)
            fill_qb(0)
            pe.wait_ge(qa_max, SU)
            fill_qa(1)
            fill_ka(1, 0)
            fill_ka(1, 1)
            for h in range(HEADS):
                for i in range(EU + 2):
                    if i < EU:
                        qa_scores_t(h, i)
                    if i < SU // 2 and h + 1 < HEADS:
                        qa_scores(h + 1, 2 * i)
                        qa_scores(h + 1, 2 * i + 1)
                    if i >= 2:
                        qa_values(h, i - 2)
                    if h + 1 < HEADS:
                        if i == 18:
                            fill_kb(h + 1, 0)
                        if i == 20:
                            fill_kb(h + 1, 1)
                        if i == 22:
                            fill_qb(h + 1)
                    if h + 2 < HEADS:
                        if i == 24:
                            fill_qa(h + 2)
                        if i == 26:
                            fill_ka(h + 2, 0)
                        if i == 28:
                            fill_ka(h + 2, 1)
            pe.wait_ge(qa_grp, 2 * HEADS // 4)
            for t in range(TT):
                linear(y_bank(1, t), cols(qa_of, t * P, (t + 1) * P), cols(qa_wp, 0, D)).then_inc(y_made[1], 1)
            pe_turn_x(pe, 1)
            if stop == 2:
                return

            pe.wait_ge(ff_load, 48)

            def ff_y(t):
                pe.wait_ge(ff_rvt_made, t + 1)
                linear(y_bank(2, t), [ff_rvt[:, t % 2, k, :] for k in range(TT)] + cols(x_feat, t * P, (t + 1) * P),
                       cols(ff_b, 0, D) + cols(ff_w, 0, D)).then_inc(y_made[2], 1)

            def ff_turn(t):
                pe.wait_ge(ff_rv_made, t + 1)
                if t >= 1:
                    pe.wait_ge(ff_rvt_made, t)
                for k in range(TT):
                    ins = nc.tensor.transpose(bank(2 + k // 4)[:, k % 4 * P:(k % 4 + 1) * P],
                                              ff_rv[:, t % 2, k * P:(k + 1) * P], ident[:, :])
                ins.then_inc(ff_turned, 1)

            for t in range(TT + 2):
                if t < TT:
                    pe.wait_ge(xf_made[1], t + 1)
                    if t >= 1:
                        pe.wait_ge(ff_vec_out, t)
                    linear(bank(0), cols(x_feat, t * P, (t + 1) * P), cols(ff_a, 0, 512))
                    linear(bank(1), cols(x_feat, t * P, (t + 1) * P), cols(ff_a, 512, 1024)).then_inc(ff_vecs, 1)
                if 1 <= t <= TT:
                    ff_turn(t - 1)
                if t >= 2:
                    ff_y(t - 2)
            pe_turn_x(pe, 2)
            if stop == 3:
                return

            pe.wait_ge(rc_load, 7 * 16)
            pe.wait_ge(xf_made[2], TT)
            for c in range(HALF):
                linear(bank(c), cols(rc_win, 0, P), cols(x_feat, c * 512, (c + 1) * 512)).then_inc(rc_zl, 1)
            for c in range(HALF):
                pe.wait_ge(rc_z_out, c + 1)
                mm(bank(2 + c), rc_wd[:, :], rc_z[:, c * 512:(c + 1) * 512], start=True, stop=True)
                if c == 0:
                    pe.wait_ge(rc_z_out, 2)
                mm(bank(c), rc_wg[:, :], rc_z[:, c * 512:(c + 1) * 512], start=True, stop=True).then_inc(rc_gl, 1)
            for t in range(TT):
                pe.wait_ge(rc_h_made, 2 * (t // TB + 1))
                mm(y_bank(3, t), rc_h[:, t * P:(t + 1) * P], rc_wout[:, :], start=True, stop=True
                   ).then_inc(y_made[3], 1)
            if stop == 4:
                return

            pe_turn_x(pe, 4, src=ca_xn)
            pe.wait_ge(ca_load, 7 * 16)
            pe.wait_ge(ca_mask_set, 2)
            MT = bank(6).bitcast(BF16)

            def ca_scores(b, h, i):
                n = (b * HEADS + h) * CU + i
                t, c = i // 2, i % 2
                r = slice(h % 4 * HD, h % 4 * HD + HD)
                if n >= 2:
                    pe.wait_ge(ca_max, n - 1)
                mm(bank(n % 2), ca_q[r, h // 4, t * P:(t + 1) * P], ca_k[r, h // 4, c * 512:(c + 1) * 512],
                   start=True, stop=False)
                o = h % 4 * HD
                mm(bank(n % 2), ones_bf[o:o + 1, :], ca_row[o:o + 1, b * CTX + c * 512:b * CTX + (c + 1) * 512],
                   start=False, stop=True).then_inc(ca_s, 1)

            def ca_turn_m(u):
                pe.wait_ge(ca_m_made, u + 1)
                if u >= 1:
                    pe.wait_ge(ca_mrow_made, u)
                o = u % 4 * HD
                for t in range(TB):
                    ins = nc.tensor.transpose(MT[o:o + 3, t * P:(t + 1) * P], ca_mb[:, u % 2, :, t], ident_bf[:, :])
                ins.then_inc(ca_mt, 1)

            def ca_scores_t(b, h, k):
                u = b * HEADS + h
                n = u * CE + k
                r = slice(h % 4 * HD, h % 4 * HD + HD)
                if n >= 3:
                    pe.wait_ge(ca_exp, n - 2)
                if k == 0:
                    pe.wait_ge(ca_mrow_made, u + 1)
                mm(bank(2 + n % 3), ca_k[r, h // 4, k * P:(k + 1) * P], ca_q[r, h // 4, :], start=True, stop=False)
                mm(bank(2 + n % 3), ones_bf[r.start:r.start + 3, :], ca_mrow[r.start:r.start + 3, u % 2, :], start=False, stop=True).then_inc(ca_st, 1)

            def ca_values(b, h, k):
                u = b * HEADS + h
                n = u * CE + k
                if k == 0 and u >= 2:
                    pe.wait_ge(ca_oz, 2 * (u - 1))
                pe.wait_ge(ca_exp, n + 1)
                o = (5, 7)[u % 2]
                mm(bank(o)[0:2 * HD, :], ca_v[:, k, h // 2, h % 2 * HD:h % 2 * HD + 2 * HD], ca_e[:, n % 4, :],
                   start=(k == 0), stop=(k == KB - 1)).then_inc(ca_pv, 1)

            for b in range(BATCH):
                pe.wait_ge(ca_ctx_in, 16 * (b + 1))
                if b == 0:
                    pe.wait_ge(xf_made[4], TT)
                else:
                    pe.wait_ge(ca_exp, HEADS * CE)
                g = 24 * b

                def lin_bank(g):
                    if g >= 4 and g % 24 >= 4:
                        pe.wait_ge(ca_lin_out, g - 3)
                    return bank(g % 4)

                for m in range(FT):
                    for c in range(2):
                        linear(lin_bank(g), cols(ca_wk, m * P, (m + 1) * P),
                               cols(ca_ctx, c * 512, (c + 1) * 512)).then_inc(ca_lin, 1)
                        g += 1
                for t in range(KB):
                    linear(lin_bank(g), cols(ca_ctx, t * P, (t + 1) * P), cols(ca_wv, 0, D)).then_inc(ca_lin, 1)
                    g += 1
                for m in range(FT):
                    linear(lin_bank(g), cols(ca_wq, m * P, (m + 1) * P),
                           cols(x_feat, b * SEQ, (b + 1) * SEQ)).then_inc(ca_lin, 1)
                    g += 1
                for t in range(TB):
                    linear(lin_bank(g), cols(x_feat, (b * TB + t) * P, (b * TB + t + 1) * P),
                           cols(ca_wg, 0, D)).then_inc(ca_lin, 1)
                    g += 1
                pe.wait_ge(ca_lin_out, g)
                for h in range(2):
                    for i in range(CU):
                        ca_scores(b, h, i)
                    if h == 0:
                        ca_turn_m(b * HEADS)
                for h in range(HEADS):
                    u = b * HEADS + h
                    for i in range(CE + 2):
                        if i < CE:
                            ca_scores_t(b, h, i)
                            if h + 2 < HEADS:
                                ca_scores(b, h + 2, i)
                        if i >= 2:
                            ca_values(b, h, i - 2)
                        if i == 3 and h + 1 < HEADS:
                            ca_turn_m(u + 1)
                pe.wait_ge(ca_grp, 4 * (b + 1))
                for t in range(b * TB, (b + 1) * TB):
                    linear(y_bank(5, t), cols(x_feat, t * P, (t + 1) * P), cols(ca_wo, 0, D)).then_inc(y_made[5], 1)
            pe_turn_x(pe, 5)
            if stop == 5:
                return

            pe.wait_ge(me_load, 64)
            pe.wait_ge(xf_made[5], TT)
            for c in range(HALF):
                linear(bank(c), cols(me_wd, 0, LAT), cols(x_feat, c * 512, (c + 1) * 512)).then_inc(me_l, 1)
            for t in range(TT):
                ins = linear(bank(2)[:, t * EXPERTS:(t + 1) * EXPERTS], cols(x_feat, t * P, (t + 1) * P),
                             cols(me_wr, 0, EXPERTS))
            ins.then_inc(me_r, 1)
            pe.wait_ge(me_l_out, HALF)
            pe.wait_ge(me_pr_made, 1)

            def me_hidden(e, i):
                n = 4 * e + i
                m, c = i // 2, i % 2
                if n >= 2:
                    pe.wait_ge(me_u_made, n - 1)
                for which, (shared, routed) in enumerate(((me_s1, me_w1), (me_sg, me_wg))):
                    if e == 0:
                        ins = linear(bank(which * 2 + n % 2), cols(shared, m * P, (m + 1) * P),
                                     cols(x_feat, c * 512, (c + 1) * 512))
                    else:
                        ins = mm(bank(which * 2 + n % 2), routed[:, e - 1, m * P:(m + 1) * P],
                                 me_xl[:, c * 512:(c + 1) * 512], start=True, stop=True)
                ins.then_inc(me_h, 1)

            def me_out(e, half):
                n = 2 * (e - 1) + half
                if half == 0:
                    pe.wait_ge(me_u_made, 4 * (e + 1))
                if n >= 2:
                    pe.wait_ge(me_y_out, (n - 1) * TB)
                for t in range(TB):
                    tt = half * TB + t
                    ins = linear(bank(4 + n % 2)[:, t * LAT:(t + 1) * LAT],
                                 [me_u[:, e % 2, m, tt * P:(tt + 1) * P] for m in range(2)],
                                 [me_w2[:, 2 * (e - 1) + m, :] for m in range(2)])
                ins.then_inc(me_y, 1)

            for e in range(EXPERTS + 1):
                if e == 1:
                    pe.wait_ge(me_load2, 5 * 16)
                for i in range(4):
                    me_hidden(e, i)
                    if i % 2 == 1 and e >= 2:
                        me_out(e - 1, i // 2)
            me_out(EXPERTS, 0)
            me_out(EXPERTS, 1)
            pe.wait_ge(me_y_out, EXPERTS * TT)
            for t in range(TT):
                ins = nc.tensor.transpose(bank(t // 4)[:, t % 4 * P:(t % 4 + 1) * P], me_acc[:, t, :], ident[:, :])
                if t % 4 == 3:
                    ins.then_inc(me_at, 1)
            for t in range(TT):
                pe.wait_ge(me_at_out, t // 4 + 1)
                linear(y_bank(6, t), [me_us[:, m, t * P:(t + 1) * P] for m in range(2)] + [me_acct[:, t, :]],
                       [me_s2[:, m, :] for m in range(2)] + [me_wu[:, :]]).then_inc(y_made[6], 1)

        @block.vector
        def _(dve):
            v = nc.vector
            steps = [0]

            def step(ins):
                steps[0] += 1
                ins.then_inc(dve_step, 1)
                dve.wait_ge(dve_step, steps[0])

            def norm_half(i, half, src, dst, rel=None):
                dve.wait_ge(std_made[i], half + 1)
                step(v.reciprocal(rstd[:, half * TB:(half + 1) * TB], std[:, half * TB:(half + 1) * TB]))
                for t in range(half * TB, (half + 1) * TB):
                    v.tensor_scalar(dst[:, t, :], src[:, t, :], meanvar[:, t, 0:1], rstd[:, t:t + 1],
                                    ALU.subtract, ALU.mult).then_inc(x_normed[i], 1)

            def tile_stats(i, t, src):
                step(v.bn_stats(stats[:, t, :], src[:, t, :]))
                ins = v.bn_aggr(meanvar[:, t, :], stats[:, t, :])
                if t % TB == TB - 1:
                    ins.then_inc(var_made[i], 1)

            def add_tile(i, t, bias=True):
                if bias:
                    dve.wait_ge(bias_in[i], t + 1)
                dve.wait_ge(y_made[i], t + 1)
                v.tensor_tensor(x_tok[:, t, :], bank(Y0 + t % 2), x_tok[:, t, :], ALU.add).then_inc(y_added[i], 1)
                dve.wait_ge(y_added[i], t + 1)
                tile_stats(i, t, x_tok)

            def add_and_norm(i, bias=True):
                for t in range(TT):
                    add_tile(i, t, bias)
                for half in range(2):
                    norm_half(i, half, x_tok, x_tok)

            v.memset(ln255[:, :], LN255).then_inc(consts_set, 1)
            v.memset(eps_ln[:, :], LN_EPS).then_inc(consts_set, 1)
            v.memset(eps_rms[:, :], RMS_EPS).then_inc(consts_set, 1)
            v.memset(ones_f[:, :], 1.0).then_inc(consts_set, 1)
            v.memset(ones_bf[:, :], 1.0).then_inc(consts_set, 1)
            dve.wait_ge(consts_in, 13 * 16)
            v.tensor_copy(ident_bf[:, :], ident[:, :]).then_inc(consts_set, 1)

            for g in range(SA_LIN):
                dve.wait_ge(sa_lin, g + 1)
                if g < 8:
                    v.tensor_scalar(sa_q[:, g // 2, g % 2 * 512:(g % 2 + 1) * 512], bank(g % 4),
                                    q_bias[:, g // 2:g // 2 + 1], -SCALE, ALU.add, ALU.mult
                                    ).then_inc(sa_lin_out, 1)
                elif g < 16:
                    m = g // 2 - 4
                    v.tensor_scalar(sa_k[:, m, g % 2 * 512:(g % 2 + 1) * 512], bank(g % 4),
                                    k_bias[:, m:m + 1], None, ALU.add).then_inc(sa_lin_out, 1)
                else:
                    v.tensor_tensor(sa_v[:, g - 16, :], bank(g % 4), sa_vb[:, :], ALU.add
                                    ).then_inc(sa_lin_out, 1)

            def sa_finish(u):
                b, h = u // HEADS, u % HEADS
                dve.wait_ge(sa_p_made, TB * (u + 1))
                v.reciprocal(sa_rs[:, TB * u:TB * (u + 1)], sa_sum[:, TB * u:TB * (u + 1)]).then_inc(sa_rs_made, 1)
                dve.wait_ge(sa_rs_made, u + 1)
                dve.wait_ge(sa_pv, TB * (u + 1))
                v.tensor_tensor(sa_o[:, b * TB:(b + 1) * TB, h * HD:(h + 1) * HD],
                                bank(6 + u % 2)[:, 0:P].rearrange("p (t d) -> p t d", t=TB),
                                sa_rs[:, TB * u:TB * (u + 1)].unsqueeze(2).broadcast_to([P, TB, HD]),
                                ALU.mult).then_inc(sa_o_made, 1)

            for n in range(SA_JOBS):
                b, h, t, seen = sa_unit(n)
                dve.wait_ge(sa_scored, n + 1)
                if n >= 3:
                    dve.wait_ge(sa_p_made, n - 2)
                v.tensor_tensor_reduce(sa_s[:, n % 3, 0:seen], bank(n % 3)[:, 0:seen],
                                       decay[:, SEQ - seen:SEQ], 1.0, 3.0e38, ALU.add, ALU.min,
                                       sa_nm[:, n:n + 1]).then_inc(sa_nm_made, 1)
                if n % TB == 0 and n >= 2 * TB:
                    sa_finish(n // TB - 2)
            for u in range(BATCH * HEADS - 2, BATCH * HEADS):
                sa_finish(u)
            add_and_norm(0)
            if stop == 1:
                return

            def quantise(src, n_tile, scale, s_all, r_all, dst):
                x3 = src.rearrange("p (h d) -> p h d", h=HEADS)
                step(v.tensor_reduce(qa_sm[:, 0, :], x3, AX_X, ALU.max, apply_absolute_value=True))
                step(v.tensor_scalar(qa_sm[:, 1, :], qa_sm[:, 0, :], scale, 1.0 / 127.0, ALU.mult, ALU.mult))
                step(v.tensor_scalar(s_all, qa_sm[:, 1, :], 1e-8, None, ALU.max))
                step(v.reciprocal(r_all, s_all))
                t3 = qa_x2[:, n_tile % 2, :].rearrange("p (h d) -> p h d", h=HEADS)
                step(v.scalar_tensor_tensor(t3, x3, scale, r_all.unsqueeze(2).broadcast_to([P, HEADS, HD]),
                                            ALU.mult, ALU.mult))
                step(v.tensor_scalar(x3, t3, ROUND, -ROUND, ALU.add, ALU.add))
                step(v.tensor_scalar(dst, x3, 127.0, -127.0, ALU.min, ALU.max))

            for t in range(TT):
                dve.wait_ge(qa_q, t + 1)
                v.tensor_tensor(qa_x1[:, t % 2, :], bank(t % 2), qa_qb[:, :], ALU.add).then_inc(qa_q_out, 1)
                dve.wait_ge(qa_q_out, t + 1)
                quantise(qa_x1[:, t % 2, :], t, SCALE, qa_sq[:, t, :], qa_rk1[:, t, :],
                         qa_qint[:, t, :].rearrange("p (h d) -> p h d", h=HEADS))
            for m in range(FT):
                dve.wait_ge(qa_vl_out, 4 * (m + 1))
                vf = qa_vf[:, m % 2, :]
                step(v.tensor_reduce(qa_sm[:, 0, 0:1], vf, AX_X, ALU.max, apply_absolute_value=True))
                step(v.tensor_scalar(qa_sv[:, m:m + 1], qa_sm[:, 0, 0:1], 1.0 / 127.0, 1e-8, ALU.mult, ALU.max))
                step(v.reciprocal(qa_rv[:, m:m + 1], qa_sv[:, m:m + 1]))
                step(v.tensor_scalar(vf, vf, qa_rv[:, m:m + 1], 127.0, ALU.mult, ALU.min))
                step(v.tensor_scalar(vf, vf, -127.0, ROUND, ALU.max, ALU.add))
                v.tensor_scalar(qa_vint[:, m, :], vf, -ROUND, None, ALU.add).then_inc(qa_v_q, 1)
            for t in range(KT):
                dve.wait_ge(qa_k, t + 1)
                v.tensor_tensor(qa_x1[:, t % 2, :], bank(t % 2), qa_kb[:, :], ALU.add).then_inc(qa_k_out, 1)
                dve.wait_ge(qa_k_out, t + 1)
                quantise(qa_x1[:, t % 2, :], t, 1.0, qa_sk[:, t, :], qa_rk[:, t, :], qa_kint[:, t, :, 0:HD])
            step(v.tensor_copy(qa_kint[:, :, :, HD], qa_rk[:, :, :]))
            step(v.tensor_tensor(qa_rk1[:, :, :], qa_rk[:, :, :], qa_kint[:, :, :, HD], ALU.subtract))
            step(v.tensor_copy(qa_kint[:, :, :, HD + 1], qa_rk1[:, :, :]))
            v.tensor_tensor(qa_kint[:, :, :, HD + 2], qa_rk1[:, :, :], qa_kint[:, :, :, HD + 1],
                            ALU.subtract).then_inc(qa_ints, 1)

            def qa_maximum(h, i):
                n = h * SU + i
                dve.wait_ge(qa_s, n + 1)
                v.tensor_reduce(qa_mx8[:, i // 4, i % 4:i % 4 + 1], bank(n % 2), AX_X, ALU.max).then_inc(qa_max, 1)

            def qa_splits(h):
                dve.wait_ge(qa_max, SU * (h + 1))
                if h >= 1:
                    dve.wait_ge(qa_turned, TURNS * h)
                step(v.tensor_reduce(qa_m[:, 0, :], qa_mx8[:, :, :], AX_X, ALU.max))
                step(v.scalar_tensor_tensor(qa_m[:, 1, :], qa_m[:, 0, :], -1.0, qa_sq[:, :, h], ALU.mult, ALU.mult))
                m1 = qa_m[:, 1, :].unsqueeze(2)
                step(v.tensor_copy(qa_qt[:, :, 0, HD:REP], m1.broadcast_to([P, TT, 3])))
                step(v.tensor_tensor(qa_m[:, 2, :], qa_m[:, 1, :], qa_qt[:, :, 0, HD], ALU.subtract))
                step(v.tensor_copy(qa_qt[:, :, 1, HD:REP - 1], qa_m[:, 2, :].unsqueeze(2).broadcast_to([P, TT, 2])))
                v.tensor_tensor(qa_qt[:, :, 2, HD], qa_m[:, 2, :], qa_qt[:, :, 1, HD], ALU.subtract
                                ).then_inc(qa_m_made, 1)

            def qa_round(h, i):
                n = h * EU + i
                dve.wait_ge(qa_exp, n + 1)
                if n >= 4:
                    dve.wait_ge(qa_pv, n - 3)
                v.tensor_scalar(qa_r[:, n % 4, :], qa_e[:, n % 4, :], ROUND, -ROUND, ALU.add, ALU.add
                                ).then_inc(qa_rnd, 1)

            def qa_group(h):
                dve.wait_ge(qa_oz, HALF * (h + 1))
                for c in range(HALF):
                    step(v.reciprocal(qa_rz[:, c, :], qa_zs[:, c, :]))
                    v.scalar_tensor_tensor(qa_of[:, h // 4, c * 512:(c + 1) * 512], qa_os[:, c, :],
                                           qa_sv[:, h // 4:h // 4 + 1], qa_rz[:, c, :], ALU.mult, ALU.mult
                                           ).then_inc(qa_grp, 1)

            def qa_repeat_k(h):
                if h >= 1:
                    dve.wait_ge(qa_turned, TURNS * (h - 1) + 5)
                v.tensor_copy(qa_krep[:, :, :, :], qa_kint[:, :, h, :].unsqueeze(2).broadcast_to([P, KT, 3, REP])
                              ).then_inc(qa_krep_made, 1)

            def qa_repeat_q(h):
                if h >= 1:
                    dve.wait_ge(qa_turned, TURNS * (h - 1) + 1)
                v.tensor_copy(qa_qrep[:, :, :, :], qa_qint[:, :, h * HD:(h + 1) * HD].unsqueeze(2)
                              .broadcast_to([P, TT, 3, HD])).then_inc(qa_qrep_made, 1)

            dve.wait_ge(qa_ctx_in, 16)
            dve.wait_ge(qa_k, KT)
            dve.wait_ge(qa_ints, 1)
            qa_repeat_k(0)
            qa_repeat_q(0)
            qa_repeat_q(1)
            v.memset(qa_qt[:, :, :, :], 0.0).then_inc(qa_qt_zero, 1)
            dve.wait_ge(qa_vt, KT)
            for i in range(SU):
                qa_maximum(0, i)
            qa_splits(0)
            for h in range(HEADS):
                for i in range(EU):
                    if i < SU // 2 and h + 1 < HEADS:
                        qa_maximum(h + 1, 2 * i)
                        qa_maximum(h + 1, 2 * i + 1)
                    qa_round(h, i)
                    if i == SU // 2 and h + 1 < HEADS:
                        qa_splits(h + 1)
                    if i == 4 and h % 4 == 0 and h > 0:
                        qa_group(h - 1)
                    if i == 12 and h + 1 < HEADS:
                        qa_repeat_k(h + 1)
                    if i == 20 and h + 2 < HEADS:
                        qa_repeat_q(h + 2)
            qa_group(HEADS - 1)
            dve.wait_ge(y_made[0], TT)
            dve.wait_ge(qa_pv, HEADS * EU)
            step(v.memset(rc_wd[:, :], 0.0))
            v.memset(rc_wg[:, :], 0.0).then_inc(rc_set, 1)
            add_and_norm(1)
            if stop == 2:
                return

            step(v.memset(ff_norm[:, ARROWS:], -1.0))
            for t in range(TT):
                dve.wait_ge(ff_vec_out, t + 1)
                vec = ff_vec[:, t % 2, :, :]
                step(v.tensor_tensor(ff_sq[:, :, :], vec, vec, ALU.mult))
                step(v.tensor_reduce(ff_norm[:, 0:ARROWS], ff_sq[:, :, :], AX_X, ALU.add))
                step(v.max(ff_top[:, :], ff_norm[:, :]))
                step(v.memset(ff_top[:, 4:8], -1.0))
                step(v.match_replace(ff_rep[:, :], ff_top[:, :], ff_norm[:, :], -2.0))
                step(v.tensor_scalar(ff_route[:, :], ff_rep[:, 0:ARROWS], -2.0, 0.25, ALU.is_equal, ALU.mult))
                route = ff_route[:, :].unsqueeze(2).broadcast_to([P, ARROWS, RANK])
                step(v.tensor_tensor(ff_sq[:, :, :], vec, route, ALU.mult))
                step(v.tensor_reduce(ff_v[:, :], ff_sq[:, :, :].rearrange("p a r -> p r a"), AX_X, ALU.add))
                if t >= 2:
                    dve.wait_ge(ff_turned, t - 1)
                v.tensor_tensor(ff_rv[:, t % 2, :].rearrange("p (a r) -> p a r", a=ARROWS), route,
                                ff_v[:, :].unsqueeze(1).broadcast_to([P, ARROWS, RANK]), ALU.mult
                                ).then_inc(ff_rv_made, 1)
                if t >= 2:
                    add_tile(2, t - 2)
            add_tile(2, TT - 2)
            add_tile(2, TT - 1)
            for half in range(2):
                norm_half(2, half, x_tok, x_tok)
            if stop == 3:
                return

            for c in range(HALF):
                dve.wait_ge(rc_gl, c + 1)
                v.tensor_tensor(rc_g[:, c * 512:(c + 1) * 512], bank(c), rc_z[:, c * 512:(c + 1) * 512],
                                ALU.mult).then_inc(rc_g_out, 1)
                dve.wait_ge(rc_g_out, c + 1)
                dve.wait_ge(rc_d_out, c + 1)
                lo, hi = c * SEQ, (c + 1) * SEQ
                v.tensor_tensor_scan(rc_h[0:DI, lo:hi], rc_d[0:DI, lo:hi], rc_g[0:DI, lo:hi], 0.0,
                                     ALU.mult, ALU.add).then_inc(rc_h_made, 1)
                back = slice(hi - 1, lo - 1 if lo else None, -1)
                v.tensor_tensor_scan(rc_h[DI:P, back], rc_d[DI:P, back], rc_g[DI:P, back], 0.0,
                                     ALU.mult, ALU.add).then_inc(rc_h_made, 1)
            for t in range(TT):
                dve.wait_ge(y_made[3], t + 1)
                v.tensor_tensor(rc_y[:, t, :], bank(Y0 + t % 2), x_tok[:, t, :], ALU.add).then_inc(y_added[3], 1)
                dve.wait_ge(y_added[3], t + 1)
                tile_stats(3, t, rc_y)
            for half in range(2):
                norm_half(3, half, rc_y, rc_n)
                for t in range(half * TB, (half + 1) * TB):
                    dve.wait_ge(x_normed[3], t + 1)
                    step(v.tensor_tensor(rc_n[:, t, :], rc_n[:, t, :], rc_gamma[:, :], ALU.mult))
                    step(v.tensor_tensor(rc_n[:, t, :], rc_n[:, t, :], rc_beta[:, :], ALU.add))
                    step(v.tensor_tensor(x_tok[:, t, :], rc_n[:, t, :], x_tok[:, t, :], ALU.add))
            for t in range(TT):
                tile_stats(4, t, x_tok)
            if stop == 4:
                for half in range(2):
                    norm_half(4, half, x_tok, x_tok)
                return
            for half in range(2):
                dve.wait_ge(std_made[4], half + 1)
                step(v.reciprocal(rstd[:, half * TB:(half + 1) * TB], std[:, half * TB:(half + 1) * TB]))
                for t in range(half * TB, (half + 1) * TB):
                    v.tensor_scalar(x_tok[:, t, :], x_tok[:, t, :], meanvar[:, t, 0:1], rstd[:, t:t + 1],
                                    ALU.subtract, ALU.mult).then_inc(ca_ss_made, 1)
            dve.wait_ge(ca_rr_made, 1)
            step(v.reciprocal(ca_rr[:, :], ca_ss[:, :]))
            dve.wait_ge(ca_load, 7 * 16)
            for t in range(TT):
                v.scalar_tensor_tensor(ca_xn[:, t, :], x_tok[:, t, :], ca_rr[:, t:t + 1], ca_nw[:, :],
                                       ALU.mult, ALU.mult).then_inc(x_normed[4], 1)
            dve.wait_ge(ca_mask_in, 32)
            v.tensor_scalar(ca_mask[:, :], ca_mask8[:, :], -1.0, -MASKED, ALU.add, ALU.mult).then_inc(ca_mask_set, 1)
            v.tensor_scalar(ca_row[:, :], ca_row8[:, :], -1.0, -MASKED, ALU.add, ALU.mult).then_inc(ca_mask_set, 1)

            step(v.memset(ca_v[:, :, :, HD:2 * HD], 1.0))

            def ca_maximum(b, h, i):
                n = (b * HEADS + h) * CU + i
                dve.wait_ge(ca_s, n + 1)
                v.tensor_reduce(ca_mx[:, i // 2, i % 2:i % 2 + 1], bank(n % 2), AX_X, ALU.max).then_inc(ca_max, 1)

            def ca_splits(b, h):
                u = b * HEADS + h
                dve.wait_ge(ca_max, CU * (u + 1))
                if u >= 2:
                    dve.wait_ge(ca_mt, u - 1)
                step(v.tensor_reduce(ca_m[:, 0, :], ca_mx[:, :, :], AX_X, ALU.max))
                step(v.tensor_scalar(ca_m[:, 1, :], ca_m[:, 0, :], -1.0e20, -1.0, ALU.max, ALU.mult))
                mb = ca_mb[:, u % 2, :, :]
                step(v.tensor_copy(mb[:, 0, :], ca_m[:, 1, :]))
                step(v.tensor_tensor(ca_m[:, 2, :], ca_m[:, 1, :], mb[:, 0, :], ALU.subtract))
                step(v.tensor_copy(mb[:, 1, :], ca_m[:, 2, :]))
                v.tensor_tensor(mb[:, 2, :], ca_m[:, 2, :], mb[:, 1, :], ALU.subtract).then_inc(ca_m_made, 1)

            def ca_group(u):
                b, h = u // HEADS, u % HEADS
                dve.wait_ge(ca_oz, 2 * (u + 1))
                step(v.tensor_scalar(ca_rz[:, :], ca_zs[:, :], 1.0e-30, None, ALU.max))
                step(v.reciprocal(ca_rz[:, :], ca_rz[:, :]))
                v.tensor_tensor(x_feat[:, h // 4, b * SEQ:(b + 1) * SEQ], ca_os[:, :], ca_rz[:, :], ALU.mult
                                ).then_inc(ca_grp, 1)

            for b in range(BATCH):
                for t in range(KB):
                    g = 24 * b + 8 + t
                    dve.wait_ge(ca_lin, g + 1)
                    dve.wait_ge(ca_lin_out, g)
                    v.tensor_copy(ca_v[:, t, :, :].rearrange("p j (a d) -> p j a d", a=3)[:, :, 0:3:2, :],
                                  bank(g % 4).rearrange("p (j a d) -> p j a d", j=HEADS // 2, a=2)
                                  ).then_inc(ca_lin_out, 1)
                for h in range(2):
                    for i in range(CU):
                        ca_maximum(b, h, i)
                    ca_splits(b, h)
                for h in range(HEADS):
                    if h + 2 < HEADS:
                        for i in range(CU):
                            ca_maximum(b, h + 2, i)
                        ca_splits(b, h + 2)
                    if h % 4 == 0 and h > 0:
                        ca_group(b * HEADS + h - 1)
                ca_group(b * HEADS + HEADS - 1)
                for t in range(b * TB, (b + 1) * TB):
                    dve.wait_ge(y_made[5], t + 1)
                    v.tensor_tensor(ca_tmp[:, t % 2, :], bank(Y0 + t % 2), ca_gate[:, t % TB, :], ALU.mult
                                    ).then_inc(y_added[5], 1)
                    dve.wait_ge(y_added[5], t + 1)
                    step(v.tensor_tensor(x_tok[:, t, :], ca_tmp[:, t % 2, :], x_tok[:, t, :], ALU.add))
                    tile_stats(5, t, x_tok)
            for half in range(2):
                norm_half(5, half, x_tok, x_tok)
            if stop == 5:
                return

            dve.wait_ge(me_pr_made, 1)
            step(v.tensor_tensor(me_pb[:, :, :], me_pr[:, :, :],
                                 me_bias[:, :].unsqueeze(1).broadcast_to([P, TT, EXPERTS]), ALU.add))
            for t in range(TT):
                step(v.max(me_top[:, t, :], me_pb[:, t, :]))
                step(v.match_replace(me_rep[:, t, :], me_top[:, t, :], me_pb[:, t, :], MASKED))
            step(v.tensor_scalar(me_rep[:, :, :], me_rep[:, :, :], MASKED, None, ALU.is_equal))
            step(v.tensor_tensor(me_w[:, :, :], me_rep[:, :, :], me_pr[:, :, :], ALU.mult))
            step(v.tensor_reduce(me_sum[:, :], me_w[:, :, :], AX_X, ALU.add))
            step(v.reciprocal(me_rsum[:, :], me_sum[:, :]))
            step(v.scalar_tensor_tensor(me_w[:, :, :], me_w[:, :, :], 2.5,
                                        me_rsum[:, :].unsqueeze(2).broadcast_to([P, TT, EXPERTS]),
                                        ALU.mult, ALU.mult))

            def me_add(e, half):
                n = 2 * (e - 1) + half
                dve.wait_ge(me_y, n + 1)
                for t in range(TB):
                    tt = half * TB + t
                    y = bank(4 + n % 2)[:, t * LAT:(t + 1) * LAT]
                    w = me_w[:, tt, e - 1:e]
                    if e == 1:
                        v.tensor_scalar(me_acc[:, tt, :], y, w, None, ALU.mult).then_inc(me_y_out, 1)
                    else:
                        v.scalar_tensor_tensor(me_acc[:, tt, :], y, w, me_acc[:, tt, :], ALU.mult, ALU.add
                                               ).then_inc(me_y_out, 1)

            for e in range(EXPERTS + 1):
                for i in range(4):
                    n = 4 * e + i
                    m, c = i // 2, i % 2
                    dve.wait_ge(me_sqr, n + 1)
                    if e >= 3 and i == 0:
                        dve.wait_ge(me_y, 2 * (e - 2))
                    dst = me_us[:, m, c * 512:(c + 1) * 512] if e == 0 else me_u[:, e % 2, m, c * 512:(c + 1) * 512]
                    v.tensor_tensor(dst, bank(n % 2), me_rq[:, n % 4, :], ALU.mult).then_inc(me_u_made, 1)
                    if i % 2 == 1 and e >= 2:
                        me_add(e - 1, i // 2)
            me_add(EXPERTS, 0)
            me_add(EXPERTS, 1)
            add_and_norm(6, bias=False)

        @block.scalar
        def _(act):
            s = nc.scalar
            act.wait_ge(consts_set, 6)

            for n in range(SA_JOBS + 2):
                if n < SA_JOBS:
                    b, h, t, seen = sa_unit(n)
                    act.wait_ge(sa_nm_made, n + 1)
                    if n >= 3:
                        act.wait_ge(sa_turned, n - 2)
                    s.activation(sa_p[:, n % 3, 0:seen], sa_s[:, n % 3, 0:seen], ACT.Exp, bias=sa_nm[:, n:n + 1],
                                 scale=-1.0, accum_out=sa_sum[:, n:n + 1]).then_inc(sa_p_made, 1)
                if n >= 2:
                    m = n - 2
                    b, h, t, seen = sa_unit(m)
                    act.wait_ge(sa_turned, m + 1)
                    if m >= 3:
                        act.wait_ge(sa_pv, m - 2)
                    s.copy(sa_pt[:, m % 3, 0:seen], bank(3 + m % 3)[:, 0:seen]).then_inc(sa_pt_made, 1)
            for t in range(TT):
                act.wait_ge(sa_o_turned, t + 1)
                s.copy(sa_of[:, :, t * P:(t + 1) * P], bank(t % 3).rearrange("p (f t) -> p f t", f=FT)
                       ).then_inc(sa_of_made, 1)
            act_std(act, 0)
            act_copy_x(act, 0)
            if stop == 1:
                return

            for g in range(16):
                m, c = g // 4, g % 4
                act.wait_ge(qa_vl, g + 1)
                if g >= 8 and c == 0:
                    act.wait_ge(qa_v_q, m - 1)
                s.activation(qa_vf[:, m % 2, c * 512:(c + 1) * 512], bank(2 + g % 2), ACT.Identity,
                             bias=v_bias2[:, m:m + 1]).then_inc(qa_vl_out, 1)
            for t in range(KT):
                act.wait_ge(qa_vt, t + 1)
                s.copy(qa_v[:, t, :], bank(6 + t % 2).bitcast(BF16)[:, 0:D]).then_inc(qa_v_made, 1)

            turn_bank = bank(6).bitcast(BF16)
            stacks = [0]

            def stack(rows, dst):
                stacks[0] += 1
                act.wait_ge(qa_turned, stacks[0])
                s.copy(dst, turn_bank[0:rows, :]).then_inc(qa_stack, 1)

            def stack_qa():
                stack(3 * HD, qa_qa[:, :])

            def stack_ka(half):
                stack(3 * HD, qa_ka[:, half * 1024:(half + 1) * 1024])

            def stack_kb(h, half):
                stack(KR, qa_kb2[:, h % 2, half * 1024:(half + 1) * 1024])

            def stack_qb(h):
                stack(KR, qa_qb2[:, h % 2, :])

            def exponent(h, i):
                n = h * EU + i
                k = i % KT
                act.wait_ge(qa_st, n + 1)
                if n >= 4:
                    act.wait_ge(qa_pv, n - 3)
                s.activation(qa_e[:, n % 4, :], bank(2 + n % 3), ACT.Exp, bias=ln255[:, :],
                             scale=qa_sk[:, k, h:h + 1]).then_inc(qa_exp, 1)

            def out_chunk(h, c):
                r = slice(h % 4 * HD, h % 4 * HD + HD)
                act.wait_ge(qa_pv, (h * HALF + c + 1) * KT)
                if h % 4 == 0 and h > 0:
                    act.wait_ge(qa_grp, HALF * (h // 4 - 1) + c + 1)
                s.copy(qa_os[r, c, :], bank(5)[r, :]).then_inc(act_step, 1)
                s.copy(qa_zs[r, c, :], bank(7)[r, :]).then_inc(qa_oz, 1)

            act.wait_ge(qa_ints, 1)
            stack_qa()
            stack_ka(0)
            stack_ka(1)
            stack_kb(0, 0)
            stack_kb(0, 1)
            stack_qb(0)
            stack_qa()
            stack_ka(0)
            stack_ka(1)
            for h in range(HEADS):
                for i in range(EU):
                    exponent(h, i)
                    if i == 2 and h > 0:
                        out_chunk(h - 1, 1)
                    if i == KT + 2:
                        out_chunk(h, 0)
                    if h + 1 < HEADS:
                        if i == 19:
                            stack_kb(h + 1, 0)
                        if i == 21:
                            stack_kb(h + 1, 1)
                        if i == 23:
                            stack_qb(h + 1)
                    if h + 2 < HEADS:
                        if i == 25:
                            stack_qa()
                        if i == 27:
                            stack_ka(0)
                        if i == 29:
                            stack_ka(1)
            out_chunk(HEADS - 1, 1)
            act_std(act, 1)
            act_copy_x(act, 1)
            if stop == 2:
                return

            def ff_copy_rv(t):
                act.wait_ge(ff_turned, t + 1)
                if t >= 2:
                    act.wait_ge(y_made[2], t - 1)
                s.copy(ff_rvt[:, t % 2, 0:4, :].rearrange("p a b -> p (a b)"), bank(2)).then_inc(act_step, 1)
                s.copy(ff_rvt[:, t % 2, 4:8, :].rearrange("p a b -> p (a b)"), bank(3)).then_inc(ff_rvt_made, 1)

            for t in range(TT + 1):
                if t < TT:
                    act.wait_ge(ff_vecs, t + 1)
                    if t >= 2:
                        act.wait_ge(ff_rv_made, t - 1)
                    s.copy(ff_vec[:, t % 2, 0:32, :].rearrange("p a b -> p (a b)"), bank(0)).then_inc(act_step, 1)
                    s.copy(ff_vec[:, t % 2, 32:64, :].rearrange("p a b -> p (a b)"), bank(1)).then_inc(ff_vec_out, 1)
                if t >= 1:
                    ff_copy_rv(t - 1)
            act_std(act, 2)
            act_copy_x(act, 2)
            if stop == 3:
                return

            for c in range(HALF):
                act.wait_ge(rc_zl, c + 1)
                s.copy(rc_z[:, c * 512:(c + 1) * 512], bank(c)).then_inc(rc_z_out, 1)
            for c in range(HALF):
                act.wait_ge(rc_gl, c + 1)
                s.activation(rc_d[:, c * 512:(c + 1) * 512], bank(2 + c), ACT.Sigmoid).then_inc(rc_d_out, 1)
            act_std(act, 3)
            act_std(act, 4)
            if stop == 4:
                return
            act.wait_ge(ca_ss_made, TT)
            for t in range(TT):
                s.activation(rc_y[:, t, :], x_tok[:, t, :], ACT.Square, scale=float(D) ** -0.5,
                             accum_out=ca_rr[:, t:t + 1]).then_inc(ca_xn_made, 1)
            act.wait_ge(ca_xn_made, TT)
            s.activation(ca_ss[:, :], ca_rr[:, :], ACT.Sqrt, bias=eps_rms[:, :]).then_inc(ca_rr_made, 1)
            act_copy_x(act, 4)

            MT = bank(6).bitcast(BF16)

            def copy_mrow(u):
                act.wait_ge(ca_mt, u + 1)
                if u >= 2:
                    act.wait_ge(ca_st, CE * (u - 1))
                o = u % 4 * HD
                s.copy(ca_mrow[o:o + 3, u % 2, :], MT[o:o + 3, 0:512]).then_inc(ca_mrow_made, 1)

            for b in range(BATCH):
                for j in range(16):
                    g = 24 * b + (j if j < 8 else j + 8)
                    act.wait_ge(ca_lin, g + 1)
                    if g:
                        act.wait_ge(ca_lin_out, g)
                    if j < 8:
                        s.copy(ca_k[:, j // 2, j % 2 * 512:(j % 2 + 1) * 512], bank(g % 4)).then_inc(ca_lin_out, 1)
                    elif j < 12:
                        s.mul(ca_q[:, j - 8, :], bank(g % 4), SCALE).then_inc(ca_lin_out, 1)
                    else:
                        if b == 1 and j == 12:
                            act.wait_ge(y_added[5], TB)
                        s.activation(ca_gate[:, j - 12, :], bank(g % 4), ACT.Sigmoid).then_inc(ca_lin_out, 1)

                def ca_out(u):
                    h = u % HEADS
                    r = slice(h % 4 * HD, h % 4 * HD + HD)
                    act.wait_ge(ca_pv, CE * (u + 1))
                    if h % 4 == 0 and u > 0:
                        act.wait_ge(ca_grp, u // 4)
                    o = bank((5, 7)[u % 2])
                    a = h % 2 * HD
                    s.copy(ca_os[r, :], o[a:a + HD, :]).then_inc(ca_oz, 1)
                    s.copy(ca_zs[r, :], o[HD - a:2 * HD - a, :]).then_inc(ca_oz, 1)

                copy_mrow(b * HEADS)
                for h in range(HEADS):
                    u = b * HEADS + h
                    for k in range(CE):
                        n = u * CE + k
                        act.wait_ge(ca_st, n + 1)
                        if n >= 4:
                            act.wait_ge(ca_pv, n - 3)
                        s.activation(ca_e[:, n % 4, :], bank(2 + n % 3), ACT.Exp,
                                     bias=ca_mask[:, b * KB + k:b * KB + k + 1]).then_inc(ca_exp, 1)
                        if k == 2 and h > 0:
                            ca_out(u - 1)
                        if k == 4 and h + 1 < HEADS:
                            copy_mrow(u + 1)
                ca_out(b * HEADS + HEADS - 1)
            act_std(act, 5)
            act_copy_x(act, 5)
            if stop == 5:
                return

            for c in range(HALF):
                act.wait_ge(me_l, c + 1)
                s.copy(me_xl[:, c * 512:(c + 1) * 512], bank(c)).then_inc(me_l_out, 1)
            act.wait_ge(me_r, 1)
            s.activation(me_pr[:, :, :].rearrange("p a b -> p (a b)"), bank(2)[:, 0:TT * EXPERTS], ACT.Sigmoid
                         ).then_inc(me_pr_made, 1)
            for n in range(ME_UNITS):
                act.wait_ge(me_h, n + 1)
                if n >= 4:
                    act.wait_ge(me_u_made, n - 3)
                s.activation(me_rl[:, n % 4, :], bank(2 + n % 2), ACT.Relu).then_inc(me_relu, 1)
                act.wait_ge(me_relu, n + 1)
                s.activation(me_rq[:, n % 4, :], me_rl[:, n % 4, :], ACT.Square).then_inc(me_sqr, 1)
            for c in range(2):
                act.wait_ge(me_at, c + 1)
                s.copy(me_acct[:, c * 4:(c + 1) * 4, :].rearrange("p a b -> p (a b)"), bank(c)).then_inc(me_at_out, 1)
            act_std(act, 6)

        @block.gpsimd
        def _(pool):
            g = nc.gpsimd
            steps = [0]

            def step(ins):
                steps[0] += 1
                ins.then_inc(pool_step, 1)
                pool.wait_ge(pool_step, steps[0])

            def add_bias(i, bias, ready, counts):
                for t in range(TT):
                    pool.wait_ge(ready, counts(t))
                    g.tensor_tensor(x_tok[:, t, :], x_tok[:, t, :], bias[:, :], ALU.add).then_inc(bias_in[i], 1)

            pool.wait_ge(consts_in, 13 * 16)
            add_bias(0, sa_ob, x_in, lambda t: 16)
            if stop == 1:
                return
            add_bias(1, qa_pb, x_turned[0], lambda t: t + 1)
            pool.wait_ge(qa_ints, 1)
            pool.wait_ge(qa_k, KT)

            def split(dst, ints, scale, shape, t1, t2):
                step(g.tensor_tensor(t1, ints, scale, ALU.mult))
                step(g.tensor_tensor(dst[0], ints, scale, ALU.mult))
                step(g.tensor_tensor(t2, t1, dst[0], ALU.subtract))
                step(g.tensor_tensor(dst[1], t1, dst[0], ALU.subtract))
                return g.tensor_tensor(dst[2], t2, dst[1], ALU.subtract)

            pool.wait_ge(qa_qt_zero, 1)
            for h in range(HEADS):
                hs = slice(h * HD, (h + 1) * HD)
                if h >= 1:
                    pool.wait_ge(qa_turned, 3 if h == 1 else TURNS * (h - 1) + 3)
                split([qa_kt[:, :, j, :] for j in range(3)], qa_kint[:, :, h, 0:HD],
                      qa_sk[:, :, h].unsqueeze(2).broadcast_to([P, KT, HD]), None, qa_t1[:, :, :], qa_t2[:, :, :]
                      ).then_inc(qa_kt_made, 1)
                if h >= 1:
                    pool.wait_ge(qa_turned, 6 if h == 1 else TURNS * h)
                split([qa_qt[:, :, j, 0:HD] for j in range(3)], qa_qint[:, :, hs],
                      qa_sq[:, :, h].unsqueeze(2).broadcast_to([P, TT, HD]), None, qa_t3[:, :, :], qa_t4[:, :, :]
                      ).then_inc(qa_qt_made, 1)
            if stop == 2:
                return
            add_bias(2, ff_bias, x_turned[1], lambda t: t + 1)


def kernel(**inputs):
    import numpy as np
    import concourse.bacc as bacc
    from concourse.bass_utils import run_bass_kernel_spmd

    a = {k: np.asarray(v) for k, v in inputs.items()}

    def tiles(w):
        return w.reshape(-1, P, w.shape[-1]).transpose(1, 0, 2)

    x = a["x"].reshape(TOK, D)
    ctx = a["ctx_2048"].reshape(KEYS, D)
    mask = a["mask_BxS2_bk0"].reshape(KEYS)
    lanes, cols = np.arange(P)[:, None], np.arange(SEQ)[None, :]
    past = cols - (SEQ - P) - lanes
    arrays = {
        "x_tok": tiles(x), "x_feat": tiles(x.T), "ctx": tiles(ctx.T),
        "ctx0": tiles(ctx[:CTX].T), "ctx1": tiles(ctx[CTX:].T),
        "ident": np.eye(P, dtype=np.float32),
        "decay": np.where(past > 0, -MASKED, -past).astype(np.float32),
        "sa_wq": tiles(a["L0_attn_q_w"].T), "sa_wk": tiles(a["L0_attn_k_w"].T),
        "sa_wv": tiles(a["L0_attn_v_w"].T), "sa_wo": tiles(a["L0_attn_o_w"].T),
        "q_b": a["L0_attn_q_b"].reshape(FT, P).T, "k_b": a["L0_attn_k_b"].reshape(FT, P).T,
        "sa_vb": a["L0_attn_v_b"], "sa_ob": a["L0_attn_o_b"],
        "qa_wq": tiles(a["L0_xattn_Wq"]), "qa_wkv": tiles(a["L0_xattn_Wkv"]), "qa_wp": tiles(a["L0_xattn_Wp"]),
        "qa_qb": a["L0_xattn_bq"], "qa_kb": a["L0_xattn_bkv"][:D], "qa_pb": a["L0_xattn_bp"],
        "qa_vb": a["L0_xattn_bkv"][D:].reshape(FT, P).T,
        "ff_a": tiles(a["L0_ffn_A"].reshape(ARROWS * RANK, D).T),
        "ff_b": tiles(a["L0_ffn_B"].transpose(0, 2, 1).reshape(ARROWS * RANK, D)),
        "ff_w": tiles(a["L0_ffn_W"].T), "ff_bias": a["L0_ffn_bias"],
        "rc_win": tiles(a["L1_attn_W_in"]), "rc_wout": a["L1_attn_W_out"],
        "rc_wf_d": a["L1_attn_W_fwd"][:, :DI], "rc_wf_g": a["L1_attn_W_fwd"][:, DI:],
        "rc_wb_d": a["L1_attn_W_bwd"][:, :DI], "rc_wb_g": a["L1_attn_W_bwd"][:, DI:],
        "rc_gamma": a["L1_attn_gamma"], "rc_beta": a["L1_attn_beta"],
        "ca_nw": a["L1_xattn_norm_w"], "ca_wq": tiles(a["L1_xattn_wq"].T), "ca_wk": tiles(a["L1_xattn_wk"].T),
        "ca_wv": tiles(a["L1_xattn_wv"].T), "ca_wo": tiles(a["L1_xattn_wo"].T), "ca_wg": tiles(a["L1_xattn_wg"].T),
        "mask_tok": mask.reshape(KT, P).T, "mask_row": mask,
        "me_s1": tiles(a["L1_ffn_sw1"].T), "me_sg": tiles(a["L1_ffn_swg"].T), "me_s2": tiles(a["L1_ffn_sw2"].T),
        "me_wd": tiles(a["L1_ffn_Wdown"].T), "me_wu": a["L1_ffn_Wup"].T, "me_wr": tiles(a["L1_ffn_Wg"].T),
        "me_w1": a["L1_ffn_rw1"].transpose(2, 0, 1), "me_wg": a["L1_ffn_rwg"].transpose(2, 0, 1),
        "me_w2": tiles(a["L1_ffn_rw2"].transpose(0, 2, 1).reshape(EXPERTS * HID, LAT)),
        "me_bias": a["L1_ffn_biases"],
    }
    arrays = {f"in_{k}": np.ascontiguousarray(v) for k, v in arrays.items()}
    nc = bacc.Bacc("TRN2", target_bir_lowering=False, num_devices=1)
    dram = {k[3:]: nc.dram_tensor(k, v.shape, mybir.dt.from_np(v.dtype), kind="ExternalInput").ap()
            for k, v in arrays.items()}
    out = nc.dram_tensor("out_x", (TOK, D), F32, kind="ExternalOutput").ap()
    decoder_program(nc, dram, out, STOP)
    r = run_bass_kernel_spmd(nc, [arrays], core_ids=[0])
    return r.results[0]["out_x"].reshape(BATCH, SEQ, D)


STOP = 6
```

```python
from contextlib import ExitStack

import concourse.bass as bass
from concourse import mybir

F32 = mybir.dt.float32
BF16 = mybir.dt.bfloat16
F32R = mybir.dt.float32r
U8 = mybir.dt.uint8
ALU = mybir.AluOpType
ACT = mybir.ActivationFunctionType
AX_X = mybir.AxisListType.X

P = 128
BATCH, SEQ, CTX, D, HEADS = 2, 512, 1024, 512, 16
HD = D // HEADS
FT = D // P
TOK = BATCH * SEQ
TT = TOK // P
TB = SEQ // P
KEYS = BATCH * CTX
KT = KEYS // P
KB = CTX // P
HALF = TOK // 512
ARROWS, RANK = 64, 16
EXPERTS, LAT, HID, TOPK = 16, 128, 256, 8
DI = 64
SCALE = float(HD) ** -0.5
ROUND = 1.5 * 2.0 ** 23
LN255 = 5.541263545158426
MASKED = -1.0e30
LN_EPS = 1e-5
RMS_EPS = 1e-6
KIB = 1024


def decoder_program(nc, dram, out, stop=6):
    with ExitStack() as ctx:
        base = (nc.sbuf_base + 255) // 256 * 256
        ctx.enter_context(nc.sbuf_tensor("arena", [P, base - nc.sbuf_base + 206 * KIB], U8))

        def at(name, kib, shape, dt=F32):
            return nc.alloc_sbuf_tensor_at(name, shape, dt, offset=base + int(kib * KIB))

        def sem(name):
            return ctx.enter_context(nc.semaphore(name))

        x_tok = at("x_tok", 0, [P, TT, D])
        x_feat = at("x_feat", 16, [P, FT, TOK])
        WA, WB, CONST, BC, R = 32, 72, 112, 118, 134
        ident = at("ident", CONST, [P, P])
        ident_bf = at("ident_bf", CONST + 0.5, [P, P], BF16)
        decay = at("decay", CONST + 0.75, [P, SEQ])
        ln255 = at("ln255", CONST + 2.75, [P, 1])
        eps_ln = at("eps_ln", CONST + 2.8125, [P, 1])
        eps_rms = at("eps_rms", CONST + 2.875, [P, 1])
        stats = at("stats", CONST + 3, [P, TT, 6])
        meanvar = at("meanvar", CONST + 3.25, [P, TT, 2])
        std = at("std", CONST + 3.5, [P, TT])
        rstd = at("rstd", CONST + 3.625, [P, TT])
        ones_f = at("ones_f", CONST + 3.75, [P, HD])
        ones_bf = at("ones_bf", CONST + 4, [P, P], BF16)
        q_bias = at("q_bias", CONST + 4.25, [P, FT])
        k_bias = at("k_bias", CONST + 4.375, [P, FT])
        v_bias2 = at("v_bias2", CONST + 4.5, [P, FT])

        psum = ctx.enter_context(nc.psum_tensor("psum", [P, 8, 512], F32))

        def bank(i):
            return psum[:, i, :]

        SUB = 7
        y_made = [sem(f"y_made{i}") if i not in (4,) else None for i in range(SUB)]
        y_added = [sem(f"y_added{i}") if i not in (4,) else None for i in range(SUB)]
        var_made = [sem(f"var_made{i}") for i in range(SUB)]
        std_made = [sem(f"std_made{i}") for i in range(SUB)]
        x_normed = [sem(f"x_normed{i}") for i in range(SUB)]
        x_turned = [sem(f"x_turned{i}") if i not in (3, 6) else None for i in range(SUB)]
        xf_made = [sem(f"xf_made{i}") if i not in (3, 6) else None for i in range(SUB)]
        bias_in = [sem(f"bias_in{i}") if i not in (3, 4, 5, 6) else None for i in range(SUB)]
        dve_step = sem("dve_step")
        act_step = sem("act_step")
        pool_step = sem("pool_step")
        consts_in = sem("consts_in")
        consts_set = sem("consts_set")
        out_done = sem("out_done")
        Y0, XT0 = 4, 6

        def pe_turn_x(pe, i, src=x_tok):
            for t in range(TT):
                pe.wait_ge(x_normed[i], t + 1)
                if t >= 2:
                    pe.wait_ge(xf_made[i], t - 1)
                for f in range(FT):
                    ins = nc.tensor.transpose(bank(XT0 + t % 2)[:, f * P:(f + 1) * P],
                                              src[:, t, f * P:(f + 1) * P], ident[:, :])
                ins.then_inc(x_turned[i], 1)

        def act_copy_x(act, i):
            for t in range(TT):
                act.wait_ge(x_turned[i], t + 1)
                nc.scalar.copy(x_feat[:, :, t * P:(t + 1) * P],
                               bank(XT0 + t % 2).rearrange("p (f t) -> p f t", f=FT)
                               ).then_inc(xf_made[i], 1)

        def act_std(act, i):
            for half in range(2):
                act.wait_ge(var_made[i], half + 1)
                nc.scalar.activation(std[:, half * TB:(half + 1) * TB],
                                     meanvar[:, half * TB:(half + 1) * TB, 1], ACT.Sqrt,
                                     bias=eps_ln[:, :]).then_inc(std_made[i], 1)

        sa_wq = at("sa_wq", WA, [P, FT, D])
        sa_wk = at("sa_wk", WA + 8, [P, FT, D])
        sa_wv = at("sa_wv", WA + 16, [P, FT, D])
        sa_wo = at("sa_wo", WA + 32, [P, FT, D])
        sa_vb = at("sa_vb", BC, [P, D])
        sa_ob = at("sa_ob", BC + 2, [P, D])
        sa_q = at("sa_q", R, [P, FT, TOK])
        sa_k = at("sa_k", R + 16, [P, FT, TOK])
        sa_v = at("sa_v", R + 32, [P, TT, D])
        sa_s = at("sa_s", R + 48, [P, 3, SEQ])
        sa_p = at("sa_p", R + 54, [P, 3, SEQ])
        sa_pt = at("sa_pt", R + 60, [P, 3, SEQ])
        sa_nm = at("sa_nm", R + 66, [P, P])
        sa_sum = at("sa_sum", R + 66.5, [P, P])
        sa_rs = at("sa_rs", R + 67, [P, P])
        sa_o = x_feat[:, :, :].rearrange("p f t -> p (f t)").rearrange("p (t d) -> p t d", t=TT)
        sa_of = sa_q
        sa_qkv_in, sa_wo_in, x_in = sem("sa_qkv_in"), sem("sa_wo_in"), sem("x_in")
        sa_lin, sa_lin_out = sem("sa_lin"), sem("sa_lin_out")
        sa_scored, sa_nm_made, sa_p_made = sem("sa_scored"), sem("sa_nm_made"), sem("sa_p_made")
        sa_turned, sa_pt_made, sa_pv = sem("sa_turned"), sem("sa_pt_made"), sem("sa_pv")
        sa_o_made, sa_o_turned, sa_of_made = sem("sa_o_made"), sem("sa_o_turned"), sem("sa_of_made")
        sa_rs_made = sem("sa_rs_made")
        SA_LIN = 3 * 8
        SA_JOBS = BATCH * HEADS * TB

        def sa_unit(n):
            b, h, t = n // (HEADS * TB), n // TB % HEADS, n % TB
            return b, h, t, (t + 1) * P

        qa_ctx = at("qa_ctx", WA, [P, FT, KEYS])
        qa_wp = at("qa_wp", WB, [P, FT, D])
        qa_wq = at("qa_wq", WB + 8, [P, FT, D])
        qa_wkv = at("qa_wkv", WB + 16, [P, FT, 2 * D])
        qa_qb = at("qa_qb", BC + 4, [P, D])
        qa_kb = at("qa_kb", BC + 6, [P, D])
        qa_pb = at("qa_pb", BC + 8, [P, D])
        qa_load, qa_ctx_in = sem("qa_load"), sem("qa_ctx_in")
        REP = HD + 3
        KR = 3 * REP
        qa_kint = at("qa_kint", R, [P, KT, HEADS, REP], BF16)
        qa_v = at("qa_v", R + 18, [P, KT, D], BF16)
        qa_qint = at("qa_qint", R + 34, [P, TT, D], BF16)
        qa_qa = at("qa_qa", R + 42, [3 * HD, TOK], BF16)
        qa_ka = at("qa_ka", R + 44, [3 * HD, KEYS], BF16)
        qa_kb2 = at("qa_kb2", R + 48, [KR, 2, KEYS], BF16)
        qa_qb2 = at("qa_qb2", R + 56, [KR, 2, TOK], BF16)
        qa_e_lo = at("qa_e_lo", WA, [P, 4, 512])
        qa_e_hi = at("qa_e_hi", R + 60, [P, 4, 512])
        qa_r = at("qa_r", R + 68, [P, 4, 512], BF16)
        qa_vf = at("qa_vf", R + 42, [P, 2, KEYS])
        qa_x1 = at("qa_x1", R + 58, [P, 2, D])
        qa_x2 = at("qa_x2", R + 62, [P, 2, D])
        qa_vint = x_feat[:, :, :].bitcast(BF16)
        qa_of = x_feat
        qa_kt = at("qa_kt", WA + 8, [P, KT, 3, HD], BF16)
        qa_qt = at("qa_qt", WA + 11, [P, TT, 3, REP], BF16)
        qa_krep = at("qa_krep", WA + 36, [P, KT, 3, REP], BF16)
        qa_qrep = at("qa_qrep", BC, [P, TT, 3, HD], BF16)
        qa_t1 = at("qa_t1", WA + 13, [P, KT, HD])
        qa_t2 = at("qa_t2", WA + 15, [P, KT, HD])
        qa_t3 = at("qa_t3", WA + 17, [P, TT, HD])
        qa_t4 = at("qa_t4", WA + 18, [P, TT, HD])
        qa_os = at("qa_os", WA + 19, [P, HALF, 512])
        qa_zs = at("qa_zs", WA + 23, [P, HALF, 512])
        qa_rz = at("qa_rz", WA + 27, [P, 512])
        qa_sum = [at("qa_sum0", WA + 29, [P, 512]), at("qa_sum1", BC + 2, [P, 512])]
        qa_mx8 = at("qa_mx8", WA + 31, [P, TT, 4])
        qa_m = at("qa_m", WA + 31.25, [P, 4, TT])
        qa_sq = at("qa_sq", WA + 32, [P, TT, HEADS])
        qa_sk = at("qa_sk", WA + 32.5, [P, KT, HEADS])
        qa_rk = at("qa_rk", WA + 33.5, [P, KT, HEADS])
        qa_rk1 = at("qa_rk1", WA + 34.5, [P, KT, HEADS])
        qa_sv = at("qa_sv", WA + 35.5, [P, FT])
        qa_rv = at("qa_rv", WA + 35.5625, [P, FT])
        qa_sm = at("qa_sm", WA + 35.625, [P, 2, HEADS])
        qa_q, qa_q_out = sem("qa_q"), sem("qa_q_out")
        qa_k, qa_k_out = sem("qa_k"), sem("qa_k_out")
        qa_vl, qa_vl_out = sem("qa_vl"), sem("qa_vl_out")
        qa_v_q, qa_vt, qa_v_made = sem("qa_v_q"), sem("qa_vt"), sem("qa_v_made")
        qa_ints, qa_qt_zero = sem("qa_ints"), sem("qa_qt_zero")
        qa_krep_made, qa_qrep_made = sem("qa_krep_made"), sem("qa_qrep_made")
        qa_kt_made, qa_qt_made, qa_m_made = sem("qa_kt_made"), sem("qa_qt_made"), sem("qa_m_made")
        qa_turned, qa_stack = sem("qa_turned"), sem("qa_stack")
        qa_s, qa_max, qa_st, qa_exp, qa_rnd = sem("qa_s"), sem("qa_max"), sem("qa_st"), sem("qa_exp"), sem("qa_rnd")
        qa_pv, qa_oz, qa_grp = sem("qa_pv"), sem("qa_oz"), sem("qa_grp")
        SU = TT * 4
        EU = HALF * KT
        PIECES = 4
        LAG = 3
        POOLED = 7
        ERING = 8
        qa_added = sem("qa_added")

        def qa_quadrants(h):
            return (slice(h % 4 * HD, h % 4 * HD + HD), slice((h + 1) % 4 * HD, (h + 1) % 4 * HD + HD))

        def qa_e(n):
            return (qa_e_lo if n % ERING < 4 else qa_e_hi)[:, n % 4, :]

        SPREAD = 24
        QA_STEP = {18: ("kb0", 1), 20: ("kb1", 1), 25: ("qa", 2), 27: ("ka0", 2), 29: ("ka1", 2), 31: ("qb", 1)}
        qa_order = [("qa", 0), ("ka0", 0), ("ka1", 0), ("kb0", 0), ("kb1", 0), ("qb", 0),
                    ("qa", 1), ("ka0", 1), ("ka1", 1)]
        qa_order += [(what, h + ahead) for h in range(HEADS) for what, ahead in QA_STEP.values()
                     if h + ahead < HEADS]
        qa_no = {x: i + 1 for i, x in enumerate(qa_order)}

        def score_units(i):
            return range(i * SU // SPREAD, (i + 1) * SU // SPREAD) if i < SPREAD else range(0)


        ff_a = at("ff_a", WB + 8, [P, FT, ARROWS * RANK])
        ff_b = at("ff_b", WB + 24, [P, TT, D])
        ff_w = at("ff_w", WA, [P, FT, D])
        ff_bias = at("ff_bias", BC + 10, [P, D])
        ff_load = sem("ff_load")
        ff_vec = at("ff_vec", R, [P, 2, ARROWS, RANK])
        ff_sq = at("ff_sq", R + 8, [P, ARROWS, RANK])
        ff_rv = at("ff_rv", R + 12, [P, 2, ARROWS * RANK])
        ff_rvt = at("ff_rvt", R + 20, [P, 2, TT, P])
        ff_norm = at("ff_norm", R + 28, [P, ARROWS + 4])
        ff_rep = at("ff_rep", R + 28.5, [P, ARROWS + 4])
        ff_route = at("ff_route", R + 29, [P, ARROWS])
        ff_top = at("ff_top", R + 29.25, [P, 8])
        ff_v = at("ff_v", R + 29.5, [P, RANK])
        ff_vecs, ff_vec_out, ff_rv_made = sem("ff_vecs"), sem("ff_vec_out"), sem("ff_rv_made")
        ff_turned, ff_rvt_made = sem("ff_turned"), sem("ff_rvt_made")

        rc_win = at("rc_win", R + 60, [P, FT, P])
        rc_wd = at("rc_wd", R + 62, [P, P])
        rc_wg = at("rc_wg", R + 62.5, [P, P])
        rc_wout = at("rc_wout", R + 63, [P, D])
        rc_gamma = at("rc_gamma", BC + 12, [P, D])
        rc_beta = at("rc_beta", BC + 14, [P, D])
        rc_load, rc_set = sem("rc_load"), sem("rc_set")
        rc_z = at("rc_z", R, [P, TOK])
        rc_d = at("rc_d", R + 4, [P, TOK])
        rc_g = at("rc_g", R + 8, [P, TOK])
        rc_h = at("rc_h", R + 12, [P, TOK])
        rc_y = at("rc_y", R + 16, [P, TT, D])
        rc_n = at("rc_n", R + 32, [P, TT, D])
        rc_zl, rc_z_out, rc_gl, rc_d_out, rc_h_made = (sem(f"rc_{n}") for n in ("zl", "z_out", "gl", "d_out", "h_made"))
        rc_g_out, rc_yn = sem("rc_g_out"), sem("rc_yn")

        ca_wk = at("ca_wk", WA + 8, [P, FT, D])
        ca_wv = at("ca_wv", WA + 16, [P, FT, D])
        ca_wq = at("ca_wq", WA + 24, [P, FT, D])
        ca_wg = at("ca_wg", WA + 32, [P, FT, D])
        ca_wo = at("ca_wo", WA, [P, FT, D])
        ca_nw = at("ca_nw", BC, [P, D])
        ca_load, ca_ctx_in = sem("ca_load"), sem("ca_ctx_in")
        ca_ctx = at("ca_ctx", WB, [P, FT, CTX])
        ca_kp = at("ca_kp", WB + 16, [P, 2, 2, CTX], F32R)
        ca_qp = at("ca_qp", WB + 32, [P, 2, 2, SEQ], F32R)
        ca_v = at("ca_v", R, [P, KB, HEADS // 2, 3 * HD])
        ca_gate = at("ca_gate", R + 24, [P, TB, D])
        ca_e = at("ca_e", R + 32, [P, 4, 512])
        ca_ks = at("ca_ks", R + 40, [P, 4, CTX], F32R)
        ca_qs = at("ca_qs", R + 56, [P, 4, SEQ], F32R)
        ca_of = at("ca_of", R + 64, [P, FT, SEQ])
        ca_xn = at("ca_xn", R + 32, [P, TT, D])
        ca_os = at("ca_os", BC + 4, [P, 512])
        ca_zs = at("ca_zs", BC + 6, [P, 512])
        ca_rz = at("ca_rz", BC + 8, [P, 512])
        ca_tmp = at("ca_tmp", BC + 10, [P, 2, D])
        ca_row8 = at("ca_row8", BC + 14, [P, KEYS], U8)
        ca_m = at("ca_m", CONST + 4.75, [P, 4, TB])
        ca_mx = at("ca_mx", CONST + 4.8125, [P, TB, 2])
        ca_mb = at("ca_mb", CONST + 4.875, [P, 2, TB, 3], F32R)
        ca_ss = at("ca_ss", CONST + 5, [P, TT])
        ca_rr = at("ca_rr", CONST + 5.0625, [P, TT])
        MROW, KA, KE = 3 * HD, 3 * HD + 1, 3 * HD + 3
        ca_mask_in, ca_set = sem("ca_mask_in"), sem("ca_set")
        ca_ss_made, ca_rr_made, ca_xn_made = sem("ca_ss_made"), sem("ca_rr_made"), sem("ca_xn_made")
        ca_vg, ca_vg_out = sem("ca_vg"), sem("ca_vg_out")
        ca_proj, ca_high, ca_low = sem("ca_proj"), sem("ca_high"), sem("ca_low")
        ca_stack = [sem(f"ca_stack{j}") for j in range(4)]
        ca_masked = sem("ca_masked")
        ca_s, ca_max, ca_m_made, ca_mt, ca_mrow_made = (sem(f"ca_{n}") for n in ("s", "max", "m_made", "mt", "mrow_made"))
        ca_st, ca_exp, ca_pv, ca_oz, ca_grp = (sem(f"ca_{n}") for n in ("st", "exp", "pv", "oz", "grp"))
        CU = TB * 2
        CE = KB
        UNITS = BATCH * HEADS
        CA_PROJ = {(0, 2): 0, (0, 6): 1, (1, 2): 2}

        me_w1 = at("me_w1", WA, [P, EXPERTS, HID])
        me_wg = at("me_wg", WA + 16, [P, EXPERTS, HID])
        me_w2 = at("me_w2", WB, [P, EXPERTS * 2, LAT])
        me_s1 = at("me_s1", WB + 16, [P, FT, HID])
        me_sg = at("me_sg", WB + 20, [P, FT, HID])
        me_s2 = at("me_s2", WB + 24, [P, 2, D])
        me_wd = at("me_wd", WB + 28, [P, FT, LAT])
        me_wu = at("me_wu", WB + 30, [P, D])
        me_wr = at("me_wr", WB + 32, [P, FT, EXPERTS])
        me_bias = at("me_bias", BC + 2, [P, EXPERTS])
        me_load, me_load2 = sem("me_load"), sem("me_load2")
        me_xl = at("me_xl", R, [P, TOK])
        me_us = at("me_us", R + 4, [P, 2, TOK])
        me_u = at("me_u", R + 12, [P, 2, 2, TOK])
        me_rl = at("me_rl", R + 28, [P, 4, 512])
        me_rq = at("me_rq", R + 36, [P, 4, 512])
        me_acc = at("me_acc", R + 44, [P, TT, LAT])
        me_acct = at("me_acct", R + 48, [P, TT, LAT])
        me_pr = at("me_pr", R + 52, [P, TT, EXPERTS])
        me_pb = at("me_pb", R + 52.5, [P, TT, EXPERTS])
        me_rep = at("me_rep", R + 53, [P, TT, EXPERTS])
        me_w = at("me_w", R + 53.5, [P, TT, EXPERTS])
        me_top = at("me_top", R + 54, [P, TT, 8])
        me_sum = at("me_sum", R + 54.25, [P, TT])
        me_rsum = at("me_rsum", R + 54.375, [P, TT])
        me_l, me_l_out, me_r, me_pr_made, me_w_made = (sem(f"me_{n}") for n in ("l", "l_out", "r", "pr_made", "w_made"))
        me_h, me_relu, me_sqr, me_u_made = (sem(f"me_{n}") for n in ("h", "relu", "sqr", "u_made"))
        me_y, me_y_out, me_at, me_at_out = (sem(f"me_{n}") for n in ("y", "y_out", "at", "at_out"))
        ME_UNITS = 4 * (EXPERTS + 1)

        block = ctx.enter_context(nc.Block())

        @block.sync
        def _(sp):
            def load(dst, name, s):
                sp.dma_start(dst, dram[name]).then_inc(s, 16)

            load(x_feat[:, :, :], "x_feat", sa_qkv_in)
            load(sa_wq[:, :, :], "sa_wq", sa_qkv_in)
            load(sa_wk[:, :, :], "sa_wk", sa_qkv_in)
            load(sa_wv[:, :, :], "sa_wv", sa_qkv_in)
            load(q_bias[:, :], "q_b", consts_in)
            load(k_bias[:, :], "k_b", consts_in)
            load(v_bias2[:, :], "qa_vb", consts_in)
            load(ident[:, :], "ident", consts_in)
            load(decay[:, :], "decay", consts_in)
            for dst, name in ((sa_vb, "sa_vb"), (sa_ob, "sa_ob"), (qa_qb, "qa_qb"), (qa_kb, "qa_kb"),
                              (qa_pb, "qa_pb"), (ff_bias, "ff_bias"), (rc_gamma, "rc_gamma"),
                              (rc_beta, "rc_beta")):
                sp.dma_start(dst[:, :], dram[name].partition_broadcast(P)).then_inc(consts_in, 16)
            load(x_tok[:, :, :], "x_tok", x_in)
            load(sa_wo[:, :, :], "sa_wo", sa_wo_in)
            load(qa_wq[:, :, :], "qa_wq", qa_load)
            load(qa_wkv[:, :, :], "qa_wkv", qa_load)
            load(qa_wp[:, :, :], "qa_wp", qa_load)
            sp.wait_ge(sa_lin, SA_LIN)
            load(qa_ctx[:, :, :], "ctx", qa_ctx_in)
            if stop >= 2:
                sp.wait_ge(qa_vl, 16)
                sp.wait_ge(qa_k, KT)
                sp.wait_ge(qa_q, TT)
                load(ff_a[:, :, :], "ff_a", ff_load)
                load(ff_b[:, :, :], "ff_b", ff_load)
                sp.wait_ge(y_made[1], TT)
                sp.wait_ge(qa_grp, PIECES * HALF * HEADS // 4)
                sp.wait_ge(qa_rnd, HEADS * EU)
                load(ff_w[:, :, :], "ff_w", ff_load)
                sp.wait_ge(rc_set, 1)
                load(rc_win[:, :, 0:DI], "rc_win", rc_load)
                load(rc_win[:, :, DI:P], "rc_win", rc_load)
                load(rc_wd[0:DI, 0:DI], "rc_wf_d", rc_load)
                load(rc_wd[DI:P, DI:P], "rc_wb_d", rc_load)
                load(rc_wg[0:DI, 0:DI], "rc_wf_g", rc_load)
                load(rc_wg[DI:P, DI:P], "rc_wb_g", rc_load)
                load(rc_wout[:, :], "rc_wout", rc_load)
                load(ca_wk[:, :, :], "ca_wk", ca_load)
                load(ca_wv[:, :, :], "ca_wv", ca_load)
                load(ca_wq[:, :, :], "ca_wq", ca_load)
                load(ca_wg[:, :, :], "ca_wg", ca_load)
            if stop >= 3:
                sp.wait_ge(y_made[2], TT)
                load(ca_wo[:, :, :], "ca_wo", ca_load)
                load(ca_ctx[:, :, :], "ctx0", ca_ctx_in)
                sp.dma_start(ca_nw[:, :], dram["ca_nw"].partition_broadcast(P)).then_inc(ca_load, 16)
                sp.dma_start(me_bias[:, :], dram["me_bias"].partition_broadcast(P)).then_inc(ca_load, 16)
            if stop >= 5:
                sp.wait_ge(var_made[4], 2)
                sp.dma_start(ca_row8[:, :], dram["mask_row"].partition_broadcast(P)).then_inc(ca_mask_in, 16)
                for u in range(UNITS):
                    g, j = u // 4, u % 4
                    if u == 12:
                        sp.wait_ge(ca_vg, 8)
                        sp.wait_ge(ca_proj, 12)
                        load(ca_ctx[:, :, :], "ctx1", ca_ctx_in)
                    sp.wait_ge(ca_low, 3 * (g + 1))
                    if u >= 4:
                        sp.wait_ge(ca_st, CE * (u - 3))
                    r = slice(j * HD, (j + 1) * HD)
                    for i, (qpart, kpart) in enumerate(((0, 0), (1, 0), (0, 1))):
                        o = slice(i * HD, (i + 1) * HD)
                        sp.dma_start(ca_ks[o, j, :].bitcast(F32), ca_kp[r, g % 2, kpart, :].bitcast(F32)).then_inc(ca_stack[j], 16)
                        sp.dma_start(ca_qs[o, j, :].bitcast(F32), ca_qp[r, g % 2, qpart, :].bitcast(F32)).then_inc(ca_stack[j], 16)
            if stop >= 6:
                sp.wait_ge(y_made[5], TT)
                load(me_wd[:, :, :], "me_wd", me_load)
                load(me_wr[:, :, :], "me_wr", me_load)
                load(me_s1[:, :, :], "me_s1", me_load)
                load(me_sg[:, :, :], "me_sg", me_load)
                load(me_w1[:, :, :], "me_w1", me_load2)
                load(me_wg[:, :, :], "me_wg", me_load2)
                load(me_w2[:, :, :], "me_w2", me_load2)
                load(me_s2[:, :, :], "me_s2", me_load2)
                load(me_wu[:, :], "me_wu", me_load2)
            last = {1: 0, 2: 1, 3: 2, 4: 4, 5: 5, 6: 6}[stop]
            for t in range(TT):
                sp.wait_ge(x_normed[last], t + 1)
                sp.dma_start(out[t * P:(t + 1) * P, :], x_tok[:, t, :]).then_inc(out_done, 16)
            sp.wait_ge(out_done, 16 * TT)

        @block.tensor
        def _(pe):
            mm = nc.tensor.matmul

            def linear(o, lhs, rhs):
                for i, (a, b) in enumerate(zip(lhs, rhs)):
                    ins = mm(o, a, b, start=(i == 0), stop=(i == len(lhs) - 1))
                return ins

            def cols(w, a, b):
                return [w[:, k, a:b] for k in range(w.shape[1])]

            def y_bank(i, t):
                if t >= 2:
                    pe.wait_ge(y_added[i], t - 1)
                return bank(Y0 + t % 2)

            pe.wait_ge(sa_qkv_in, 64)
            g = 0
            for w in (sa_wq, sa_wk):
                for m in range(FT):
                    for c in range(HALF):
                        if g >= 4:
                            pe.wait_ge(sa_lin_out, g - 3)
                        linear(bank(g % 4), cols(w, m * P, (m + 1) * P),
                               cols(x_feat, c * 512, (c + 1) * 512)).then_inc(sa_lin, 1)
                        g += 1
            for t in range(TT):
                pe.wait_ge(sa_lin_out, g - 3)
                linear(bank(g % 4), cols(x_feat, t * P, (t + 1) * P), cols(sa_wv, 0, D)).then_inc(sa_lin, 1)
                g += 1
            pe.wait_ge(sa_lin_out, SA_LIN)
            pe.wait_ge(consts_in, 13 * 16)

            def sa_scores(n):
                b, h, t, seen = sa_unit(n)
                r = slice(h % 4 * HD, h % 4 * HD + HD)
                if n >= 3:
                    pe.wait_ge(sa_nm_made, n - 2)
                mm(bank(n % 3)[:, 0:seen], sa_k[r, h // 4, b * SEQ + t * P:b * SEQ + (t + 1) * P],
                   sa_q[r, h // 4, b * SEQ:b * SEQ + seen], start=True, stop=True).then_inc(sa_scored, 1)

            def sa_turn(n):
                b, h, t, seen = sa_unit(n)
                pe.wait_ge(sa_p_made, n + 1)
                if n >= 3:
                    pe.wait_ge(sa_pt_made, n - 2)
                for j in range(t + 1):
                    ins = nc.tensor.transpose(bank(3 + n % 3)[:, j * P:(j + 1) * P],
                                              sa_p[:, n % 3, j * P:(j + 1) * P], ident[:, :])
                ins.then_inc(sa_turned, 1)

            def sa_values(n):
                b, h, t, seen = sa_unit(n)
                u = n // TB
                pe.wait_ge(sa_pt_made, n + 1)
                if t == 0 and u >= 2:
                    pe.wait_ge(sa_o_made, u - 1)
                for j in range(t + 1):
                    ins = mm(bank(6 + u % 2)[:, t * HD:(t + 1) * HD], sa_pt[:, n % 3, j * P:(j + 1) * P],
                             sa_v[:, b * TB + j, h * HD:(h + 1) * HD], start=(j == 0), stop=(j == t))
                ins.then_inc(sa_pv, 1)

            for n in range(SA_JOBS + 4):
                if n < SA_JOBS:
                    sa_scores(n)
                if 2 <= n < SA_JOBS + 2:
                    sa_turn(n - 2)
                if n >= 4:
                    sa_values(n - 4)
            pe.wait_ge(sa_wo_in, 16)
            pe.wait_ge(sa_o_made, BATCH * HEADS)
            for t in range(TT + 1):
                if t < TT:
                    if t >= 3:
                        pe.wait_ge(sa_of_made, t - 2)
                    for f in range(FT):
                        ins = nc.tensor.transpose(bank(t % 3)[:, f * P:(f + 1) * P],
                                                  sa_o[:, t, f * P:(f + 1) * P], ident[:, :])
                    ins.then_inc(sa_o_turned, 1)
                if t >= 1:
                    pe.wait_ge(sa_of_made, t)
                    linear(y_bank(0, t - 1), cols(sa_of, (t - 1) * P, t * P), cols(sa_wo, 0, D)
                           ).then_inc(y_made[0], 1)
            pe_turn_x(pe, 0)
            if stop == 1:
                return

            pe.wait_ge(qa_load, 48)
            for t in range(TT):
                pe.wait_ge(xf_made[0], t + 1)
                if t >= 2:
                    pe.wait_ge(qa_q_out, t - 1)
                linear(bank(t % 2), cols(x_feat, t * P, (t + 1) * P), cols(qa_wq, 0, D)).then_inc(qa_q, 1)
            pe.wait_ge(qa_ctx_in, 16)
            pe.wait_ge(qa_q_out, TT)
            for g in range(16):
                m, c = g // 4, g % 4
                if g >= 2:
                    pe.wait_ge(qa_vl_out, g - 1)
                linear(bank(2 + g % 2), cols(qa_wkv, D + m * P, D + (m + 1) * P),
                       cols(qa_ctx, c * 512, (c + 1) * 512)).then_inc(qa_vl, 1)
            for t in range(KT):
                if t >= 2:
                    pe.wait_ge(qa_k_out, t - 1)
                linear(bank(t % 2), cols(qa_ctx, t * P, (t + 1) * P), cols(qa_wkv, 0, D)).then_inc(qa_k, 1)
            for t in range(KT):
                pe.wait_ge(qa_v_q, FT)
                if t >= 2:
                    pe.wait_ge(qa_v_made, t - 1)
                for m in range(FT):
                    ins = nc.tensor.transpose(bank(6 + t % 2).bitcast(BF16)[:, m * P:(m + 1) * P],
                                              qa_vint[:, m, t * P:(t + 1) * P], ident_bf[:, :])
                ins.then_inc(qa_vt, 1)
            pe.wait_ge(qa_ints, 1)
            pe.wait_ge(qa_v_made, KT)

            turn_bank = bank(6).bitcast(BF16)
            fills = [0]

            def fill(rows, blocks):
                if fills[0]:
                    pe.wait_ge(qa_stack, fills[0])
                for j, src in enumerate(blocks):
                    ins = nc.tensor.transpose(turn_bank[0:rows, j * P:(j + 1) * P], src, ident_bf[:, :])
                ins.then_inc(qa_turned, 1)
                fills[0] += 1

            def fill_stack(what, h):
                if what == "qa":
                    pe.wait_ge(qa_qrep_made, h + 1)
                    fill(3 * HD, [qa_qrep[:, t, :, :].rearrange("p a b -> p (a b)") for t in range(TT)])
                elif what == "qb":
                    pe.wait_ge(qa_qt_made, h + 1)
                    pe.wait_ge(qa_m_made, h + 1)
                    fill(KR, [qa_qt[:, t, :, :].rearrange("p a b -> p (a b)") for t in range(TT)])
                else:
                    src, rows, made = (qa_kt, 3 * HD, qa_kt_made) if what < "kb" else (qa_krep, KR, qa_krep_made)
                    half = int(what[2])
                    pe.wait_ge(made, h + 1)
                    fill(rows, [src[:, half * 8 + t, :, :].rearrange("p a b -> p (a b)") for t in range(8)])

            def qa_scores(h, i):
                n = h * SU + i
                t, c = i // 4, i % 4
                if i == 0:
                    pe.wait_ge(qa_stack, qa_no["ka1", h])
                if n >= 2:
                    pe.wait_ge(qa_max, n - 1)
                mm(bank(n % 2), qa_qa[:, t * P:(t + 1) * P], qa_ka[:, c * 512:(c + 1) * 512],
                   start=True, stop=True).then_inc(qa_s, 1)

            def qa_scores_t(h, i):
                n = h * EU + i
                c, k = i // KT, i % KT
                if i == 0:
                    pe.wait_ge(qa_stack, qa_no["qb", h])
                if n >= 3:
                    pe.wait_ge(qa_exp, n - 2)
                mm(bank(2 + n % 3), qa_kb2[:, h % 2, k * P:(k + 1) * P],
                   qa_qb2[:, h % 2, c * 512:(c + 1) * 512], start=True, stop=True).then_inc(qa_st, 1)

            def qa_values(h, i):
                n = h * EU + i
                c, k = i // KT, i % KT
                o, z = qa_quadrants(h)
                if k == 0 and n >= 2 * KT:
                    pe.wait_ge(qa_oz, h * HALF + c - 1)
                if k >= POOLED:
                    pe.wait_ge(qa_exp, n + 1)
                    mm(bank((5, 7)[c])[z, :], ones_f[:, :], qa_e(n), start=(k == POOLED), stop=False)
                if k == KT - 1:
                    pe.wait_ge(qa_added, (h * HALF + c + 1) * (POOLED - 1))
                    mm(bank((5, 7)[c])[z, :], ones_f[:, :], qa_sum[c][:, :], start=False, stop=True)
                pe.wait_ge(qa_rnd, n + 1)
                mm(bank((5, 7)[c])[o, :], qa_v[:, k, h * HD:(h + 1) * HD], qa_r[:, n % 4, :],
                   start=(k == 0), stop=(k == KT - 1)).then_inc(qa_pv, 1)

            for x in qa_order[:3]:
                fill_stack(*x)
            for i in range(SU):
                qa_scores(0, i)
            for x in qa_order[3:9]:
                fill_stack(*x)
            for h in range(HEADS):
                for i in range(EU + LAG):
                    if i < EU:
                        qa_scores_t(h, i)
                        if h + 1 < HEADS:
                            for j in score_units(i):
                                qa_scores(h + 1, j)
                    if i >= LAG:
                        qa_values(h, i - LAG)
                    if i in QA_STEP and (QA_STEP[i][0], h + QA_STEP[i][1]) in qa_no:
                        fill_stack(QA_STEP[i][0], h + QA_STEP[i][1])
            pe.wait_ge(qa_grp, PIECES * HALF * HEADS // 4)
            for t in range(TT):
                linear(y_bank(1, t), cols(qa_of, t * P, (t + 1) * P), cols(qa_wp, 0, D)).then_inc(y_made[1], 1)
            pe_turn_x(pe, 1)
            if stop == 2:
                return

            pe.wait_ge(ff_load, 48)

            def ff_y(t):
                pe.wait_ge(ff_rvt_made, t + 1)
                linear(y_bank(2, t), [ff_rvt[:, t % 2, k, :] for k in range(TT)] + cols(x_feat, t * P, (t + 1) * P),
                       cols(ff_b, 0, D) + cols(ff_w, 0, D)).then_inc(y_made[2], 1)

            def ff_turn(t):
                pe.wait_ge(ff_rv_made, t + 1)
                if t >= 1:
                    pe.wait_ge(ff_rvt_made, t)
                for k in range(TT):
                    ins = nc.tensor.transpose(bank(2 + k // 4)[:, k % 4 * P:(k % 4 + 1) * P],
                                              ff_rv[:, t % 2, k * P:(k + 1) * P], ident[:, :])
                ins.then_inc(ff_turned, 1)

            for t in range(TT + 2):
                if t < TT:
                    pe.wait_ge(xf_made[1], t + 1)
                    if t >= 1:
                        pe.wait_ge(ff_vec_out, t)
                    linear(bank(0), cols(x_feat, t * P, (t + 1) * P), cols(ff_a, 0, 512))
                    linear(bank(1), cols(x_feat, t * P, (t + 1) * P), cols(ff_a, 512, 1024)).then_inc(ff_vecs, 1)
                if 1 <= t <= TT:
                    ff_turn(t - 1)
                if t >= 2:
                    ff_y(t - 2)
            pe_turn_x(pe, 2)
            if stop == 3:
                return

            pe.wait_ge(rc_load, 7 * 16)
            pe.wait_ge(xf_made[2], TT)
            for c in range(HALF):
                linear(bank(c), cols(rc_win, 0, P), cols(x_feat, c * 512, (c + 1) * 512)).then_inc(rc_zl, 1)
            for c in range(HALF):
                pe.wait_ge(rc_z_out, c + 1)
                mm(bank(2 + c), rc_wd[:, :], rc_z[:, c * 512:(c + 1) * 512], start=True, stop=True)
                if c == 0:
                    pe.wait_ge(rc_z_out, 2)
                mm(bank(c), rc_wg[:, :], rc_z[:, c * 512:(c + 1) * 512], start=True, stop=True).then_inc(rc_gl, 1)
            for t in range(TT):
                pe.wait_ge(rc_h_made, 2 * (t // TB + 1))
                mm(y_bank(3, t), rc_h[:, t * P:(t + 1) * P], rc_wout[:, :], start=True, stop=True
                   ).then_inc(y_made[3], 1)
            if stop == 4:
                return

            pe_turn_x(pe, 4, src=ca_xn)
            pe.wait_ge(ca_load, 7 * 16)
            pe.wait_ge(ca_set, 4)

            def ca_project(j):
                g, part = j // 3, j % 3
                b, m = g // FT, g % FT
                if part == 0:
                    pe.wait_ge(ca_ctx_in, 16 * (b + 1))
                if j >= 1:
                    pe.wait_ge(ca_low, j)
                if part < 2:
                    ins = linear(bank(7), cols(ca_wk, m * P, (m + 1) * P), cols(ca_ctx, part * 512, (part + 1) * 512))
                else:
                    ins = linear(bank(7), cols(ca_wq, m * P, (m + 1) * P), cols(x_feat, b * SEQ, (b + 1) * SEQ))
                ins.then_inc(ca_proj, 1)

            def ca_scores(u, i):
                n = u * CU + i
                t, c, j = i // 2, i % 2, u % 4
                if i == 0:
                    pe.wait_ge(ca_stack[j], 96 * (u // 4 + 1))
                    pe.wait_ge(ca_masked, u + 1)
                if n >= 2:
                    pe.wait_ge(ca_max, n - 1)
                mm(bank(n % 2), ca_qs[0:KA, j, t * P:(t + 1) * P], ca_ks[0:KA, j, c * 512:(c + 1) * 512],
                   start=True, stop=True).then_inc(ca_s, 1)

            def ca_turn_m(u):
                pe.wait_ge(ca_m_made, u + 1)
                if u >= 1:
                    pe.wait_ge(ca_mrow_made, u)
                for t in range(TB):
                    ins = nc.tensor.transpose(bank(6)[0:3, t * P:(t + 1) * P], ca_mb[:, u % 2, t, :].bitcast(F32),
                                              ident[:, :])
                ins.then_inc(ca_mt, 1)

            def ca_scores_t(u, k):
                n, j = u * CE + k, u % 4
                if k == 0:
                    pe.wait_ge(ca_mrow_made, u + 1)
                if n >= 2:
                    pe.wait_ge(ca_exp, n - 1)
                mm(bank(2 + n % 2), ca_ks[0:KE, j, k * P:(k + 1) * P], ca_qs[0:KE, j, :], start=True, stop=True
                   ).then_inc(ca_st, 1)

            def ca_values(u, k):
                n, h = u * CE + k, u % HEADS
                if k == 0 and u >= 2:
                    pe.wait_ge(ca_oz, 2 * (u - 1))
                pe.wait_ge(ca_exp, n + 1)
                mm(bank(4 + u % 2)[0:2 * HD, :], ca_v[:, k, h // 2, h % 2 * HD:h % 2 * HD + 2 * HD],
                   ca_e[:, n % 4, :], start=(k == 0), stop=(k == KB - 1)).then_inc(ca_pv, 1)

            pe.wait_ge(xf_made[4], TT)
            for j in range(3):
                ca_project(j)
            for b in range(BATCH):
                if b:
                    pe.wait_ge(ca_exp, b * HEADS * CE)
                    pe.wait_ge(ca_pv, b * HEADS * CE)
                for i in range(KB + TB):
                    g = b * (KB + TB) + i
                    if i >= 2:
                        pe.wait_ge(ca_vg_out, g - 1)
                    if i < KB:
                        ins = linear(bank(2 + i % 2), cols(ca_ctx, i * P, (i + 1) * P), cols(ca_wv, 0, D))
                    else:
                        t = b * TB + i - KB
                        ins = linear(bank(2 + i % 2), cols(x_feat, t * P, (t + 1) * P), cols(ca_wg, 0, D))
                    ins.then_inc(ca_vg, 1)
                pe.wait_ge(ca_vg_out, (b + 1) * (KB + TB))
                if b == 0:
                    for u in range(2):
                        for i in range(CU):
                            ca_scores(u, i)
                        if u == 0:
                            ca_turn_m(0)
                for h in range(HEADS):
                    u = b * HEADS + h
                    for i in range(CE + 2):
                        if i < CE:
                            ca_scores_t(u, i)
                            if u + 2 < UNITS:
                                ca_scores(u + 2, i)
                            if (h % 4, i) in CA_PROJ and u // 4 + 1 < UNITS // 4:
                                ca_project(3 * (u // 4 + 1) + CA_PROJ[h % 4, i])
                        if i >= 2:
                            ca_values(u, i - 2)
                        if i == 3 and u + 1 < UNITS:
                            ca_turn_m(u + 1)
                for t in range(b * TB, (b + 1) * TB):
                    pe.wait_ge(ca_grp, 16 * (b + 1))
                    linear(y_bank(5, t), cols(ca_of, t % TB * P, (t % TB + 1) * P), cols(ca_wo, 0, D)
                           ).then_inc(y_made[5], 1)
            pe_turn_x(pe, 5)
            if stop == 5:
                return

            pe.wait_ge(me_load, 64)
            pe.wait_ge(xf_made[5], TT)
            for c in range(HALF):
                linear(bank(c), cols(me_wd, 0, LAT), cols(x_feat, c * 512, (c + 1) * 512)).then_inc(me_l, 1)
            for t in range(TT):
                ins = linear(bank(2)[:, t * EXPERTS:(t + 1) * EXPERTS], cols(x_feat, t * P, (t + 1) * P),
                             cols(me_wr, 0, EXPERTS))
            ins.then_inc(me_r, 1)
            pe.wait_ge(me_l_out, HALF)
            pe.wait_ge(me_pr_made, 1)

            def me_hidden(e, i):
                n = 4 * e + i
                m, c = i // 2, i % 2
                if n >= 2:
                    pe.wait_ge(me_u_made, n - 1)
                for which, (shared, routed) in enumerate(((me_s1, me_w1), (me_sg, me_wg))):
                    if e == 0:
                        ins = linear(bank(which * 2 + n % 2), cols(shared, m * P, (m + 1) * P),
                                     cols(x_feat, c * 512, (c + 1) * 512))
                    else:
                        ins = mm(bank(which * 2 + n % 2), routed[:, e - 1, m * P:(m + 1) * P],
                                 me_xl[:, c * 512:(c + 1) * 512], start=True, stop=True)
                ins.then_inc(me_h, 1)

            def me_out(e, half):
                n = 2 * (e - 1) + half
                if half == 0:
                    pe.wait_ge(me_u_made, 4 * (e + 1))
                if n >= 2:
                    pe.wait_ge(me_y_out, (n - 1) * TB)
                for t in range(TB):
                    tt = half * TB + t
                    ins = linear(bank(4 + n % 2)[:, t * LAT:(t + 1) * LAT],
                                 [me_u[:, e % 2, m, tt * P:(tt + 1) * P] for m in range(2)],
                                 [me_w2[:, 2 * (e - 1) + m, :] for m in range(2)])
                ins.then_inc(me_y, 1)

            for e in range(EXPERTS + 1):
                if e == 1:
                    pe.wait_ge(me_load2, 5 * 16)
                for i in range(4):
                    me_hidden(e, i)
                    if i % 2 == 1 and e >= 2:
                        me_out(e - 1, i // 2)
            me_out(EXPERTS, 0)
            me_out(EXPERTS, 1)
            pe.wait_ge(me_y_out, EXPERTS * TT)
            for t in range(TT):
                ins = nc.tensor.transpose(bank(t // 4)[:, t % 4 * P:(t % 4 + 1) * P], me_acc[:, t, :], ident[:, :])
                if t % 4 == 3:
                    ins.then_inc(me_at, 1)
            for t in range(TT):
                pe.wait_ge(me_at_out, t // 4 + 1)
                linear(y_bank(6, t), [me_us[:, m, t * P:(t + 1) * P] for m in range(2)] + [me_acct[:, t, :]],
                       [me_s2[:, m, :] for m in range(2)] + [me_wu[:, :]]).then_inc(y_made[6], 1)

        @block.vector
        def _(dve):
            v = nc.vector
            steps = [0]

            def step(ins):
                steps[0] += 1
                ins.then_inc(dve_step, 1)
                dve.wait_ge(dve_step, steps[0])

            def norm_half(i, half, src, dst, rel=None):
                dve.wait_ge(std_made[i], half + 1)
                step(v.reciprocal(rstd[:, half * TB:(half + 1) * TB], std[:, half * TB:(half + 1) * TB]))
                for t in range(half * TB, (half + 1) * TB):
                    v.tensor_scalar(dst[:, t, :], src[:, t, :], meanvar[:, t, 0:1], rstd[:, t:t + 1],
                                    ALU.subtract, ALU.mult).then_inc(x_normed[i], 1)

            def tile_stats(i, t, src):
                step(v.bn_stats(stats[:, t, :], src[:, t, :]))
                ins = v.bn_aggr(meanvar[:, t, :], stats[:, t, :])
                if t % TB == TB - 1:
                    ins.then_inc(var_made[i], 1)

            def add_tile(i, t, bias=True):
                if bias:
                    dve.wait_ge(bias_in[i], t + 1)
                dve.wait_ge(y_made[i], t + 1)
                v.tensor_tensor(x_tok[:, t, :], bank(Y0 + t % 2), x_tok[:, t, :], ALU.add).then_inc(y_added[i], 1)
                dve.wait_ge(y_added[i], t + 1)
                tile_stats(i, t, x_tok)

            def add_and_norm(i, bias=True):
                for t in range(TT):
                    add_tile(i, t, bias)
                for half in range(2):
                    norm_half(i, half, x_tok, x_tok)

            v.memset(ln255[:, :], LN255).then_inc(consts_set, 1)
            v.memset(eps_ln[:, :], LN_EPS).then_inc(consts_set, 1)
            v.memset(eps_rms[:, :], RMS_EPS).then_inc(consts_set, 1)
            v.memset(ones_f[:, :], 1.0).then_inc(consts_set, 1)
            v.memset(ones_bf[:, :], 1.0).then_inc(consts_set, 1)
            dve.wait_ge(consts_in, 13 * 16)
            v.tensor_copy(ident_bf[:, :], ident[:, :]).then_inc(consts_set, 1)

            for g in range(SA_LIN):
                dve.wait_ge(sa_lin, g + 1)
                if g < 8:
                    v.tensor_scalar(sa_q[:, g // 2, g % 2 * 512:(g % 2 + 1) * 512], bank(g % 4),
                                    q_bias[:, g // 2:g // 2 + 1], -SCALE, ALU.add, ALU.mult
                                    ).then_inc(sa_lin_out, 1)
                elif g < 16:
                    m = g // 2 - 4
                    v.tensor_scalar(sa_k[:, m, g % 2 * 512:(g % 2 + 1) * 512], bank(g % 4),
                                    k_bias[:, m:m + 1], None, ALU.add).then_inc(sa_lin_out, 1)
                else:
                    v.tensor_tensor(sa_v[:, g - 16, :], bank(g % 4), sa_vb[:, :], ALU.add
                                    ).then_inc(sa_lin_out, 1)

            def sa_finish(u):
                b, h = u // HEADS, u % HEADS
                dve.wait_ge(sa_p_made, TB * (u + 1))
                v.reciprocal(sa_rs[:, TB * u:TB * (u + 1)], sa_sum[:, TB * u:TB * (u + 1)]).then_inc(sa_rs_made, 1)
                dve.wait_ge(sa_rs_made, u + 1)
                dve.wait_ge(sa_pv, TB * (u + 1))
                v.tensor_tensor(sa_o[:, b * TB:(b + 1) * TB, h * HD:(h + 1) * HD],
                                bank(6 + u % 2)[:, 0:P].rearrange("p (t d) -> p t d", t=TB),
                                sa_rs[:, TB * u:TB * (u + 1)].unsqueeze(2).broadcast_to([P, TB, HD]),
                                ALU.mult).then_inc(sa_o_made, 1)

            for n in range(SA_JOBS):
                b, h, t, seen = sa_unit(n)
                dve.wait_ge(sa_scored, n + 1)
                if n >= 3:
                    dve.wait_ge(sa_p_made, n - 2)
                v.tensor_tensor_reduce(sa_s[:, n % 3, 0:seen], bank(n % 3)[:, 0:seen],
                                       decay[:, SEQ - seen:SEQ], 1.0, 3.0e38, ALU.add, ALU.min,
                                       sa_nm[:, n:n + 1]).then_inc(sa_nm_made, 1)
                if n % TB == 0 and n >= 2 * TB:
                    sa_finish(n // TB - 2)
            for u in range(BATCH * HEADS - 2, BATCH * HEADS):
                sa_finish(u)
            add_and_norm(0)
            if stop == 1:
                return

            def quantise(src, n_tile, scale, s_all, r_all, dst):
                x3 = src.rearrange("p (h d) -> p h d", h=HEADS)
                step(v.tensor_reduce(qa_sm[:, 0, :], x3, AX_X, ALU.max, apply_absolute_value=True))
                step(v.tensor_scalar(qa_sm[:, 1, :], qa_sm[:, 0, :], scale, 1.0 / 127.0, ALU.mult, ALU.mult))
                step(v.tensor_scalar(s_all, qa_sm[:, 1, :], 1e-8, None, ALU.max))
                step(v.reciprocal(r_all, s_all))
                t3 = qa_x2[:, n_tile % 2, :].rearrange("p (h d) -> p h d", h=HEADS)
                step(v.scalar_tensor_tensor(t3, x3, scale, r_all.unsqueeze(2).broadcast_to([P, HEADS, HD]),
                                            ALU.mult, ALU.mult))
                step(v.tensor_scalar(x3, t3, ROUND, -ROUND, ALU.add, ALU.add))
                step(v.tensor_scalar(dst, x3, 127.0, -127.0, ALU.min, ALU.max))

            for t in range(TT):
                dve.wait_ge(qa_q, t + 1)
                v.tensor_tensor(qa_x1[:, t % 2, :], bank(t % 2), qa_qb[:, :], ALU.add).then_inc(qa_q_out, 1)
                dve.wait_ge(qa_q_out, t + 1)
                quantise(qa_x1[:, t % 2, :], t, SCALE, qa_sq[:, t, :], qa_rk1[:, t, :],
                         qa_qint[:, t, :].rearrange("p (h d) -> p h d", h=HEADS))
            for m in range(FT):
                dve.wait_ge(qa_vl_out, 4 * (m + 1))
                vf = qa_vf[:, m % 2, :]
                step(v.tensor_reduce(qa_sm[:, 0, 0:1], vf, AX_X, ALU.max, apply_absolute_value=True))
                step(v.tensor_scalar(qa_sv[:, m:m + 1], qa_sm[:, 0, 0:1], 1.0 / 127.0, 1e-8, ALU.mult, ALU.max))
                step(v.reciprocal(qa_rv[:, m:m + 1], qa_sv[:, m:m + 1]))
                step(v.tensor_scalar(vf, vf, qa_rv[:, m:m + 1], 127.0, ALU.mult, ALU.min))
                step(v.tensor_scalar(vf, vf, -127.0, ROUND, ALU.max, ALU.add))
                v.tensor_scalar(qa_vint[:, m, :], vf, -ROUND, None, ALU.add).then_inc(qa_v_q, 1)
            for t in range(KT):
                dve.wait_ge(qa_k, t + 1)
                v.tensor_tensor(qa_x1[:, t % 2, :], bank(t % 2), qa_kb[:, :], ALU.add).then_inc(qa_k_out, 1)
                dve.wait_ge(qa_k_out, t + 1)
                quantise(qa_x1[:, t % 2, :], t, 1.0, qa_sk[:, t, :], qa_rk[:, t, :], qa_kint[:, t, :, 0:HD])
            step(v.tensor_copy(qa_kint[:, :, :, HD], qa_rk[:, :, :]))
            step(v.tensor_tensor(qa_rk1[:, :, :], qa_rk[:, :, :], qa_kint[:, :, :, HD], ALU.subtract))
            step(v.tensor_copy(qa_kint[:, :, :, HD + 1], qa_rk1[:, :, :]))
            v.tensor_tensor(qa_kint[:, :, :, HD + 2], qa_rk1[:, :, :], qa_kint[:, :, :, HD + 1],
                            ALU.subtract).then_inc(qa_ints, 1)

            def qa_maximum(h, i):
                n = h * SU + i
                dve.wait_ge(qa_s, n + 1)
                v.tensor_reduce(qa_mx8[:, i // 4, i % 4:i % 4 + 1], bank(n % 2), AX_X, ALU.max).then_inc(qa_max, 1)

            def qa_splits(h):
                dve.wait_ge(qa_max, SU * (h + 1))
                if h >= 1:
                    dve.wait_ge(qa_turned, qa_no["qb", h - 1])
                step(v.tensor_reduce(qa_m[:, 0, :], qa_mx8[:, :, :], AX_X, ALU.max))
                step(v.scalar_tensor_tensor(qa_m[:, 1, :], qa_m[:, 0, :], -1.0, qa_sq[:, :, h], ALU.mult, ALU.mult))
                m1 = qa_m[:, 1, :].unsqueeze(2)
                step(v.tensor_copy(qa_qt[:, :, 0, HD:REP], m1.broadcast_to([P, TT, 3])))
                step(v.tensor_tensor(qa_m[:, 2, :], qa_m[:, 1, :], qa_qt[:, :, 0, HD], ALU.subtract))
                step(v.tensor_copy(qa_qt[:, :, 1, HD:REP - 1], qa_m[:, 2, :].unsqueeze(2).broadcast_to([P, TT, 2])))
                v.tensor_tensor(qa_qt[:, :, 2, HD], qa_m[:, 2, :], qa_qt[:, :, 1, HD], ALU.subtract
                                ).then_inc(qa_m_made, 1)

            def qa_round(h, i):
                n = h * EU + i
                dve.wait_ge(qa_exp, n + 1)
                if n >= 4:
                    dve.wait_ge(qa_pv, n - 3)
                v.tensor_scalar(qa_r[:, n % 4, :], qa_e(n), ROUND, -ROUND, ALU.add, ALU.add
                                ).then_inc(qa_rnd, 1)

            def qa_group(h, piece):
                c, j = piece // PIECES, piece % PIECES
                n = 512 // PIECES
                dve.wait_ge(qa_oz, HALF * h + c + 1)
                if piece or h >= 4:
                    dve.wait_ge(qa_grp, h // 4 * HALF * PIECES + piece)
                step(v.reciprocal(qa_rz[:, 0:n], qa_zs[:, c, j * n:(j + 1) * n]))
                v.scalar_tensor_tensor(qa_of[:, h // 4, c * 512 + j * n:c * 512 + (j + 1) * n],
                                       qa_os[:, c, j * n:(j + 1) * n], qa_sv[:, h // 4:h // 4 + 1],
                                       qa_rz[:, 0:n], ALU.mult, ALU.mult).then_inc(qa_grp, 1)

            def qa_repeat_k(h):
                if h >= 1:
                    dve.wait_ge(qa_turned, qa_no["kb1", h - 1])
                v.tensor_copy(qa_krep[:, :, :, :], qa_kint[:, :, h, :].unsqueeze(2).broadcast_to([P, KT, 3, REP])
                              ).then_inc(qa_krep_made, 1)

            def qa_repeat_q(h):
                if h >= 1:
                    dve.wait_ge(qa_turned, qa_no["qa", h - 1])
                v.tensor_copy(qa_qrep[:, :, :, :], qa_qint[:, :, h * HD:(h + 1) * HD].unsqueeze(2)
                              .broadcast_to([P, TT, 3, HD])).then_inc(qa_qrep_made, 1)

            dve.wait_ge(qa_ctx_in, 16)
            dve.wait_ge(qa_k, KT)
            dve.wait_ge(qa_ints, 1)
            qa_repeat_k(0)
            qa_repeat_q(0)
            qa_repeat_q(1)
            v.memset(qa_qt[:, :, :, :], 0.0).then_inc(qa_qt_zero, 1)
            dve.wait_ge(qa_vt, KT)
            for i in range(SU):
                qa_maximum(0, i)
            qa_splits(0)
            for h in range(HEADS):
                for i in range(EU):
                    if h + 1 < HEADS:
                        for j in score_units(i):
                            qa_maximum(h + 1, j)
                    qa_round(h, i)
                    if i == SPREAD and h + 1 < HEADS:
                        qa_splits(h + 1)
                    if i % 3 == 2 and i // 3 < HALF * PIECES and h % 4 == 0 and h > 0:
                        qa_group(h - 1, i // 3)
                    if i == 12 and h + 1 < HEADS:
                        qa_repeat_k(h + 1)
                    if i == 20 and h + 2 < HEADS:
                        qa_repeat_q(h + 2)
            for piece in range(HALF * PIECES):
                qa_group(HEADS - 1, piece)
            dve.wait_ge(y_made[0], TT)
            dve.wait_ge(qa_pv, HEADS * EU)
            step(v.memset(rc_wd[:, :], 0.0))
            v.memset(rc_wg[:, :], 0.0).then_inc(rc_set, 1)
            add_and_norm(1)
            if stop == 2:
                return

            step(v.memset(ff_norm[:, ARROWS:], -1.0))
            for t in range(TT):
                dve.wait_ge(ff_vec_out, t + 1)
                vec = ff_vec[:, t % 2, :, :]
                step(v.tensor_tensor(ff_sq[:, :, :], vec, vec, ALU.mult))
                step(v.tensor_reduce(ff_norm[:, 0:ARROWS], ff_sq[:, :, :], AX_X, ALU.add))
                step(v.max(ff_top[:, :], ff_norm[:, :]))
                step(v.memset(ff_top[:, 4:8], -1.0))
                step(v.match_replace(ff_rep[:, :], ff_top[:, :], ff_norm[:, :], -2.0))
                step(v.tensor_scalar(ff_route[:, :], ff_rep[:, 0:ARROWS], -2.0, 0.25, ALU.is_equal, ALU.mult))
                route = ff_route[:, :].unsqueeze(2).broadcast_to([P, ARROWS, RANK])
                step(v.tensor_tensor(ff_sq[:, :, :], vec, route, ALU.mult))
                step(v.tensor_reduce(ff_v[:, :], ff_sq[:, :, :].rearrange("p a r -> p r a"), AX_X, ALU.add))
                if t >= 2:
                    dve.wait_ge(ff_turned, t - 1)
                v.tensor_tensor(ff_rv[:, t % 2, :].rearrange("p (a r) -> p a r", a=ARROWS), route,
                                ff_v[:, :].unsqueeze(1).broadcast_to([P, ARROWS, RANK]), ALU.mult
                                ).then_inc(ff_rv_made, 1)
                if t >= 2:
                    add_tile(2, t - 2)
            add_tile(2, TT - 2)
            add_tile(2, TT - 1)
            for half in range(2):
                norm_half(2, half, x_tok, x_tok)
            if stop == 3:
                return

            for c in range(HALF):
                dve.wait_ge(rc_gl, c + 1)
                v.tensor_tensor(rc_g[:, c * 512:(c + 1) * 512], bank(c), rc_z[:, c * 512:(c + 1) * 512],
                                ALU.mult).then_inc(rc_g_out, 1)
                dve.wait_ge(rc_g_out, c + 1)
                dve.wait_ge(rc_d_out, c + 1)
                lo, hi = c * SEQ, (c + 1) * SEQ
                v.tensor_tensor_scan(rc_h[0:DI, lo:hi], rc_d[0:DI, lo:hi], rc_g[0:DI, lo:hi], 0.0,
                                     ALU.mult, ALU.add).then_inc(rc_h_made, 1)
                back = slice(hi - 1, lo - 1 if lo else None, -1)
                v.tensor_tensor_scan(rc_h[DI:P, back], rc_d[DI:P, back], rc_g[DI:P, back], 0.0,
                                     ALU.mult, ALU.add).then_inc(rc_h_made, 1)
            for t in range(TT):
                dve.wait_ge(y_made[3], t + 1)
                v.tensor_tensor(rc_y[:, t, :], bank(Y0 + t % 2), x_tok[:, t, :], ALU.add).then_inc(y_added[3], 1)
                dve.wait_ge(y_added[3], t + 1)
                tile_stats(3, t, rc_y)
            for half in range(2):
                norm_half(3, half, rc_y, rc_n)
                for t in range(half * TB, (half + 1) * TB):
                    dve.wait_ge(x_normed[3], t + 1)
                    step(v.tensor_tensor(rc_n[:, t, :], rc_n[:, t, :], rc_gamma[:, :], ALU.mult))
                    step(v.tensor_tensor(rc_n[:, t, :], rc_n[:, t, :], rc_beta[:, :], ALU.add))
                    step(v.tensor_tensor(x_tok[:, t, :], rc_n[:, t, :], x_tok[:, t, :], ALU.add))
            for t in range(TT):
                tile_stats(4, t, x_tok)
            if stop == 4:
                for half in range(2):
                    norm_half(4, half, x_tok, x_tok)
                return
            for half in range(2):
                dve.wait_ge(std_made[4], half + 1)
                step(v.reciprocal(rstd[:, half * TB:(half + 1) * TB], std[:, half * TB:(half + 1) * TB]))
                for t in range(half * TB, (half + 1) * TB):
                    v.tensor_scalar(x_tok[:, t, :], x_tok[:, t, :], meanvar[:, t, 0:1], rstd[:, t:t + 1],
                                    ALU.subtract, ALU.mult).then_inc(ca_ss_made, 1)
            dve.wait_ge(ca_rr_made, 1)
            step(v.reciprocal(ca_rr[:, :], ca_ss[:, :]))
            dve.wait_ge(ca_load, 7 * 16)
            for t in range(TT):
                v.scalar_tensor_tensor(ca_xn[:, t, :], x_tok[:, t, :], ca_rr[:, t:t + 1], ca_nw[:, :],
                                       ALU.mult, ALU.mult).then_inc(x_normed[4], 1)

            dve.wait_ge(x_turned[4], TT)
            v.memset(ca_v[:, :, :, HD:2 * HD], 1.0).then_inc(ca_set, 1)
            v.memset(ca_mb[:, :, :, :].bitcast(F32), 1.0).then_inc(ca_set, 1)
            v.memset(ca_ks[MROW:MROW + 3, :, :].bitcast(F32), 1.0).then_inc(ca_set, 1)
            v.memset(ca_qs[MROW:MROW + 3, :, :].bitcast(F32), 1.0).then_inc(ca_set, 1)
            dve.wait_ge(ca_set, 4)
            dve.wait_ge(ca_mask_in, 16)

            def ca_mask_row(u):
                b, j = u // HEADS, u % 4
                if u % HEADS < 4:
                    if b:
                        dve.wait_ge(ca_st, CE * (u - 3))
                    v.tensor_scalar(ca_ks[MROW:KA, j, :], ca_row8[MROW:KA, b * CTX:(b + 1) * CTX], -1.0, -MASKED,
                                    ALU.add, ALU.mult).then_inc(ca_masked, 1)
                elif u % HEADS == 4:
                    v.engine_nop().then_inc(ca_masked, HEADS - 4)

            def ca_maximum(u, i):
                n = u * CU + i
                dve.wait_ge(ca_s, n + 1)
                v.tensor_reduce(ca_mx[:, i // 2, i % 2:i % 2 + 1], bank(n % 2), AX_X, ALU.max).then_inc(ca_max, 1)

            def ca_splits(u):
                dve.wait_ge(ca_max, CU * (u + 1))
                if u >= 2:
                    dve.wait_ge(ca_mt, u - 1)
                step(v.tensor_reduce(ca_m[:, 0, :], ca_mx[:, :, :], AX_X, ALU.max))
                step(v.tensor_scalar(ca_m[:, 1, :], ca_m[:, 0, :], -1.0e20, -1.0, ALU.max, ALU.mult))
                mb = ca_mb[:, u % 2, :, :]
                step(v.tensor_copy(mb[:, :, 1], ca_m[:, 1, :]))
                v.tensor_tensor(mb[:, :, 2], ca_m[:, 1, :], mb[:, :, 1].bitcast(F32), ALU.subtract
                                ).then_inc(ca_m_made, 1)

            def ca_split_low(j):
                g, part = j // 3, j % 3
                dve.wait_ge(ca_high, j + 1)
                if part < 2:
                    o = slice(part * 512, (part + 1) * 512)
                    v.tensor_tensor(ca_kp[:, g % 2, 1, o], bank(7), ca_kp[:, g % 2, 0, o].bitcast(F32), ALU.subtract
                                    ).then_inc(ca_low, 1)
                else:
                    v.scalar_tensor_tensor(ca_qp[:, g % 2, 1, :], bank(7), SCALE, ca_qp[:, g % 2, 0, :].bitcast(F32),
                                           ALU.mult, ALU.subtract).then_inc(ca_low, 1)

            def ca_group(g, piece):
                o = slice(piece * P, (piece + 1) * P)
                dve.wait_ge(ca_oz, 8 * (g + 1))
                if g or piece:
                    dve.wait_ge(ca_grp, 4 * g + piece)
                if g == 4:
                    dve.wait_ge(y_made[5], TB)
                step(v.tensor_scalar(ca_rz[:, 0:P], ca_zs[:, o], 1.0e-30, None, ALU.max))
                step(v.reciprocal(ca_rz[:, P:2 * P], ca_rz[:, 0:P]))
                v.tensor_tensor(ca_of[:, g % FT, o], ca_os[:, o], ca_rz[:, P:2 * P], ALU.mult).then_inc(ca_grp, 1)

            for j in range(3):
                ca_split_low(j)
            for b in range(BATCH):
                for t in range(KB):
                    g = b * (KB + TB) + t
                    dve.wait_ge(ca_vg, g + 1)
                    v.tensor_copy(ca_v[:, t, :, :].rearrange("p j (a d) -> p j a d", a=3)[:, :, 0:3:2, :],
                                  bank(2 + t % 2).rearrange("p (j a d) -> p j a d", j=HEADS // 2, a=2)
                                  ).then_inc(ca_vg_out, 1)
                if b == 0:
                    for u in range(2):
                        ca_mask_row(u)
                        for i in range(CU):
                            ca_maximum(u, i)
                        ca_splits(u)
                for h in range(HEADS):
                    u = b * HEADS + h
                    if u + 2 < UNITS:
                        ca_mask_row(u + 2)
                    for i in range(CU):
                        if u + 2 < UNITS:
                            ca_maximum(u + 2, i)
                        if (h % 4, i) in CA_PROJ and u // 4 + 1 < UNITS // 4:
                            ca_split_low(3 * (u // 4 + 1) + CA_PROJ[h % 4, i])
                        if h % 4 == 0 and h > 0 and i % 2 == 1:
                            ca_group(u // 4 - 1, i // 2)
                    if u + 2 < UNITS:
                        ca_splits(u + 2)
                for piece in range(4):
                    ca_group(4 * b + 3, piece)
                for t in range(b * TB, (b + 1) * TB):
                    dve.wait_ge(y_made[5], t + 1)
                    if t >= 2:
                        dve.wait_ge(y_added[5], t - 1)
                    v.tensor_tensor(ca_tmp[:, t % 2, :], bank(Y0 + t % 2), ca_gate[:, t % TB, :], ALU.mult
                                    ).then_inc(y_added[5], 1)
                    dve.wait_ge(y_added[5], t + 1)
                    step(v.tensor_tensor(x_tok[:, t, :], ca_tmp[:, t % 2, :], x_tok[:, t, :], ALU.add))
                    tile_stats(5, t, x_tok)
            for half in range(2):
                norm_half(5, half, x_tok, x_tok)
            if stop == 5:
                return

            dve.wait_ge(me_pr_made, 1)
            step(v.tensor_tensor(me_pb[:, :, :], me_pr[:, :, :],
                                 me_bias[:, :].unsqueeze(1).broadcast_to([P, TT, EXPERTS]), ALU.add))
            for t in range(TT):
                step(v.max(me_top[:, t, :], me_pb[:, t, :]))
                step(v.match_replace(me_rep[:, t, :], me_top[:, t, :], me_pb[:, t, :], MASKED))
            step(v.tensor_scalar(me_rep[:, :, :], me_rep[:, :, :], MASKED, None, ALU.is_equal))
            step(v.tensor_tensor(me_w[:, :, :], me_rep[:, :, :], me_pr[:, :, :], ALU.mult))
            step(v.tensor_reduce(me_sum[:, :], me_w[:, :, :], AX_X, ALU.add))
            step(v.reciprocal(me_rsum[:, :], me_sum[:, :]))
            step(v.scalar_tensor_tensor(me_w[:, :, :], me_w[:, :, :], 2.5,
                                        me_rsum[:, :].unsqueeze(2).broadcast_to([P, TT, EXPERTS]),
                                        ALU.mult, ALU.mult))

            def me_add(e, half):
                n = 2 * (e - 1) + half
                dve.wait_ge(me_y, n + 1)
                for t in range(TB):
                    tt = half * TB + t
                    y = bank(4 + n % 2)[:, t * LAT:(t + 1) * LAT]
                    w = me_w[:, tt, e - 1:e]
                    if e == 1:
                        v.tensor_scalar(me_acc[:, tt, :], y, w, None, ALU.mult).then_inc(me_y_out, 1)
                    else:
                        v.scalar_tensor_tensor(me_acc[:, tt, :], y, w, me_acc[:, tt, :], ALU.mult, ALU.add
                                               ).then_inc(me_y_out, 1)

            for e in range(EXPERTS + 1):
                for i in range(4):
                    n = 4 * e + i
                    m, c = i // 2, i % 2
                    dve.wait_ge(me_sqr, n + 1)
                    if e >= 3 and i == 0:
                        dve.wait_ge(me_y, 2 * (e - 2))
                    dst = me_us[:, m, c * 512:(c + 1) * 512] if e == 0 else me_u[:, e % 2, m, c * 512:(c + 1) * 512]
                    v.tensor_tensor(dst, bank(n % 2), me_rq[:, n % 4, :], ALU.mult).then_inc(me_u_made, 1)
                    if i % 2 == 1 and e >= 2:
                        me_add(e - 1, i // 2)
            me_add(EXPERTS, 0)
            me_add(EXPERTS, 1)
            add_and_norm(6, bias=False)

        @block.scalar
        def _(act):
            s = nc.scalar
            act.wait_ge(consts_set, 6)

            for n in range(SA_JOBS + 2):
                if n < SA_JOBS:
                    b, h, t, seen = sa_unit(n)
                    act.wait_ge(sa_nm_made, n + 1)
                    if n >= 3:
                        act.wait_ge(sa_turned, n - 2)
                    s.activation(sa_p[:, n % 3, 0:seen], sa_s[:, n % 3, 0:seen], ACT.Exp, bias=sa_nm[:, n:n + 1],
                                 scale=-1.0, accum_out=sa_sum[:, n:n + 1]).then_inc(sa_p_made, 1)
                if n >= 2:
                    m = n - 2
                    b, h, t, seen = sa_unit(m)
                    act.wait_ge(sa_turned, m + 1)
                    if m >= 3:
                        act.wait_ge(sa_pv, m - 2)
                    s.copy(sa_pt[:, m % 3, 0:seen], bank(3 + m % 3)[:, 0:seen]).then_inc(sa_pt_made, 1)
            for t in range(TT):
                act.wait_ge(sa_o_turned, t + 1)
                s.copy(sa_of[:, :, t * P:(t + 1) * P], bank(t % 3).rearrange("p (f t) -> p f t", f=FT)
                       ).then_inc(sa_of_made, 1)
            act_std(act, 0)
            act_copy_x(act, 0)
            if stop == 1:
                return

            for g in range(16):
                m, c = g // 4, g % 4
                act.wait_ge(qa_vl, g + 1)
                if g >= 8 and c == 0:
                    act.wait_ge(qa_v_q, m - 1)
                s.activation(qa_vf[:, m % 2, c * 512:(c + 1) * 512], bank(2 + g % 2), ACT.Identity,
                             bias=v_bias2[:, m:m + 1]).then_inc(qa_vl_out, 1)
            for t in range(KT):
                act.wait_ge(qa_vt, t + 1)
                s.copy(qa_v[:, t, :], bank(6 + t % 2).bitcast(BF16)[:, 0:D]).then_inc(qa_v_made, 1)

            turn_bank = bank(6).bitcast(BF16)
            stacks = [0]

            def stack(rows, dst):
                stacks[0] += 1
                act.wait_ge(qa_turned, stacks[0])
                s.copy(dst, turn_bank[0:rows, :]).then_inc(qa_stack, 1)

            def copy_stack(what, h):
                if what == "qa":
                    stack(3 * HD, qa_qa[:, :])
                elif what == "qb":
                    stack(KR, qa_qb2[:, h % 2, :])
                elif what < "kb":
                    stack(3 * HD, qa_ka[:, int(what[2]) * 1024:(int(what[2]) + 1) * 1024])
                else:
                    stack(KR, qa_kb2[:, h % 2, int(what[2]) * 1024:(int(what[2]) + 1) * 1024])

            def exponent(h, i):
                n = h * EU + i
                k = i % KT
                act.wait_ge(qa_st, n + 1)
                if n >= ERING:
                    act.wait_ge(qa_pv, n - ERING + 1)
                    if (n - ERING) % KT < POOLED:
                        act.wait_ge(qa_added, (n - ERING) // KT * (POOLED - 1) + max((n - ERING) % KT, 1))
                s.activation(qa_e(n), bank(2 + n % 3), ACT.Exp, bias=ln255[:, :],
                             scale=qa_sk[:, k, h:h + 1]).then_inc(qa_exp, 1)

            def out_chunk(h, c):
                o, z = qa_quadrants(h)
                act.wait_ge(qa_pv, (h * HALF + c + 1) * KT)
                if h % 4 == 0 and h > 0:
                    act.wait_ge(qa_grp, PIECES * (HALF * (h // 4 - 1) + c + 1))
                s.copy(qa_os[o, c, :], bank((5, 7)[c])[o, :]).then_inc(act_step, 1)
                s.copy(qa_zs[o, c, :], bank((5, 7)[c])[z, :]).then_inc(qa_oz, 1)

            act.wait_ge(qa_ints, 1)
            for x in qa_order[:9]:
                copy_stack(*x)
            for h in range(HEADS):
                for i in range(EU):
                    exponent(h, i)
                    if i == 1 and h > 0:
                        out_chunk(h - 1, 1)
                    if i == KT + LAG:
                        out_chunk(h, 0)
                    if i in QA_STEP and (QA_STEP[i][0], h + QA_STEP[i][1]) in qa_no:
                        copy_stack(QA_STEP[i][0], h + QA_STEP[i][1])
            out_chunk(HEADS - 1, 1)
            act_std(act, 1)
            act_copy_x(act, 1)
            if stop == 2:
                return

            def ff_copy_rv(t):
                act.wait_ge(ff_turned, t + 1)
                if t >= 2:
                    act.wait_ge(y_made[2], t - 1)
                s.copy(ff_rvt[:, t % 2, 0:4, :].rearrange("p a b -> p (a b)"), bank(2)).then_inc(act_step, 1)
                s.copy(ff_rvt[:, t % 2, 4:8, :].rearrange("p a b -> p (a b)"), bank(3)).then_inc(ff_rvt_made, 1)

            for t in range(TT + 1):
                if t < TT:
                    act.wait_ge(ff_vecs, t + 1)
                    if t >= 2:
                        act.wait_ge(ff_rv_made, t - 1)
                    s.copy(ff_vec[:, t % 2, 0:32, :].rearrange("p a b -> p (a b)"), bank(0)).then_inc(act_step, 1)
                    s.copy(ff_vec[:, t % 2, 32:64, :].rearrange("p a b -> p (a b)"), bank(1)).then_inc(ff_vec_out, 1)
                if t >= 1:
                    ff_copy_rv(t - 1)
            act_std(act, 2)
            act_copy_x(act, 2)
            if stop == 3:
                return

            for c in range(HALF):
                act.wait_ge(rc_zl, c + 1)
                s.copy(rc_z[:, c * 512:(c + 1) * 512], bank(c)).then_inc(rc_z_out, 1)
            for c in range(HALF):
                act.wait_ge(rc_gl, c + 1)
                s.activation(rc_d[:, c * 512:(c + 1) * 512], bank(2 + c), ACT.Sigmoid).then_inc(rc_d_out, 1)
            act_std(act, 3)
            act_std(act, 4)
            if stop == 4:
                return
            act.wait_ge(ca_ss_made, TT)
            for t in range(TT):
                s.activation(rc_y[:, t, :], x_tok[:, t, :], ACT.Square, scale=float(D) ** -0.5,
                             accum_out=ca_rr[:, t:t + 1]).then_inc(ca_xn_made, 1)
            act.wait_ge(ca_xn_made, TT)
            s.activation(ca_ss[:, :], ca_rr[:, :], ACT.Sqrt, bias=eps_rms[:, :]).then_inc(ca_rr_made, 1)
            act_copy_x(act, 4)

            act.wait_ge(ca_set, 4)

            def ca_split_high(j):
                g, part = j // 3, j % 3
                act.wait_ge(ca_proj, j + 1)
                if g >= 2 and part == 0:
                    for q in ca_stack:
                        act.wait_ge(q, 96 * (g - 1))
                if part < 2:
                    s.copy(ca_kp[:, g % 2, 0, part * 512:(part + 1) * 512], bank(7)).then_inc(ca_high, 1)
                else:
                    s.mul(ca_qp[:, g % 2, 0, :], bank(7), SCALE).then_inc(ca_high, 1)

            def copy_mrow(u):
                act.wait_ge(ca_mt, u + 1)
                s.copy(ca_qs[MROW:KE, u % 4, :], bank(6)[0:3, :]).then_inc(ca_mrow_made, 1)

            def ca_out(u):
                h = u % HEADS
                r = slice(h % 4 * HD, h % 4 * HD + HD)
                act.wait_ge(ca_pv, CE * (u + 1))
                if u >= 4 and h % 4 == 0:
                    act.wait_ge(ca_grp, u)
                o = bank(4 + u % 2)
                a = h % 2 * HD
                s.copy(ca_os[r, :], o[a:a + HD, :]).then_inc(ca_oz, 1)
                s.copy(ca_zs[r, :], o[HD - a:2 * HD - a, :]).then_inc(ca_oz, 1)

            for j in range(3):
                ca_split_high(j)
            for b in range(BATCH):
                for t in range(TB):
                    g = b * (KB + TB) + KB + t
                    act.wait_ge(ca_vg, g + 1)
                    act.wait_ge(ca_vg_out, g)
                    if b and t == 0:
                        act.wait_ge(y_added[5], TB)
                    s.activation(ca_gate[:, t, :], bank(2 + t % 2), ACT.Sigmoid).then_inc(ca_vg_out, 1)
                if b == 0:
                    copy_mrow(0)
                for h in range(HEADS):
                    u = b * HEADS + h
                    for k in range(CE):
                        n = u * CE + k
                        act.wait_ge(ca_st, n + 1)
                        if n >= 4:
                            act.wait_ge(ca_pv, n - 3)
                        s.activation(ca_e[:, n % 4, :], bank(2 + n % 2), ACT.Exp).then_inc(ca_exp, 1)
                        if k == 1 and h > 0:
                            ca_out(u - 1)
                        if (h % 4, k) in CA_PROJ and u // 4 + 1 < UNITS // 4:
                            ca_split_high(3 * (u // 4 + 1) + CA_PROJ[h % 4, k])
                        if k == 4 and u + 1 < UNITS:
                            copy_mrow(u + 1)
                ca_out(u)
            act_std(act, 5)
            act_copy_x(act, 5)
            if stop == 5:
                return

            for c in range(HALF):
                act.wait_ge(me_l, c + 1)
                s.copy(me_xl[:, c * 512:(c + 1) * 512], bank(c)).then_inc(me_l_out, 1)
            act.wait_ge(me_r, 1)
            s.activation(me_pr[:, :, :].rearrange("p a b -> p (a b)"), bank(2)[:, 0:TT * EXPERTS], ACT.Sigmoid
                         ).then_inc(me_pr_made, 1)
            for n in range(ME_UNITS):
                act.wait_ge(me_h, n + 1)
                if n >= 4:
                    act.wait_ge(me_u_made, n - 3)
                s.activation(me_rl[:, n % 4, :], bank(2 + n % 2), ACT.Relu).then_inc(me_relu, 1)
                act.wait_ge(me_relu, n + 1)
                s.activation(me_rq[:, n % 4, :], me_rl[:, n % 4, :], ACT.Square).then_inc(me_sqr, 1)
            for c in range(2):
                act.wait_ge(me_at, c + 1)
                s.copy(me_acct[:, c * 4:(c + 1) * 4, :].rearrange("p a b -> p (a b)"), bank(c)).then_inc(me_at_out, 1)
            act_std(act, 6)

        @block.gpsimd
        def _(pool):
            g = nc.gpsimd
            steps = [0]

            def step(ins):
                steps[0] += 1
                ins.then_inc(pool_step, 1)
                pool.wait_ge(pool_step, steps[0])

            def add_bias(i, bias, ready, counts):
                for t in range(TT):
                    pool.wait_ge(ready, counts(t))
                    g.tensor_tensor(x_tok[:, t, :], x_tok[:, t, :], bias[:, :], ALU.add).then_inc(bias_in[i], 1)

            pool.wait_ge(consts_in, 13 * 16)
            add_bias(0, sa_ob, x_in, lambda t: 16)
            if stop == 1:
                return
            add_bias(1, qa_pb, x_turned[0], lambda t: t + 1)
            pool.wait_ge(qa_ints, 1)
            pool.wait_ge(qa_k, KT)

            def split(dst, ints, scale, t1, t2):
                step(g.tensor_tensor(t1, ints, scale, ALU.mult))
                step(g.tensor_tensor(dst[0], ints, scale, ALU.mult))
                step(g.tensor_tensor(t2, t1, dst[0], ALU.subtract))
                step(g.tensor_tensor(dst[1], t1, dst[0], ALU.subtract))
                return g.tensor_tensor(dst[2], t2, dst[1], ALU.subtract)

            pool.wait_ge(qa_qt_zero, 1)

            def split_k(h):
                if h >= 1:
                    pool.wait_ge(qa_turned, qa_no["ka1", h - 1])
                split([qa_kt[:, :, j, :] for j in range(3)], qa_kint[:, :, h, 0:HD],
                      qa_sk[:, :, h].unsqueeze(2).broadcast_to([P, KT, HD]), qa_t1[:, :, :], qa_t2[:, :, :]
                      ).then_inc(qa_kt_made, 1)

            def split_q(h):
                if h >= 1:
                    pool.wait_ge(qa_turned, qa_no["qb", h - 1])
                split([qa_qt[:, :, j, 0:HD] for j in range(3)], qa_qint[:, :, h * HD:(h + 1) * HD],
                      qa_sq[:, :, h].unsqueeze(2).broadcast_to([P, TT, HD]), qa_t3[:, :, :], qa_t4[:, :, :]
                      ).then_inc(qa_qt_made, 1)

            def sum_chunk(h, c):
                n0 = h * EU + c * KT
                dst = qa_sum[c][:, :]
                if h >= 1:
                    pool.wait_ge(qa_pv, n0 - EU + KT)
                for k in range(1, POOLED):
                    pool.wait_ge(qa_exp, n0 + k + 1)
                    if k > 1:
                        pool.wait_ge(qa_added, (h * HALF + c) * (POOLED - 1) + k - 1)
                    g.tensor_tensor(dst, qa_e(n0) if k == 1 else dst, qa_e(n0 + k), ALU.add).then_inc(qa_added, 1)

            split_k(0)
            split_q(0)
            split_k(1)
            for h in range(HEADS):
                sum_chunk(h, 0)
                if h + 2 < HEADS:
                    split_k(h + 2)
                sum_chunk(h, 1)
                if h + 1 < HEADS:
                    split_q(h + 1)
            if stop == 2:
                return
            add_bias(2, ff_bias, x_turned[1], lambda t: t + 1)


def kernel(**inputs):
    import numpy as np
    import concourse.bacc as bacc
    from concourse.bass_utils import run_bass_kernel_spmd

    a = {k: np.asarray(v) for k, v in inputs.items()}

    def tiles(w):
        return w.reshape(-1, P, w.shape[-1]).transpose(1, 0, 2)

    x = a["x"].reshape(TOK, D)
    ctx = a["ctx_2048"].reshape(KEYS, D)
    mask = a["mask_BxS2_bk0"].reshape(KEYS)
    lanes, cols = np.arange(P)[:, None], np.arange(SEQ)[None, :]
    past = cols - (SEQ - P) - lanes
    arrays = {
        "x_tok": tiles(x), "x_feat": tiles(x.T), "ctx": tiles(ctx.T),
        "ctx0": tiles(ctx[:CTX].T), "ctx1": tiles(ctx[CTX:].T),
        "ident": np.eye(P, dtype=np.float32),
        "decay": np.where(past > 0, -MASKED, -past).astype(np.float32),
        "sa_wq": tiles(a["L0_attn_q_w"].T), "sa_wk": tiles(a["L0_attn_k_w"].T),
        "sa_wv": tiles(a["L0_attn_v_w"].T), "sa_wo": tiles(a["L0_attn_o_w"].T),
        "q_b": a["L0_attn_q_b"].reshape(FT, P).T, "k_b": a["L0_attn_k_b"].reshape(FT, P).T,
        "sa_vb": a["L0_attn_v_b"], "sa_ob": a["L0_attn_o_b"],
        "qa_wq": tiles(a["L0_xattn_Wq"]), "qa_wkv": tiles(a["L0_xattn_Wkv"]), "qa_wp": tiles(a["L0_xattn_Wp"]),
        "qa_qb": a["L0_xattn_bq"], "qa_kb": a["L0_xattn_bkv"][:D], "qa_pb": a["L0_xattn_bp"],
        "qa_vb": a["L0_xattn_bkv"][D:].reshape(FT, P).T,
        "ff_a": tiles(a["L0_ffn_A"].reshape(ARROWS * RANK, D).T),
        "ff_b": tiles(a["L0_ffn_B"].transpose(0, 2, 1).reshape(ARROWS * RANK, D)),
        "ff_w": tiles(a["L0_ffn_W"].T), "ff_bias": a["L0_ffn_bias"],
        "rc_win": tiles(a["L1_attn_W_in"]), "rc_wout": a["L1_attn_W_out"],
        "rc_wf_d": a["L1_attn_W_fwd"][:, :DI], "rc_wf_g": a["L1_attn_W_fwd"][:, DI:],
        "rc_wb_d": a["L1_attn_W_bwd"][:, :DI], "rc_wb_g": a["L1_attn_W_bwd"][:, DI:],
        "rc_gamma": a["L1_attn_gamma"], "rc_beta": a["L1_attn_beta"],
        "ca_nw": a["L1_xattn_norm_w"], "ca_wq": tiles(a["L1_xattn_wq"].T), "ca_wk": tiles(a["L1_xattn_wk"].T),
        "ca_wv": tiles(a["L1_xattn_wv"].T), "ca_wo": tiles(a["L1_xattn_wo"].T), "ca_wg": tiles(a["L1_xattn_wg"].T),
        "mask_row": mask,
        "me_s1": tiles(a["L1_ffn_sw1"].T), "me_sg": tiles(a["L1_ffn_swg"].T), "me_s2": tiles(a["L1_ffn_sw2"].T),
        "me_wd": tiles(a["L1_ffn_Wdown"].T), "me_wu": a["L1_ffn_Wup"].T, "me_wr": tiles(a["L1_ffn_Wg"].T),
        "me_w1": a["L1_ffn_rw1"].transpose(2, 0, 1), "me_wg": a["L1_ffn_rwg"].transpose(2, 0, 1),
        "me_w2": tiles(a["L1_ffn_rw2"].transpose(0, 2, 1).reshape(EXPERTS * HID, LAT)),
        "me_bias": a["L1_ffn_biases"],
    }
    arrays = {f"in_{k}": np.ascontiguousarray(v) for k, v in arrays.items()}
    nc = bacc.Bacc("TRN2", target_bir_lowering=False, num_devices=1)
    dram = {k[3:]: nc.dram_tensor(k, v.shape, mybir.dt.from_np(v.dtype), kind="ExternalInput").ap()
            for k, v in arrays.items()}
    out = nc.dram_tensor("out_x", (TOK, D), F32, kind="ExternalOutput").ap()
    decoder_program(nc, dram, out, STOP)
    r = run_bass_kernel_spmd(nc, [arrays], core_ids=[0])
    return r.results[0]["out_x"].reshape(BATCH, SEQ, D)


STOP = 6
```

```python
from contextlib import ExitStack

import concourse.bass as bass
from concourse import mybir

F32 = mybir.dt.float32
BF16 = mybir.dt.bfloat16
F32R = mybir.dt.float32r
U8 = mybir.dt.uint8
ALU = mybir.AluOpType
ACT = mybir.ActivationFunctionType
AX_X = mybir.AxisListType.X

P = 128
BATCH, SEQ, CTX, D, HEADS = 2, 512, 1024, 512, 16
HD = D // HEADS
FT = D // P
TOK = BATCH * SEQ
TT = TOK // P
TB = SEQ // P
KEYS = BATCH * CTX
KT = KEYS // P
KB = CTX // P
HALF = TOK // 512
ARROWS, RANK = 64, 16
EXPERTS, LAT, HID, TOPK = 16, 128, 256, 8
DI = 64
SCALE = float(HD) ** -0.5
ROUND = 1.5 * 2.0 ** 23
LN255 = 5.541263545158426
MASKED = -1.0e30
LN_EPS = 1e-5
RMS_EPS = 1e-6
KIB = 1024


def decoder_program(nc, dram, out):
    with ExitStack() as ctx:
        base = (nc.sbuf_base + 255) // 256 * 256
        ctx.enter_context(nc.sbuf_tensor("arena", [P, base - nc.sbuf_base + 206 * KIB], U8))

        def at(name, kib, shape, dt=F32):
            return nc.alloc_sbuf_tensor_at(name, shape, dt, offset=base + int(kib * KIB))

        def sem(name):
            return ctx.enter_context(nc.semaphore(name))

        x_tok = at("x_tok", 0, [P, TT, D])
        x_feat = at("x_feat", 16, [P, FT, TOK])
        WA, WB, CONST, BC, R = 32, 72, 112, 118, 134
        ident = at("ident", CONST, [P, P])
        ident_bf = at("ident_bf", CONST + 0.5, [P, P], BF16)
        decay = at("decay", CONST + 0.75, [P, SEQ])
        ln255 = at("ln255", CONST + 2.75, [P, 1])
        eps_ln = at("eps_ln", CONST + 2.8125, [P, 1])
        eps_rms = at("eps_rms", CONST + 2.875, [P, 1])
        stats = at("stats", CONST + 3, [P, TT, 6])
        meanvar = at("meanvar", CONST + 3.25, [P, TT, 2])
        std = at("std", CONST + 3.5, [P, TT])
        rstd = at("rstd", CONST + 3.625, [P, TT])
        ones_f = at("ones_f", CONST + 3.75, [P, HD])
        q_bias = at("q_bias", CONST + 4.25, [P, FT])
        k_bias = at("k_bias", CONST + 4.375, [P, FT])
        v_bias2 = at("v_bias2", CONST + 4.5, [P, FT])

        psum = ctx.enter_context(nc.psum_tensor("psum", [P, 8, 512], F32))

        def bank(i):
            return psum[:, i, :]

        SUB = 7
        y_made = [sem(f"y_made{i}") if i not in (4,) else None for i in range(SUB)]
        y_added = [sem(f"y_added{i}") if i not in (4,) else None for i in range(SUB)]
        var_made = [sem(f"var_made{i}") for i in range(SUB)]
        std_made = [sem(f"std_made{i}") for i in range(SUB)]
        x_normed = [sem(f"x_normed{i}") for i in range(SUB)]
        x_turned = [sem(f"x_turned{i}") if i not in (3, 6) else None for i in range(SUB)]
        xf_made = [sem(f"xf_made{i}") if i not in (3, 6) else None for i in range(SUB)]
        bias_in = [sem(f"bias_in{i}") if i not in (3, 4, 5, 6) else None for i in range(SUB)]
        dve_step = sem("dve_step")
        act_step = sem("act_step")
        pool_step = sem("pool_step")
        consts_in = sem("consts_in")
        consts_set = sem("consts_set")
        out_done = sem("out_done")
        Y0, XT0 = 4, 6

        def pe_turn_x(pe, i, src=x_tok):
            for t in range(TT):
                pe.wait_ge(x_normed[i], t + 1)
                if t >= 2:
                    pe.wait_ge(xf_made[i], t - 1)
                for f in range(FT):
                    ins = nc.tensor.transpose(bank(XT0 + t % 2)[:, f * P:(f + 1) * P],
                                              src[:, t, f * P:(f + 1) * P], ident[:, :])
                ins.then_inc(x_turned[i], 1)

        def act_copy_x(act, i):
            for t in range(TT):
                act.wait_ge(x_turned[i], t + 1)
                nc.scalar.copy(x_feat[:, :, t * P:(t + 1) * P],
                               bank(XT0 + t % 2).rearrange("p (f t) -> p f t", f=FT)
                               ).then_inc(xf_made[i], 1)

        def act_std(act, i):
            for half in range(2):
                act.wait_ge(var_made[i], half + 1)
                nc.scalar.activation(std[:, half * TB:(half + 1) * TB],
                                     meanvar[:, half * TB:(half + 1) * TB, 1], ACT.Sqrt,
                                     bias=eps_ln[:, :]).then_inc(std_made[i], 1)

        sa_wq = at("sa_wq", WA, [P, FT, D])
        sa_wk = at("sa_wk", WA + 8, [P, FT, D])
        sa_wv = at("sa_wv", WA + 16, [P, FT, D])
        sa_wo = at("sa_wo", WA + 32, [P, FT, D])
        sa_vb = at("sa_vb", BC, [P, D])
        sa_ob = at("sa_ob", BC + 2, [P, D])
        sa_q = at("sa_q", R, [P, FT, TOK])
        sa_k = at("sa_k", R + 16, [P, FT, TOK])
        sa_v = at("sa_v", R + 32, [P, TT, D])
        sa_s = at("sa_s", R + 48, [P, 3, SEQ])
        sa_p = at("sa_p", R + 54, [P, 3, SEQ])
        sa_pt = at("sa_pt", R + 60, [P, 3, SEQ])
        sa_nm = at("sa_nm", R + 66, [P, P])
        sa_sum = at("sa_sum", R + 66.5, [P, P])
        sa_rs = at("sa_rs", R + 67, [P, P])
        sa_of = x_feat
        sa_high = [at("sa_high0", WA + 24, [P, 2, TOK], F32R), at("sa_high1", WB + 32, [P, 2, TOK], F32R)]
        sa_qs = at("sa_qs", WA, [3 * HD, 2, TOK], F32R)
        sa_ks = at("sa_ks", WA + 8, [3 * HD, 2, TOK], F32R)
        sa_high_made, sa_low_made = sem("sa_high_made"), sem("sa_low_made")
        sa_stack = [sem(f"sa_stack{j}") for j in range(2)]
        sa_normed = sem("sa_normed")
        sa_first_in, sa_qkv_in, sa_wo_in, x_in = sem("sa_first_in"), sem("sa_qkv_in"), sem("sa_wo_in"), sem("x_in")
        sa_lin, sa_lin_out = sem("sa_lin"), sem("sa_lin_out")
        sa_scored, sa_nm_made, sa_p_made = sem("sa_scored"), sem("sa_nm_made"), sem("sa_p_made")
        sa_turned, sa_pt_made, sa_pv = sem("sa_turned"), sem("sa_pt_made"), sem("sa_pv")
        sa_of_made = sem("sa_of_made")
        SA_LIN = 3 * 8
        SA_HEAD, SA_GROUP = BATCH * TB, 4 * BATCH * TB
        SA_JOBS = BATCH * HEADS * TB

        def sa_unit(n):
            b, h, t = n // TB % BATCH, n // (BATCH * TB), n % TB
            return b, h, t, (t + 1) * P

        qa_ctx = at("qa_ctx", WA, [P, FT, KEYS])
        qa_wp = at("qa_wp", WB, [P, FT, D])
        qa_wq = at("qa_wq", WB + 8, [P, FT, D])
        qa_wkv = at("qa_wkv", WB + 16, [P, FT, 2 * D])
        qa_qb = at("qa_qb", BC + 4, [P, D])
        qa_kb = at("qa_kb", BC + 6, [P, D])
        qa_pb = at("qa_pb", BC + 8, [P, D])
        qa_load, qa_ctx_in = sem("qa_load"), sem("qa_ctx_in")
        REP = HD + 3
        KR = 3 * REP
        qa_kint = at("qa_kint", R, [P, KT, HEADS, REP], BF16)
        qa_v = at("qa_v", R + 18, [P, KT, D], BF16)
        qa_qint = at("qa_qint", R + 34, [P, TT, D], BF16)
        qa_qa = at("qa_qa", R + 42, [3 * HD, TOK], BF16)
        qa_ka = at("qa_ka", R + 44, [3 * HD, KEYS], BF16)
        qa_kb2 = at("qa_kb2", R + 48, [KR, 2, KEYS], BF16)
        qa_qb2 = at("qa_qb2", R + 56, [KR, 2, TOK], BF16)
        qa_e_lo = at("qa_e_lo", WA, [P, 4, 512])
        qa_e_hi = at("qa_e_hi", R + 60, [P, 4, 512])
        qa_r = at("qa_r", R + 68, [P, 4, 512], BF16)
        qa_vf = at("qa_vf", R + 42, [P, 2, KEYS])
        qa_x1 = at("qa_x1", R + 58, [P, 2, D])
        qa_x2 = at("qa_x2", R + 62, [P, 2, D])
        qa_vint = x_feat[:, :, :].bitcast(BF16)
        qa_of = x_feat
        qa_kt = at("qa_kt", WA + 8, [P, KT, 3, HD], BF16)
        qa_qt = at("qa_qt", WA + 11, [P, TT, 3, REP], BF16)
        qa_krep = at("qa_krep", WA + 36, [P, KT, 3, REP], BF16)
        qa_qrep = at("qa_qrep", BC, [P, TT, 3, HD], BF16)
        qa_t1 = at("qa_t1", WA + 13, [P, KT, HD])
        qa_t2 = at("qa_t2", WA + 15, [P, KT, HD])
        qa_t3 = at("qa_t3", WA + 17, [P, TT, HD])
        qa_t4 = at("qa_t4", WA + 18, [P, TT, HD])
        qa_os = at("qa_os", WA + 19, [P, HALF, 512])
        qa_zs = at("qa_zs", WA + 23, [P, HALF, 512])
        qa_rz = at("qa_rz", WA + 27, [P, 512])
        qa_sum = [at("qa_sum0", WA + 29, [P, 512]), at("qa_sum1", BC + 2, [P, 512])]
        qa_mx8 = at("qa_mx8", WA + 31, [P, TT, 4])
        qa_m = at("qa_m", WA + 31.25, [P, 4, TT])
        qa_sq = at("qa_sq", WA + 32, [P, TT, HEADS])
        qa_sk = at("qa_sk", WA + 32.5, [P, KT, HEADS])
        qa_rk = at("qa_rk", WA + 33.5, [P, KT, HEADS])
        qa_rk1 = at("qa_rk1", WA + 34.5, [P, KT, HEADS])
        qa_sv = at("qa_sv", WA + 35.5, [P, FT])
        qa_rv = at("qa_rv", WA + 35.5625, [P, FT])
        qa_sm = at("qa_sm", WA + 35.625, [P, 2, HEADS])
        qa_q, qa_q_out = sem("qa_q"), sem("qa_q_out")
        qa_k, qa_k_out = sem("qa_k"), sem("qa_k_out")
        qa_vl, qa_vl_out = sem("qa_vl"), sem("qa_vl_out")
        qa_v_q, qa_vt, qa_v_made = sem("qa_v_q"), sem("qa_vt"), sem("qa_v_made")
        qa_ints, qa_qt_zero = sem("qa_ints"), sem("qa_qt_zero")
        qa_krep_made, qa_qrep_made = sem("qa_krep_made"), sem("qa_qrep_made")
        qa_kt_made, qa_qt_made, qa_m_made = sem("qa_kt_made"), sem("qa_qt_made"), sem("qa_m_made")
        qa_turned, qa_stack = sem("qa_turned"), sem("qa_stack")
        qa_s, qa_max, qa_st, qa_exp, qa_rnd = sem("qa_s"), sem("qa_max"), sem("qa_st"), sem("qa_exp"), sem("qa_rnd")
        qa_pv, qa_oz, qa_grp = sem("qa_pv"), sem("qa_oz"), sem("qa_grp")
        SU = TT * 4
        EU = HALF * KT
        PIECES = 4
        LAG = 4
        POOLED = 7
        ERING = 8
        qa_added = sem("qa_added")

        def qa_quadrants(h):
            return (slice(h % 4 * HD, h % 4 * HD + HD), slice((h + 1) % 4 * HD, (h + 1) % 4 * HD + HD))

        def qa_e(n):
            return (qa_e_lo if n % ERING < 4 else qa_e_hi)[:, n % 4, :]

        SPREAD = 27
        QA_STEP = {18: ("kb0", 1), 20: ("kb1", 1), 27: ("qa", 2), 28: ("ka0", 2), 30: ("ka1", 2), 31: ("qb", 1)}
        qa_order = [("qa", 0), ("ka0", 0), ("ka1", 0), ("kb0", 0), ("kb1", 0), ("qb", 0),
                    ("qa", 1), ("ka0", 1), ("ka1", 1)]
        qa_order += [(what, h + ahead) for h in range(HEADS) for what, ahead in QA_STEP.values()
                     if h + ahead < HEADS]
        qa_no = {x: i + 1 for i, x in enumerate(qa_order)}

        def score_units(i):
            return range(i * SU // SPREAD, (i + 1) * SU // SPREAD) if i < SPREAD else range(0)


        ff_a = at("ff_a", WB + 8, [P, FT, ARROWS * RANK])
        ff_b = at("ff_b", WB + 24, [P, TT, D])
        ff_w = at("ff_w", WA, [P, FT, D])
        ff_bias = at("ff_bias", BC + 10, [P, D])
        ff_load = sem("ff_load")
        ff_vec = at("ff_vec", R, [P, 2, ARROWS, RANK])
        ff_sq = at("ff_sq", R + 8, [P, ARROWS, RANK])
        ff_rv = at("ff_rv", R + 12, [P, 2, ARROWS * RANK])
        ff_rvt = at("ff_rvt", R + 20, [P, 2, TT, P])
        ff_norm = at("ff_norm", R + 28, [P, ARROWS + 4])
        ff_rep = at("ff_rep", R + 28.5, [P, ARROWS + 4])
        ff_route = at("ff_route", R + 29, [P, ARROWS])
        ff_top = at("ff_top", R + 29.25, [P, 8])
        ff_v = at("ff_v", R + 29.5, [P, RANK])
        ff_vecs, ff_vec_out, ff_rv_made = sem("ff_vecs"), sem("ff_vec_out"), sem("ff_rv_made")
        ff_turned, ff_rvt_made = sem("ff_turned"), sem("ff_rvt_made")

        rc_win = at("rc_win", R + 60, [P, FT, P])
        rc_wd = at("rc_wd", R + 62, [P, P])
        rc_wg = at("rc_wg", R + 62.5, [P, P])
        rc_wout = at("rc_wout", R + 63, [P, D])
        rc_gamma = at("rc_gamma", BC + 12, [P, D])
        rc_beta = at("rc_beta", BC + 14, [P, D])
        rc_load, rc_set = sem("rc_load"), sem("rc_set")
        rc_z = at("rc_z", R, [P, TOK])
        rc_d = at("rc_d", R + 4, [P, TOK])
        rc_g = at("rc_g", R + 8, [P, TOK])
        rc_h = at("rc_h", R + 12, [P, TOK])
        rc_y = at("rc_y", R + 40, [P, TT, D])
        rc_n = at("rc_n", R + 24, [P, TT, D])
        rc_zl, rc_z_out, rc_gl, rc_d_out, rc_h_made = (sem(f"rc_{n}") for n in ("zl", "z_out", "gl", "d_out", "h_made"))
        rc_done, rc_beta_in = sem("rc_done"), sem("rc_beta_in")

        ca_wk = at("ca_wk", WA + 8, [P, FT, D])
        ca_wv = at("ca_wv", WA + 16, [P, FT, D])
        ca_wq = at("ca_wq", WA + 24, [P, FT, D])
        ca_wg = at("ca_wg", WA + 32, [P, FT, D])
        ca_wo = at("ca_wo", WA, [P, FT, D])
        ca_nw = at("ca_nw", BC, [P, D])
        ca_load, ca_ctx_in = sem("ca_load"), sem("ca_ctx_in")
        ca_ctx = at("ca_ctx", WB, [P, FT, CTX])
        ca_kp = at("ca_kp", WB + 16, [P, 2, 2, CTX], F32R)
        ca_qp = at("ca_qp", WB + 32, [P, 2, 2, SEQ], F32R)
        ca_v = at("ca_v", R, [P, KB, HEADS // 2, 3 * HD])
        ca_gate = at("ca_gate", R + 24, [P, TB, D])
        ca_e = at("ca_e", R + 32, [P, 4, 512])
        ca_ks = at("ca_ks", R + 40, [P, 4, CTX], F32R)
        ca_qs = at("ca_qs", R + 56, [P, 4, SEQ], F32R)
        ca_of = at("ca_of", R + 64, [P, FT, SEQ])
        ca_xn = at("ca_xn", R + 24, [P, TT, D])
        ca_os = at("ca_os", BC + 4, [P, 512])
        ca_zs = at("ca_zs", BC + 6, [P, 512])
        ca_rz = at("ca_rz", BC + 8, [P, 512])
        ca_tmp = at("ca_tmp", BC + 10, [P, 2, D])
        ca_row8 = at("ca_row8", BC + 14, [P, KEYS], U8)
        ca_m = at("ca_m", CONST + 4.75, [P, 4, TB])
        ca_mx = at("ca_mx", CONST + 4.8125, [P, TB, 2])
        ca_mb = at("ca_mb", CONST + 4.875, [P, 2, TB, 3], F32R)
        ca_ss = at("ca_ss", CONST + 5, [P, TT])
        ca_rr = at("ca_rr", CONST + 5.0625, [P, TT])
        MROW, KA, KE = 3 * HD, 3 * HD + 1, 3 * HD + 3
        ca_mask_in, ca_set = sem("ca_mask_in"), sem("ca_set")
        ca_ss_made, ca_rr_made, ca_xn_made = sem("ca_ss_made"), sem("ca_rr_made"), sem("ca_xn_made")
        ca_vg, ca_vg_out = sem("ca_vg"), sem("ca_vg_out")
        ca_proj, ca_high, ca_low = sem("ca_proj"), sem("ca_high"), sem("ca_low")
        ca_stack = [sem(f"ca_stack{j}") for j in range(4)]
        ca_masked = sem("ca_masked")
        ca_s, ca_max, ca_m_made, ca_mt, ca_mrow_made = (sem(f"ca_{n}") for n in ("s", "max", "m_made", "mt", "mrow_made"))
        ca_st, ca_exp, ca_pv, ca_oz, ca_grp = (sem(f"ca_{n}") for n in ("st", "exp", "pv", "oz", "grp"))
        CU = TB * 2
        CE = KB
        UNITS = BATCH * HEADS
        CA_PROJ = {(0, 2): 0, (0, 6): 1, (1, 2): 2}

        me_w1 = at("me_w1", WA, [P, EXPERTS, HID])
        me_wg = at("me_wg", WA + 16, [P, EXPERTS, HID])
        me_w2 = at("me_w2", WB, [P, EXPERTS * 2, LAT])
        me_s1 = at("me_s1", WB + 16, [P, FT, HID])
        me_sg = at("me_sg", WB + 20, [P, FT, HID])
        me_s2 = at("me_s2", WB + 24, [P, 2, D])
        me_wd = at("me_wd", WB + 28, [P, FT, LAT])
        me_wu = at("me_wu", WB + 30, [P, D])
        me_wr = at("me_wr", WB + 32, [P, FT, EXPERTS])
        me_bias = at("me_bias", CONST + 5.25, [P, EXPERTS])
        me_w1l = at("me_w1l", WA, [P, EXPERTS, HID], F32R)
        me_wgl = at("me_wgl", WA + 16, [P, EXPERTS, HID], F32R)
        me_w1h = at("me_w1h", R + 55.5, [P, EXPERTS, HID], F32R)
        me_wgh = at("me_wgh", BC, [P, EXPERTS, HID], F32R)
        me_xh = at("me_xh", WA + 32, [P, TOK], F32R)
        ME_HALVES = [(w, slice(j * EXPERTS // 2, (j + 1) * EXPERTS // 2)) for w in range(2) for j in range(2)]
        me_low, me_xlow = sem("me_low"), sem("me_xlow")
        me_load, me_load2 = sem("me_load"), sem("me_load2")
        me_xl = at("me_xl", R, [P, TOK], F32R)
        me_us = at("me_us", R + 4, [P, 2, TOK])
        me_u = at("me_u", R + 12, [P, 2, 2, TOK])
        me_rl = at("me_rl", R + 28, [P, 4, 512])
        me_rq = at("me_rq", R + 36, [P, 4, 512])
        me_acc = at("me_acc", R + 44, [P, TT, LAT])
        me_acct = at("me_acct", R + 48, [P, TT, LAT])
        me_pr = at("me_pr", R + 52, [P, TT, EXPERTS])
        me_pb = at("me_pb", R + 52.5, [P, TT, EXPERTS])
        me_rep = at("me_rep", R + 53, [P, TT, EXPERTS])
        me_w = at("me_w", R + 53.5, [P, TT, EXPERTS])
        me_top = at("me_top", R + 54, [P, TT, 8])
        me_sum = at("me_sum", R + 54.25, [P, TT])
        me_rsum = at("me_rsum", R + 54.375, [P, TT])
        me_l, me_high, me_r, me_pr_made = (sem(f"me_{n}") for n in ("l", "high_made", "r", "pr_made"))
        me_h, me_relu, me_sqr, me_u_made = (sem(f"me_{n}") for n in ("h", "relu", "sqr", "u_made"))
        me_y, me_y_out, me_at, me_at_out = (sem(f"me_{n}") for n in ("y", "y_out", "at", "at_out"))
        ME_UNITS = 4 * (EXPERTS + 1)

        block = ctx.enter_context(nc.Block())

        @block.sync
        def _(sp):
            def load(dst, name, s):
                sp.dma_start(dst, dram[name]).then_inc(s, 16)

            load(sa_wq[:, :, :], "sa_wq", sa_first_in)
            sp.dma_start(x_feat[:, :, 0:512], dram["x_feat"][:, :, 0:512]).then_inc(sa_first_in, 16)
            sp.dma_start(x_feat[:, :, 512:TOK], dram["x_feat"][:, :, 512:TOK]).then_inc(sa_qkv_in, 16)
            load(sa_wk[:, :, :], "sa_wk", sa_qkv_in)
            load(sa_wv[:, :, :], "sa_wv", sa_qkv_in)
            load(q_bias[:, :], "q_b", consts_in)
            load(k_bias[:, :], "k_b", consts_in)
            load(v_bias2[:, :], "qa_vb", consts_in)
            load(ident[:, :], "ident", consts_in)
            load(decay[:, :], "decay", consts_in)
            for dst, name in ((sa_vb, "sa_vb"), (sa_ob, "sa_ob"), (qa_qb, "qa_qb"), (qa_kb, "qa_kb"),
                              (qa_pb, "qa_pb"), (ff_bias, "ff_bias"), (rc_gamma, "rc_gamma"),
                              (rc_beta, "rc_beta")):
                sp.dma_start(dst[:, :], dram[name].partition_broadcast(P)).then_inc(consts_in, 16)
            load(x_tok[:, :, :], "x_tok", x_in)
            load(sa_wo[:, :, :], "sa_wo", sa_wo_in)
            load(qa_wq[:, :, :], "qa_wq", qa_load)
            load(qa_wkv[:, :, :], "qa_wkv", qa_load)
            load(qa_wp[:, :, :], "qa_wp", qa_load)
            sp.wait_ge(sa_lin, 16)
            for h in range(HEADS):
                sp.wait_ge(sa_low_made, 2 * (h // 4 + 1))
                if h >= 2:
                    sp.wait_ge(sa_scored, SA_HEAD * (h - 1))
                r = slice(h % 4 * HD, h % 4 * HD + HD)
                high, low = sa_high[h // 4 % 2], (sa_q, sa_k)
                for i, (qlow, klow) in enumerate(((0, 0), (1, 0), (0, 1))):
                    o = slice(i * HD, (i + 1) * HD)
                    for stack, which, is_low in ((sa_qs, 0, qlow), (sa_ks, 1, klow)):
                        part = low[which][r, h // 4, :] if is_low else high[r, which, :].bitcast(F32)
                        sp.dma_start(stack[o, h % 2, :].bitcast(F32), part).then_inc(sa_stack[h % 2], 16)
            sp.wait_ge(sa_lin, SA_LIN)
            sp.wait_ge(sa_scored, SA_JOBS)
            load(qa_ctx[:, :, :], "ctx", qa_ctx_in)
            sp.wait_ge(qa_vl, 16)
            sp.wait_ge(qa_k, KT)
            sp.wait_ge(qa_q, TT)
            load(ff_a[:, :, :], "ff_a", ff_load)
            load(ff_b[:, :, :], "ff_b", ff_load)
            sp.wait_ge(y_made[1], TT)
            sp.wait_ge(qa_grp, PIECES * HALF * HEADS // 4)
            sp.wait_ge(qa_rnd, HEADS * EU)
            load(ff_w[:, :, :], "ff_w", ff_load)
            sp.wait_ge(rc_set, 1)
            load(rc_win[:, :, 0:DI], "rc_win", rc_load)
            load(rc_win[:, :, DI:P], "rc_win", rc_load)
            load(rc_wd[0:DI, 0:DI], "rc_wf_d", rc_load)
            load(rc_wd[DI:P, DI:P], "rc_wb_d", rc_load)
            load(rc_wg[0:DI, 0:DI], "rc_wf_g", rc_load)
            load(rc_wg[DI:P, DI:P], "rc_wb_g", rc_load)
            load(rc_wout[:, :], "rc_wout", rc_load)
            load(ca_wk[:, :, :], "ca_wk", ca_load)
            load(ca_wv[:, :, :], "ca_wv", ca_load)
            load(ca_wq[:, :, :], "ca_wq", ca_load)
            load(ca_wg[:, :, :], "ca_wg", ca_load)
            sp.wait_ge(y_made[2], TT)
            load(ca_wo[:, :, :], "ca_wo", ca_load)
            load(ca_ctx[:, :, :], "ctx0", ca_ctx_in)
            sp.dma_start(ca_nw[:, :], dram["ca_nw"].partition_broadcast(P)).then_inc(ca_load, 16)
            sp.dma_start(me_bias[:, :], dram["me_bias"].partition_broadcast(P)).then_inc(ca_load, 16)
            sp.wait_ge(var_made[4], 2)
            sp.dma_start(ca_row8[:, :], dram["mask_row"].partition_broadcast(P)).then_inc(ca_mask_in, 16)
            for u in range(UNITS):
                g, j = u // 4, u % 4
                if u == 12:
                    sp.wait_ge(ca_vg, 8)
                    sp.wait_ge(ca_proj, 12)
                    load(ca_ctx[:, :, :], "ctx1", ca_ctx_in)
                sp.wait_ge(ca_low, 3 * (g + 1))
                if u >= 4:
                    sp.wait_ge(ca_st, CE * (u - 3))
                r = slice(j * HD, (j + 1) * HD)
                for i, (qpart, kpart) in enumerate(((0, 0), (1, 0), (0, 1))):
                    o = slice(i * HD, (i + 1) * HD)
                    sp.dma_start(ca_ks[o, j, :].bitcast(F32), ca_kp[r, g % 2, kpart, :].bitcast(F32)).then_inc(ca_stack[j], 16)
                    sp.dma_start(ca_qs[o, j, :].bitcast(F32), ca_qp[r, g % 2, qpart, :].bitcast(F32)).then_inc(ca_stack[j], 16)
            for q in ca_stack:
                sp.wait_ge(q, 96 * UNITS // 4)
            sp.wait_ge(ca_proj, 3 * UNITS // 4)
            sp.wait_ge(ca_vg, BATCH * (KB + TB))
            load(me_wd[:, :, :], "me_wd", me_load)
            load(me_wr[:, :, :], "me_wr", me_load)
            load(me_s1[:, :, :], "me_s1", me_load)
            load(me_sg[:, :, :], "me_sg", me_load)
            load(me_w2[:, :, :], "me_w2", me_load2)
            load(me_s2[:, :, :], "me_s2", me_load2)
            load(me_wu[:, :], "me_wu", me_load2)
            load(me_wg[:, :, :], "me_wg", me_load2)
            sp.wait_ge(y_made[5], TT)
            load(me_w1[:, :, :], "me_w1", me_load2)
            for t in range(TT):
                sp.wait_ge(x_normed[6], t + 1)
                sp.dma_start(out[t * P:(t + 1) * P, :], x_tok[:, t, :]).then_inc(out_done, 16)
            sp.wait_ge(out_done, 16 * TT)

        @block.tensor
        def _(pe):
            mm = nc.tensor.matmul

            def linear(o, lhs, rhs):
                for i, (a, b) in enumerate(zip(lhs, rhs)):
                    ins = mm(o, a, b, start=(i == 0), stop=(i == len(lhs) - 1))
                return ins

            def cols(w, a, b):
                return [w[:, k, a:b] for k in range(w.shape[1])]

            def y_bank(i, t):
                if t >= 2:
                    pe.wait_ge(y_added[i], t - 1)
                return bank(Y0 + t % 2)

            pe.wait_ge(sa_first_in, 32)
            g = 0
            for w in (sa_wq, sa_wk):
                for c in range(HALF):
                    for m in range(FT):
                        if g == FT:
                            pe.wait_ge(sa_qkv_in, 48)
                        if g >= 4:
                            pe.wait_ge(sa_lin_out, g - 3)
                        linear(bank(g % 4), cols(w, m * P, (m + 1) * P),
                               cols(x_feat, c * 512, (c + 1) * 512)).then_inc(sa_lin, 1)
                        g += 1
            for t in range(TT):
                pe.wait_ge(sa_lin_out, g - 3)
                linear(bank(g % 4), cols(x_feat, t * P, (t + 1) * P), cols(sa_wv, 0, D)).then_inc(sa_lin, 1)
                g += 1
            pe.wait_ge(sa_lin_out, SA_LIN)
            pe.wait_ge(consts_in, 13 * 16)

            def sa_scores(n):
                b, h, t, seen = sa_unit(n)
                if n % SA_HEAD == 0:
                    pe.wait_ge(sa_stack[h % 2], 96 * (h // 2 + 1))
                if n >= 3:
                    pe.wait_ge(sa_nm_made, n - 2)
                mm(bank(n % 3)[:, 0:seen], sa_ks[:, h % 2, b * SEQ + t * P:b * SEQ + (t + 1) * P],
                   sa_qs[:, h % 2, b * SEQ:b * SEQ + seen], start=True, stop=True).then_inc(sa_scored, 1)

            def sa_turn(n):
                b, h, t, seen = sa_unit(n)
                pe.wait_ge(sa_normed, n + 1)
                if n >= 3:
                    pe.wait_ge(sa_pt_made, n - 2)
                for j in range(t + 1):
                    ins = nc.tensor.transpose(bank(3 + n % 3)[:, j * P:(j + 1) * P],
                                              sa_p[:, n % 3, j * P:(j + 1) * P], ident[:, :])
                ins.then_inc(sa_turned, 1)

            def sa_values(n):
                b, h, t, seen = sa_unit(n)
                pe.wait_ge(sa_pt_made, n + 1)
                if h and h % 4 == 0 and t == 0:
                    pe.wait_ge(sa_of_made, BATCH * (h // 4 - 1) + b + 1)
                for j in range(t + 1):
                    ins = mm(bank(6 + b)[h % 4 * HD:h % 4 * HD + HD, t * P:(t + 1) * P],
                             sa_v[:, b * TB + j, h * HD:(h + 1) * HD], sa_pt[:, n % 3, j * P:(j + 1) * P],
                             start=(j == 0), stop=(j == t))
                ins.then_inc(sa_pv, 1)

            for n in range(SA_JOBS + 5):
                if n < SA_JOBS:
                    sa_scores(n)
                if 3 <= n < SA_JOBS + 3:
                    sa_turn(n - 3)
                if n >= 5:
                    sa_values(n - 5)
            pe.wait_ge(sa_wo_in, 16)
            pe.wait_ge(sa_of_made, BATCH * FT)
            for t in range(TT):
                linear(y_bank(0, t), cols(sa_of, t * P, (t + 1) * P), cols(sa_wo, 0, D)).then_inc(y_made[0], 1)
            pe_turn_x(pe, 0)

            pe.wait_ge(qa_load, 48)
            for t in range(TT):
                pe.wait_ge(xf_made[0], t + 1)
                if t >= 2:
                    pe.wait_ge(qa_q_out, t - 1)
                linear(bank(t % 2), cols(x_feat, t * P, (t + 1) * P), cols(qa_wq, 0, D)).then_inc(qa_q, 1)
            pe.wait_ge(qa_ctx_in, 16)
            pe.wait_ge(qa_q_out, TT)
            for g in range(16):
                m, c = g // 4, g % 4
                if g >= 2:
                    pe.wait_ge(qa_vl_out, g - 1)
                linear(bank(2 + g % 2), cols(qa_wkv, D + m * P, D + (m + 1) * P),
                       cols(qa_ctx, c * 512, (c + 1) * 512)).then_inc(qa_vl, 1)
            for t in range(KT):
                if t >= 2:
                    pe.wait_ge(qa_k_out, t - 1)
                linear(bank(t % 2), cols(qa_ctx, t * P, (t + 1) * P), cols(qa_wkv, 0, D)).then_inc(qa_k, 1)
            for t in range(KT):
                pe.wait_ge(qa_v_q, FT)
                if t >= 2:
                    pe.wait_ge(qa_v_made, t - 1)
                for m in range(FT):
                    ins = nc.tensor.transpose(bank(6 + t % 2).bitcast(BF16)[:, m * P:(m + 1) * P],
                                              qa_vint[:, m, t * P:(t + 1) * P], ident_bf[:, :])
                ins.then_inc(qa_vt, 1)
            pe.wait_ge(qa_ints, 1)
            pe.wait_ge(qa_v_made, KT)

            turn_bank = bank(6).bitcast(BF16)
            fills = [0]

            def fill(rows, blocks):
                if fills[0]:
                    pe.wait_ge(qa_stack, fills[0])
                for j, src in enumerate(blocks):
                    ins = nc.tensor.transpose(turn_bank[0:rows, j * P:(j + 1) * P], src, ident_bf[:, :])
                ins.then_inc(qa_turned, 1)
                fills[0] += 1

            def fill_stack(what, h):
                if what == "qa":
                    pe.wait_ge(qa_qrep_made, h + 1)
                    fill(3 * HD, [qa_qrep[:, t, :, :].rearrange("p a b -> p (a b)") for t in range(TT)])
                elif what == "qb":
                    pe.wait_ge(qa_qt_made, h + 1)
                    pe.wait_ge(qa_m_made, h + 1)
                    fill(KR, [qa_qt[:, t, :, :].rearrange("p a b -> p (a b)") for t in range(TT)])
                else:
                    src, rows, made = (qa_kt, 3 * HD, qa_kt_made) if what < "kb" else (qa_krep, KR, qa_krep_made)
                    half = int(what[2])
                    pe.wait_ge(made, h + 1)
                    fill(rows, [src[:, half * 8 + t, :, :].rearrange("p a b -> p (a b)") for t in range(8)])

            def qa_scores(h, i):
                n = h * SU + i
                t, c = i // 4, i % 4
                if i == 0:
                    pe.wait_ge(qa_stack, qa_no["ka1", h])
                if n >= 3:
                    pe.wait_ge(qa_max, n - 2)
                mm(bank((0, 1, 4)[n % 3]), qa_qa[:, t * P:(t + 1) * P], qa_ka[:, c * 512:(c + 1) * 512],
                   start=True, stop=True).then_inc(qa_s, 1)

            def qa_scores_t(h, i):
                n = h * EU + i
                c, k = i // KT, i % KT
                if i == 0:
                    pe.wait_ge(qa_stack, qa_no["qb", h])
                if n >= 2:
                    pe.wait_ge(qa_exp, n - 1)
                mm(bank(2 + n % 2), qa_kb2[:, h % 2, k * P:(k + 1) * P],
                   qa_qb2[:, h % 2, c * 512:(c + 1) * 512], start=True, stop=True).then_inc(qa_st, 1)

            def qa_values(h, i):
                n = h * EU + i
                c, k = i // KT, i % KT
                o, z = qa_quadrants(h)
                if k == 0 and n >= 2 * KT:
                    pe.wait_ge(qa_oz, h * HALF + c - 1)
                if k >= POOLED:
                    pe.wait_ge(qa_exp, n + 1)
                    mm(bank((5, 7)[c])[z, :], ones_f[:, :], qa_e(n), start=(k == POOLED), stop=False)
                if k == KT - 1:
                    pe.wait_ge(qa_added, (h * HALF + c + 1) * (POOLED - 1))
                    mm(bank((5, 7)[c])[z, :], ones_f[:, :], qa_sum[c][:, :], start=False, stop=True)
                pe.wait_ge(qa_rnd, n + 1)
                mm(bank((5, 7)[c])[o, :], qa_v[:, k, h * HD:(h + 1) * HD], qa_r[:, n % 4, :],
                   start=(k == 0), stop=(k == KT - 1)).then_inc(qa_pv, 1)

            for x in qa_order[:3]:
                fill_stack(*x)
            for i in range(SU):
                qa_scores(0, i)
            for x in qa_order[3:9]:
                fill_stack(*x)
            for n in range(HEADS * EU + LAG):
                h, i = divmod(n, EU)
                late = divmod(n - LAG, EU)
                if n >= LAG and i == 0:
                    qa_values(*late)
                if h < HEADS:
                    qa_scores_t(h, i)
                if n >= LAG and i > 0:
                    qa_values(*late)
                if h + 1 < HEADS:
                    for j in score_units(i):
                        qa_scores(h + 1, j)
                if i in QA_STEP and (QA_STEP[i][0], h + QA_STEP[i][1]) in qa_no:
                    fill_stack(QA_STEP[i][0], h + QA_STEP[i][1])
            pe.wait_ge(qa_grp, PIECES * HALF * HEADS // 4)
            for t in range(TT):
                linear(y_bank(1, t), cols(qa_of, t * P, (t + 1) * P), cols(qa_wp, 0, D)).then_inc(y_made[1], 1)
            pe_turn_x(pe, 1)

            pe.wait_ge(ff_load, 48)

            def ff_y(t):
                pe.wait_ge(ff_rvt_made, t + 1)
                linear(y_bank(2, t), [ff_rvt[:, t % 2, k, :] for k in range(TT)] + cols(x_feat, t * P, (t + 1) * P),
                       cols(ff_b, 0, D) + cols(ff_w, 0, D)).then_inc(y_made[2], 1)

            def ff_turn(t):
                pe.wait_ge(ff_rv_made, t + 1)
                if t >= 1:
                    pe.wait_ge(ff_rvt_made, t)
                for k in range(TT):
                    ins = nc.tensor.transpose(bank(2 + k // 4)[:, k % 4 * P:(k % 4 + 1) * P],
                                              ff_rv[:, t % 2, k * P:(k + 1) * P], ident[:, :])
                ins.then_inc(ff_turned, 1)

            for t in range(TT + 2):
                if t < TT:
                    pe.wait_ge(xf_made[1], t + 1)
                    if t >= 1:
                        pe.wait_ge(ff_vec_out, t)
                    linear(bank(0), cols(x_feat, t * P, (t + 1) * P), cols(ff_a, 0, 512))
                    linear(bank(1), cols(x_feat, t * P, (t + 1) * P), cols(ff_a, 512, 1024)).then_inc(ff_vecs, 1)
                if 1 <= t <= TT:
                    ff_turn(t - 1)
                if t >= 2:
                    ff_y(t - 2)
            pe_turn_x(pe, 2)

            pe.wait_ge(rc_load, 7 * 16)
            pe.wait_ge(xf_made[2], TT)
            for c in range(HALF):
                linear(bank(c), cols(rc_win, 0, P), cols(x_feat, c * 512, (c + 1) * 512)).then_inc(rc_zl, 1)
            for c in range(HALF):
                pe.wait_ge(rc_z_out, c + 1)
                mm(bank(2 + c), rc_wd[:, :], rc_z[:, c * 512:(c + 1) * 512], start=True, stop=True)
                if c == 0:
                    pe.wait_ge(rc_z_out, 2)
                mm(bank(c), rc_wg[:, :], rc_z[:, c * 512:(c + 1) * 512], start=True, stop=True).then_inc(rc_gl, 1)
            for t in range(TT):
                pe.wait_ge(rc_h_made, 2 * (t // TB + 1))
                mm(y_bank(3, t), rc_h[:, t * P:(t + 1) * P], rc_wout[:, :], start=True, stop=True
                   ).then_inc(y_made[3], 1)

            pe.wait_ge(ca_load, 7 * 16)
            pe.wait_ge(ca_ctx_in, 16)
            for i in range(KB):
                if i >= 2:
                    pe.wait_ge(ca_vg_out, i - 1)
                linear(bank(2 + i % 2), cols(ca_ctx, i * P, (i + 1) * P), cols(ca_wv, 0, D)).then_inc(ca_vg, 1)
            pe_turn_x(pe, 4, src=ca_xn)
            pe.wait_ge(ca_set, 4)

            def ca_project(j):
                g, part = j // 3, j % 3
                b, m = g // FT, g % FT
                if part == 0:
                    pe.wait_ge(ca_ctx_in, 16 * (b + 1))
                if j >= 1:
                    pe.wait_ge(ca_low, j)
                if part < 2:
                    ins = linear(bank(7), cols(ca_wk, m * P, (m + 1) * P), cols(ca_ctx, part * 512, (part + 1) * 512))
                else:
                    ins = linear(bank(7), cols(ca_wq, m * P, (m + 1) * P), cols(x_feat, b * SEQ, (b + 1) * SEQ))
                ins.then_inc(ca_proj, 1)

            def ca_scores(u, i):
                n = u * CU + i
                t, c, j = i // 2, i % 2, u % 4
                if i == 0:
                    pe.wait_ge(ca_stack[j], 96 * (u // 4 + 1))
                    pe.wait_ge(ca_masked, u + 1)
                if n >= 2:
                    pe.wait_ge(ca_max, n - 1)
                mm(bank(n % 2), ca_qs[0:KA, j, t * P:(t + 1) * P], ca_ks[0:KA, j, c * 512:(c + 1) * 512],
                   start=True, stop=True).then_inc(ca_s, 1)

            def ca_turn_m(u):
                pe.wait_ge(ca_m_made, u + 1)
                if u >= 1:
                    pe.wait_ge(ca_mrow_made, u)
                for t in range(TB):
                    ins = nc.tensor.transpose(bank(6)[0:3, t * P:(t + 1) * P], ca_mb[:, u % 2, t, :].bitcast(F32),
                                              ident[:, :])
                ins.then_inc(ca_mt, 1)

            def ca_scores_t(u, k):
                n, j = u * CE + k, u % 4
                if k == 0:
                    pe.wait_ge(ca_mrow_made, u + 1)
                if n >= 2:
                    pe.wait_ge(ca_exp, n - 1)
                mm(bank(2 + n % 2), ca_ks[0:KE, j, k * P:(k + 1) * P], ca_qs[0:KE, j, :], start=True, stop=True
                   ).then_inc(ca_st, 1)

            def ca_values(u, k):
                n, h = u * CE + k, u % HEADS
                if k == 0 and u >= 2:
                    pe.wait_ge(ca_oz, 2 * (u - 1))
                pe.wait_ge(ca_exp, n + 1)
                mm(bank(4 + u % 2)[0:2 * HD, :], ca_v[:, k, h // 2, h % 2 * HD:h % 2 * HD + 2 * HD],
                   ca_e[:, n % 4, :], start=(k == 0), stop=(k == KB - 1)).then_inc(ca_pv, 1)

            pe.wait_ge(xf_made[4], TT)
            for j in range(3):
                ca_project(j)
            for b in range(BATCH):
                if b:
                    pe.wait_ge(ca_exp, b * HEADS * CE)
                    pe.wait_ge(ca_pv, b * HEADS * CE)
                for i in range(KB if b == 0 else 0, KB + TB):
                    g = b * (KB + TB) + i
                    if i >= 2:
                        pe.wait_ge(ca_vg_out, g - 1)
                    if i < KB:
                        ins = linear(bank(2 + i % 2), cols(ca_ctx, i * P, (i + 1) * P), cols(ca_wv, 0, D))
                    else:
                        t = b * TB + i - KB
                        ins = linear(bank(2 + i % 2), cols(x_feat, t * P, (t + 1) * P), cols(ca_wg, 0, D))
                    ins.then_inc(ca_vg, 1)
                pe.wait_ge(ca_vg_out, (b + 1) * (KB + TB))
                if b == 0:
                    for u in range(2):
                        for i in range(CU):
                            ca_scores(u, i)
                        if u == 0:
                            ca_turn_m(0)
                for h in range(HEADS):
                    u = b * HEADS + h
                    for i in range(CE + 2):
                        if i < CE:
                            ca_scores_t(u, i)
                            if u + 2 < UNITS:
                                ca_scores(u + 2, i)
                            if (h % 4, i) in CA_PROJ and u // 4 + 1 < UNITS // 4:
                                ca_project(3 * (u // 4 + 1) + CA_PROJ[h % 4, i])
                        if i >= 2:
                            ca_values(u, i - 2)
                        if i == 3 and u + 1 < UNITS:
                            ca_turn_m(u + 1)
                for t in range(b * TB, (b + 1) * TB):
                    pe.wait_ge(ca_grp, 16 * (b + 1))
                    linear(y_bank(5, t), cols(ca_of, t % TB * P, (t % TB + 1) * P), cols(ca_wo, 0, D)
                           ).then_inc(y_made[5], 1)
            pe_turn_x(pe, 5)

            pe.wait_ge(me_load, 64)
            pe.wait_ge(xf_made[5], TT)
            for c in range(HALF):
                linear(bank(c), cols(me_wd, 0, LAT), cols(x_feat, c * 512, (c + 1) * 512)).then_inc(me_l, 1)
            for t in range(TT):
                ins = linear(bank(2)[:, t * EXPERTS:(t + 1) * EXPERTS], cols(x_feat, t * P, (t + 1) * P),
                             cols(me_wr, 0, EXPERTS))
            ins.then_inc(me_r, 1)
            pe.wait_ge(me_xlow, HALF)
            pe.wait_ge(me_pr_made, 1)

            def me_hidden(e, i):
                n = 4 * e + i
                m, c = i // 2, i % 2
                if n >= 2:
                    pe.wait_ge(me_u_made, n - 1)
                if n == 4:
                    pe.wait_ge(me_low, len(ME_HALVES))
                for which, (shared, high, low) in enumerate(((me_s1, me_w1h, me_w1l), (me_sg, me_wgh, me_wgl))):
                    if e == 0:
                        ins = linear(bank(which * 2 + n % 2), cols(shared, m * P, (m + 1) * P),
                                     cols(x_feat, c * 512, (c + 1) * 512))
                    else:
                        o, w = slice(c * 512, (c + 1) * 512), slice(m * P, (m + 1) * P)
                        high, low = high[:, e - 1, w], low[:, e - 1, w]
                        ins = linear(bank(which * 2 + n % 2), (high, low, high),
                                     (me_xh[:, o], me_xh[:, o], me_xl[:, o]))
                ins.then_inc(me_h, 1)

            def me_out(e, half):
                n = 2 * (e - 1) + half
                if half == 0:
                    pe.wait_ge(me_u_made, 4 * (e + 1))
                if n >= 2:
                    pe.wait_ge(me_y_out, (n - 1) * TB)
                for t in range(TB):
                    tt = half * TB + t
                    ins = linear(bank(4 + n % 2)[:, t * LAT:(t + 1) * LAT],
                                 [me_u[:, e % 2, m, tt * P:(tt + 1) * P] for m in range(2)],
                                 [me_w2[:, 2 * (e - 1) + m, :] for m in range(2)])
                ins.then_inc(me_y, 1)

            for e in range(EXPERTS + 1):
                if e == 1:
                    pe.wait_ge(me_load2, 5 * 16)
                for i in range(4):
                    me_hidden(e, i)
                    if i % 2 == 1 and e >= 2:
                        me_out(e - 1, i // 2)
            me_out(EXPERTS, 0)
            me_out(EXPERTS, 1)
            pe.wait_ge(me_y_out, EXPERTS * TT)
            for t in range(TT):
                ins = nc.tensor.transpose(bank(t // 4)[:, t % 4 * P:(t % 4 + 1) * P], me_acc[:, t, :], ident[:, :])
                if t % 4 == 3:
                    ins.then_inc(me_at, 1)
            for t in range(TT):
                pe.wait_ge(me_at_out, t // 4 + 1)
                linear(y_bank(6, t), [me_us[:, m, t * P:(t + 1) * P] for m in range(2)] + [me_acct[:, t, :]],
                       [me_s2[:, m, :] for m in range(2)] + [me_wu[:, :]]).then_inc(y_made[6], 1)

        @block.vector
        def _(dve):
            v = nc.vector
            steps = [0]

            def step(ins):
                steps[0] += 1
                ins.then_inc(dve_step, 1)
                dve.wait_ge(dve_step, steps[0])

            def norm_half(i, half, src, dst, rel=None):
                dve.wait_ge(std_made[i], half + 1)
                step(v.reciprocal(rstd[:, half * TB:(half + 1) * TB], std[:, half * TB:(half + 1) * TB]))
                for t in range(half * TB, (half + 1) * TB):
                    v.tensor_scalar(dst[:, t, :], src[:, t, :], meanvar[:, t, 0:1], rstd[:, t:t + 1],
                                    ALU.subtract, ALU.mult).then_inc(x_normed[i], 1)

            def tile_stats(i, t, src):
                step(v.bn_stats(stats[:, t, :], src[:, t, :]))
                ins = v.bn_aggr(meanvar[:, t, :], stats[:, t, :])
                if t % TB == TB - 1:
                    ins.then_inc(var_made[i], 1)

            def add_tile(i, t, bias=True):
                if bias:
                    dve.wait_ge(bias_in[i], t + 1)
                dve.wait_ge(y_made[i], t + 1)
                v.tensor_tensor(x_tok[:, t, :], bank(Y0 + t % 2), x_tok[:, t, :], ALU.add).then_inc(y_added[i], 1)
                dve.wait_ge(y_added[i], t + 1)
                tile_stats(i, t, x_tok)

            def add_and_norm(i, bias=True):
                for t in range(TT):
                    add_tile(i, t, bias)
                for half in range(2):
                    norm_half(i, half, x_tok, x_tok)

            v.memset(ln255[:, :], LN255).then_inc(consts_set, 1)
            v.memset(eps_ln[:, :], LN_EPS).then_inc(consts_set, 1)
            v.memset(eps_rms[:, :], RMS_EPS).then_inc(consts_set, 1)
            v.memset(ones_f[:, :], 1.0).then_inc(consts_set, 1)
            dve.wait_ge(consts_in, 13 * 16)
            v.tensor_copy(ident_bf[:, :], ident[:, :]).then_inc(consts_set, 1)

            def sa_split_low(g):
                dve.wait_ge(sa_lin_out, 16)
                for i, x in enumerate((sa_q, sa_k)):
                    dve.wait_ge(sa_high_made, 2 * g + i + 1)
                    v.tensor_tensor(x[:, g, :].bitcast(F32R), x[:, g, :], sa_high[g % 2][:, i, :].bitcast(F32),
                                    ALU.subtract).then_inc(sa_low_made, 1)

            for g in range(SA_LIN):
                dve.wait_ge(sa_lin, g + 1)
                if g < 8:
                    c, m = g // FT, g % FT
                    v.tensor_scalar(sa_q[:, m, c * 512:(c + 1) * 512], bank(g % 4),
                                    q_bias[:, m:m + 1], -SCALE, ALU.add, ALU.mult
                                    ).then_inc(sa_lin_out, 1)
                elif g < 16:
                    c, m = g // FT - HALF, g % FT
                    v.tensor_scalar(sa_k[:, m, c * 512:(c + 1) * 512], bank(g % 4),
                                    k_bias[:, m:m + 1], None, ALU.add).then_inc(sa_lin_out, 1)
                else:
                    v.tensor_tensor(sa_v[:, g - 16, :], bank(g % 4), sa_vb[:, :], ALU.add
                                    ).then_inc(sa_lin_out, 1)
                if g == 19:
                    sa_split_low(0)

            def sa_norm(n):
                b, h, t, seen = sa_unit(n)
                dve.wait_ge(sa_p_made, n + 1)
                step(v.reciprocal(sa_rs[:, n:n + 1], sa_sum[:, n:n + 1]))
                v.tensor_scalar(sa_p[:, n % 3, 0:seen], sa_p[:, n % 3, 0:seen], sa_rs[:, n:n + 1], None, ALU.mult
                                ).then_inc(sa_normed, 1)

            for n in range(SA_JOBS + 1):
                if n < SA_JOBS:
                    b, h, t, seen = sa_unit(n)
                    dve.wait_ge(sa_scored, n + 1)
                    if n >= 3:
                        dve.wait_ge(sa_p_made, n - 2)
                    v.tensor_tensor_reduce(sa_s[:, n % 3, 0:seen], bank(n % 3)[:, 0:seen],
                                           decay[:, SEQ - seen:SEQ], 1.0, 3.0e38, ALU.add, ALU.min,
                                           sa_nm[:, n:n + 1]).then_inc(sa_nm_made, 1)
                if n >= 1:
                    sa_norm(n - 1)
                if n % SA_GROUP == 2 and n // SA_GROUP + 1 < FT:
                    sa_split_low(n // SA_GROUP + 1)
            add_and_norm(0)

            def quantise(src, n_tile, scale, s_all, r_all, dst):
                x3 = src.rearrange("p (h d) -> p h d", h=HEADS)
                step(v.tensor_reduce(qa_sm[:, 0, :], x3, AX_X, ALU.max, apply_absolute_value=True))
                step(v.tensor_scalar(qa_sm[:, 1, :], qa_sm[:, 0, :], scale, 1.0 / 127.0, ALU.mult, ALU.mult))
                step(v.tensor_scalar(s_all, qa_sm[:, 1, :], 1e-8, None, ALU.max))
                step(v.reciprocal(r_all, s_all))
                t3 = qa_x2[:, n_tile % 2, :].rearrange("p (h d) -> p h d", h=HEADS)
                step(v.scalar_tensor_tensor(t3, x3, scale, r_all.unsqueeze(2).broadcast_to([P, HEADS, HD]),
                                            ALU.mult, ALU.mult))
                step(v.tensor_scalar(x3, t3, ROUND, -ROUND, ALU.add, ALU.add))
                step(v.tensor_scalar(dst, x3, 127.0, -127.0, ALU.min, ALU.max))

            for t in range(TT):
                dve.wait_ge(qa_q, t + 1)
                v.tensor_tensor(qa_x1[:, t % 2, :], bank(t % 2), qa_qb[:, :], ALU.add).then_inc(qa_q_out, 1)
                dve.wait_ge(qa_q_out, t + 1)
                quantise(qa_x1[:, t % 2, :], t, SCALE, qa_sq[:, t, :], qa_rk1[:, t, :],
                         qa_qint[:, t, :].rearrange("p (h d) -> p h d", h=HEADS))
            for m in range(FT):
                dve.wait_ge(qa_vl_out, 4 * (m + 1))
                vf = qa_vf[:, m % 2, :]
                step(v.tensor_reduce(qa_sm[:, 0, 0:1], vf, AX_X, ALU.max, apply_absolute_value=True))
                step(v.tensor_scalar(qa_sv[:, m:m + 1], qa_sm[:, 0, 0:1], 1.0 / 127.0, 1e-8, ALU.mult, ALU.max))
                step(v.reciprocal(qa_rv[:, m:m + 1], qa_sv[:, m:m + 1]))
                step(v.tensor_scalar(vf, vf, qa_rv[:, m:m + 1], 127.0, ALU.mult, ALU.min))
                step(v.tensor_scalar(vf, vf, -127.0, ROUND, ALU.max, ALU.add))
                v.tensor_scalar(qa_vint[:, m, :], vf, -ROUND, None, ALU.add).then_inc(qa_v_q, 1)
            for t in range(KT):
                dve.wait_ge(qa_k, t + 1)
                v.tensor_tensor(qa_x1[:, t % 2, :], bank(t % 2), qa_kb[:, :], ALU.add).then_inc(qa_k_out, 1)
                dve.wait_ge(qa_k_out, t + 1)
                quantise(qa_x1[:, t % 2, :], t, 1.0, qa_sk[:, t, :], qa_rk[:, t, :], qa_kint[:, t, :, 0:HD])
            step(v.tensor_copy(qa_kint[:, :, :, HD], qa_rk[:, :, :]))
            step(v.tensor_tensor(qa_rk1[:, :, :], qa_rk[:, :, :], qa_kint[:, :, :, HD], ALU.subtract))
            step(v.tensor_copy(qa_kint[:, :, :, HD + 1], qa_rk1[:, :, :]))
            v.tensor_tensor(qa_kint[:, :, :, HD + 2], qa_rk1[:, :, :], qa_kint[:, :, :, HD + 1],
                            ALU.subtract).then_inc(qa_ints, 1)

            def qa_maximum(h, i):
                n = h * SU + i
                dve.wait_ge(qa_s, n + 1)
                v.tensor_reduce(qa_mx8[:, i // 4, i % 4:i % 4 + 1], bank((0, 1, 4)[n % 3]), AX_X, ALU.max).then_inc(qa_max, 1)

            def qa_splits(h):
                dve.wait_ge(qa_max, SU * (h + 1))
                if h >= 1:
                    dve.wait_ge(qa_turned, qa_no["qb", h - 1])
                step(v.tensor_reduce(qa_m[:, 0, :], qa_mx8[:, :, :], AX_X, ALU.max))
                step(v.scalar_tensor_tensor(qa_m[:, 1, :], qa_m[:, 0, :], -1.0, qa_sq[:, :, h], ALU.mult, ALU.mult))
                m1 = qa_m[:, 1, :].unsqueeze(2)
                step(v.tensor_copy(qa_qt[:, :, 0, HD:REP], m1.broadcast_to([P, TT, 3])))
                step(v.tensor_tensor(qa_m[:, 2, :], qa_m[:, 1, :], qa_qt[:, :, 0, HD], ALU.subtract))
                step(v.tensor_copy(qa_qt[:, :, 1, HD:REP - 1], qa_m[:, 2, :].unsqueeze(2).broadcast_to([P, TT, 2])))
                v.tensor_tensor(qa_qt[:, :, 2, HD], qa_m[:, 2, :], qa_qt[:, :, 1, HD], ALU.subtract
                                ).then_inc(qa_m_made, 1)

            def qa_round(h, i):
                n = h * EU + i
                dve.wait_ge(qa_exp, n + 1)
                if n >= 4:
                    dve.wait_ge(qa_pv, n - 3)
                v.tensor_scalar(qa_r[:, n % 4, :], qa_e(n), ROUND, -ROUND, ALU.add, ALU.add
                                ).then_inc(qa_rnd, 1)

            def qa_group(h, piece):
                c, j = piece // PIECES, piece % PIECES
                n = 512 // PIECES
                dve.wait_ge(qa_oz, HALF * h + c + 1)
                if piece or h >= 4:
                    dve.wait_ge(qa_grp, h // 4 * HALF * PIECES + piece)
                step(v.reciprocal(qa_rz[:, 0:n], qa_zs[:, c, j * n:(j + 1) * n]))
                v.scalar_tensor_tensor(qa_of[:, h // 4, c * 512 + j * n:c * 512 + (j + 1) * n],
                                       qa_os[:, c, j * n:(j + 1) * n], qa_sv[:, h // 4:h // 4 + 1],
                                       qa_rz[:, 0:n], ALU.mult, ALU.mult).then_inc(qa_grp, 1)

            def qa_repeat_k(h):
                if h >= 1:
                    dve.wait_ge(qa_turned, qa_no["kb1", h - 1])
                v.tensor_copy(qa_krep[:, :, :, :], qa_kint[:, :, h, :].unsqueeze(2).broadcast_to([P, KT, 3, REP])
                              ).then_inc(qa_krep_made, 1)

            def qa_repeat_q(h):
                if h >= 1:
                    dve.wait_ge(qa_turned, qa_no["qa", h - 1])
                v.tensor_copy(qa_qrep[:, :, :, :], qa_qint[:, :, h * HD:(h + 1) * HD].unsqueeze(2)
                              .broadcast_to([P, TT, 3, HD])).then_inc(qa_qrep_made, 1)

            dve.wait_ge(qa_ctx_in, 16)
            dve.wait_ge(qa_k, KT)
            dve.wait_ge(qa_ints, 1)
            qa_repeat_k(0)
            qa_repeat_q(0)
            qa_repeat_q(1)
            v.memset(qa_qt[:, :, :, :], 0.0).then_inc(qa_qt_zero, 1)
            dve.wait_ge(qa_vt, KT)
            for i in range(SU):
                qa_maximum(0, i)
            qa_splits(0)
            for h in range(HEADS):
                for i in range(EU):
                    if h + 1 < HEADS:
                        for j in score_units(i):
                            qa_maximum(h + 1, j)
                    qa_round(h, i)
                    if i == SPREAD and h + 1 < HEADS:
                        qa_splits(h + 1)
                    if i % 3 == 2 and i // 3 < HALF * PIECES and h % 4 == 0 and h > 0:
                        qa_group(h - 1, i // 3)
                    if i == 12 and h + 1 < HEADS:
                        qa_repeat_k(h + 1)
                    if i == 20 and h + 2 < HEADS:
                        qa_repeat_q(h + 2)
            for piece in range(HALF * PIECES):
                qa_group(HEADS - 1, piece)
            dve.wait_ge(y_made[0], TT)
            dve.wait_ge(qa_pv, HEADS * EU)
            step(v.memset(rc_wd[:, :], 0.0))
            v.memset(rc_wg[:, :], 0.0).then_inc(rc_set, 1)
            add_and_norm(1)

            step(v.memset(ff_norm[:, ARROWS:], -1.0))
            for t in range(TT):
                dve.wait_ge(ff_vec_out, t + 1)
                vec = ff_vec[:, t % 2, :, :]
                step(v.tensor_tensor(ff_sq[:, :, :], vec, vec, ALU.mult))
                step(v.tensor_reduce(ff_norm[:, 0:ARROWS], ff_sq[:, :, :], AX_X, ALU.add))
                step(v.max(ff_top[:, :], ff_norm[:, :]))
                step(v.memset(ff_top[:, 4:8], -1.0))
                step(v.match_replace(ff_rep[:, :], ff_top[:, :], ff_norm[:, :], -2.0))
                step(v.tensor_scalar(ff_route[:, :], ff_rep[:, 0:ARROWS], -2.0, 0.25, ALU.is_equal, ALU.mult))
                route = ff_route[:, :].unsqueeze(2).broadcast_to([P, ARROWS, RANK])
                step(v.tensor_tensor(ff_sq[:, :, :], vec, route, ALU.mult))
                step(v.tensor_reduce(ff_v[:, :], ff_sq[:, :, :].rearrange("p a r -> p r a"), AX_X, ALU.add))
                if t >= 2:
                    dve.wait_ge(ff_turned, t - 1)
                v.tensor_tensor(ff_rv[:, t % 2, :].rearrange("p (a r) -> p a r", a=ARROWS), route,
                                ff_v[:, :].unsqueeze(1).broadcast_to([P, ARROWS, RANK]), ALU.mult
                                ).then_inc(ff_rv_made, 1)
                if t >= 2:
                    add_tile(2, t - 2)
            add_tile(2, TT - 2)
            add_tile(2, TT - 1)
            for half in range(2):
                norm_half(2, half, x_tok, x_tok)

            for c in range(HALF):
                dve.wait_ge(rc_gl, c + 1)
                step(v.tensor_tensor(rc_g[:, c * 512:(c + 1) * 512], bank(c), rc_z[:, c * 512:(c + 1) * 512],
                                     ALU.mult))
                dve.wait_ge(rc_d_out, c + 1)
                lo, hi = c * SEQ, (c + 1) * SEQ
                v.tensor_tensor_scan(rc_h[0:DI, lo:hi], rc_d[0:DI, lo:hi], rc_g[0:DI, lo:hi], 0.0,
                                     ALU.mult, ALU.add).then_inc(rc_h_made, 1)
                back = slice(hi - 1, lo - 1 if lo else None, -1)
                v.tensor_tensor_scan(rc_h[DI:P, back], rc_d[DI:P, back], rc_g[DI:P, back], 0.0,
                                     ALU.mult, ALU.add).then_inc(rc_h_made, 1)
            for t in range(TT):
                dve.wait_ge(y_made[3], t + 1)
                v.tensor_tensor(rc_y[:, t, :], bank(Y0 + t % 2), x_tok[:, t, :], ALU.add).then_inc(y_added[3], 1)
                dve.wait_ge(y_added[3], t + 1)
                tile_stats(3, t, rc_y)
            for half in range(2):
                tiles = range(half * TB, (half + 1) * TB)
                dve.wait_ge(std_made[3], half + 1)
                step(v.reciprocal(rstd[:, half * TB:(half + 1) * TB], std[:, half * TB:(half + 1) * TB]))
                for t in tiles:
                    v.scalar_tensor_tensor(rc_n[:, t, :], rc_y[:, t, :], meanvar[:, t, 0:1], rc_gamma[:, :],
                                           ALU.subtract, ALU.mult).then_inc(x_normed[3], 1)
                for t in tiles:
                    dve.wait_ge(x_normed[3], t + 1)
                    dve.wait_ge(rc_beta_in, t + 1)
                    v.scalar_tensor_tensor(x_tok[:, t, :], rc_n[:, t, :], rstd[:, t:t + 1], x_tok[:, t, :],
                                           ALU.mult, ALU.add).then_inc(rc_done, 1)
            dve.wait_ge(rc_done, TT)
            for t in range(TT):
                tile_stats(4, t, x_tok)
            for half in range(2):
                dve.wait_ge(std_made[4], half + 1)
                step(v.reciprocal(rstd[:, half * TB:(half + 1) * TB], std[:, half * TB:(half + 1) * TB]))
                for t in range(half * TB, (half + 1) * TB):
                    v.tensor_scalar(x_tok[:, t, :], x_tok[:, t, :], meanvar[:, t, 0:1], rstd[:, t:t + 1],
                                    ALU.subtract, ALU.mult).then_inc(ca_ss_made, 1)
            dve.wait_ge(ca_rr_made, 1)
            step(v.reciprocal(ca_rr[:, :], ca_ss[:, :]))
            dve.wait_ge(ca_load, 7 * 16)
            for t in range(TT):
                v.scalar_tensor_tensor(ca_xn[:, t, :], x_tok[:, t, :], ca_rr[:, t:t + 1], ca_nw[:, :],
                                       ALU.mult, ALU.mult).then_inc(x_normed[4], 1)

            dve.wait_ge(x_turned[4], TT)
            v.memset(ca_v[:, :, :, HD:2 * HD], 1.0).then_inc(ca_set, 1)
            v.memset(ca_mb[:, :, :, :].bitcast(F32), 1.0).then_inc(ca_set, 1)
            v.memset(ca_ks[MROW:MROW + 3, :, :].bitcast(F32), 1.0).then_inc(ca_set, 1)
            v.memset(ca_qs[MROW:MROW + 3, :, :].bitcast(F32), 1.0).then_inc(ca_set, 1)
            dve.wait_ge(ca_set, 4)
            dve.wait_ge(ca_mask_in, 16)

            def ca_mask_row(u):
                b, j = u // HEADS, u % 4
                if u % HEADS < 4:
                    if b:
                        dve.wait_ge(ca_st, CE * (u - 3))
                    v.tensor_scalar(ca_ks[MROW:KA, j, :], ca_row8[MROW:KA, b * CTX:(b + 1) * CTX], -1.0, -MASKED,
                                    ALU.add, ALU.mult).then_inc(ca_masked, 1)
                elif u % HEADS == 4:
                    v.engine_nop().then_inc(ca_masked, HEADS - 4)

            def ca_maximum(u, i):
                n = u * CU + i
                dve.wait_ge(ca_s, n + 1)
                v.tensor_reduce(ca_mx[:, i // 2, i % 2:i % 2 + 1], bank(n % 2), AX_X, ALU.max).then_inc(ca_max, 1)

            def ca_splits(u):
                dve.wait_ge(ca_max, CU * (u + 1))
                if u >= 2:
                    dve.wait_ge(ca_mt, u - 1)
                step(v.tensor_reduce(ca_m[:, 0, :], ca_mx[:, :, :], AX_X, ALU.max))
                step(v.tensor_scalar(ca_m[:, 1, :], ca_m[:, 0, :], -1.0e20, -1.0, ALU.max, ALU.mult))
                mb = ca_mb[:, u % 2, :, :]
                step(v.tensor_copy(mb[:, :, 1], ca_m[:, 1, :]))
                v.tensor_tensor(mb[:, :, 2], ca_m[:, 1, :], mb[:, :, 1].bitcast(F32), ALU.subtract
                                ).then_inc(ca_m_made, 1)

            def ca_split_low(j):
                g, part = j // 3, j % 3
                dve.wait_ge(ca_high, j + 1)
                if part < 2:
                    o = slice(part * 512, (part + 1) * 512)
                    v.tensor_tensor(ca_kp[:, g % 2, 1, o], bank(7), ca_kp[:, g % 2, 0, o].bitcast(F32), ALU.subtract
                                    ).then_inc(ca_low, 1)
                else:
                    v.scalar_tensor_tensor(ca_qp[:, g % 2, 1, :], bank(7), SCALE, ca_qp[:, g % 2, 0, :].bitcast(F32),
                                           ALU.mult, ALU.subtract).then_inc(ca_low, 1)

            def ca_group(g, piece):
                o = slice(piece * P, (piece + 1) * P)
                dve.wait_ge(ca_oz, 8 * (g + 1))
                if g or piece:
                    dve.wait_ge(ca_grp, 4 * g + piece)
                if g == 4:
                    dve.wait_ge(y_made[5], TB)
                step(v.tensor_scalar(ca_rz[:, 0:P], ca_zs[:, o], 1.0e-30, None, ALU.max))
                step(v.reciprocal(ca_rz[:, P:2 * P], ca_rz[:, 0:P]))
                v.tensor_tensor(ca_of[:, g % FT, o], ca_os[:, o], ca_rz[:, P:2 * P], ALU.mult).then_inc(ca_grp, 1)

            for j in range(3):
                ca_split_low(j)
            for b in range(BATCH):
                for t in range(KB if b else 0):
                    g = b * (KB + TB) + t
                    dve.wait_ge(ca_vg, g + 1)
                    v.tensor_copy(ca_v[:, t, :, :].rearrange("p j (a d) -> p j a d", a=3)[:, :, 0:3:2, :],
                                  bank(2 + t % 2).rearrange("p (j a d) -> p j a d", j=HEADS // 2, a=2)
                                  ).then_inc(ca_vg_out, 1)
                if b == 0:
                    for u in range(2):
                        ca_mask_row(u)
                        for i in range(CU):
                            ca_maximum(u, i)
                        ca_splits(u)
                for h in range(HEADS):
                    u = b * HEADS + h
                    if u + 2 < UNITS:
                        ca_mask_row(u + 2)
                    for i in range(CU):
                        if u + 2 < UNITS:
                            ca_maximum(u + 2, i)
                        if (h % 4, i) in CA_PROJ and u // 4 + 1 < UNITS // 4:
                            ca_split_low(3 * (u // 4 + 1) + CA_PROJ[h % 4, i])
                        if h % 4 == 0 and h > 0 and i % 2 == 1:
                            ca_group(u // 4 - 1, i // 2)
                    if u + 2 < UNITS:
                        ca_splits(u + 2)
                for piece in range(4):
                    ca_group(4 * b + 3, piece)
                for t in range(b * TB, (b + 1) * TB):
                    dve.wait_ge(y_made[5], t + 1)
                    if t >= 2:
                        dve.wait_ge(y_added[5], t - 1)
                    v.tensor_tensor(ca_tmp[:, t % 2, :], bank(Y0 + t % 2), ca_gate[:, t % TB, :], ALU.mult
                                    ).then_inc(y_added[5], 1)
                    dve.wait_ge(y_added[5], t + 1)
                    step(v.tensor_tensor(x_tok[:, t, :], ca_tmp[:, t % 2, :], x_tok[:, t, :], ALU.add))
                    tile_stats(5, t, x_tok)
            for half in range(2):
                norm_half(5, half, x_tok, x_tok)

            for c in range(HALF):
                o = slice(c * 512, (c + 1) * 512)
                dve.wait_ge(me_high, c + 1)
                v.tensor_tensor(me_xl[:, o], bank(c), me_xh[:, o].bitcast(F32), ALU.subtract
                                ).then_inc(me_xlow, 1)
            dve.wait_ge(me_pr_made, 1)
            step(v.tensor_tensor(me_pb[:, :, :], me_pr[:, :, :],
                                 me_bias[:, :].unsqueeze(1).broadcast_to([P, TT, EXPERTS]), ALU.add))
            for t in range(TT):
                step(v.max(me_top[:, t, :], me_pb[:, t, :]))
                step(v.match_replace(me_rep[:, t, :], me_top[:, t, :], me_pb[:, t, :], MASKED))
            step(v.tensor_scalar(me_rep[:, :, :], me_rep[:, :, :], MASKED, None, ALU.is_equal))
            step(v.tensor_tensor(me_w[:, :, :], me_rep[:, :, :], me_pr[:, :, :], ALU.mult))
            step(v.tensor_reduce(me_sum[:, :], me_w[:, :, :], AX_X, ALU.add))
            step(v.reciprocal(me_rsum[:, :], me_sum[:, :]))
            step(v.scalar_tensor_tensor(me_w[:, :, :], me_w[:, :, :], 2.5,
                                        me_rsum[:, :].unsqueeze(2).broadcast_to([P, TT, EXPERTS]),
                                        ALU.mult, ALU.mult))

            def me_add(e, half):
                n = 2 * (e - 1) + half
                dve.wait_ge(me_y, n + 1)
                for t in range(TB):
                    tt = half * TB + t
                    y = bank(4 + n % 2)[:, t * LAT:(t + 1) * LAT]
                    w = me_w[:, tt, e - 1:e]
                    if e == 1:
                        v.tensor_scalar(me_acc[:, tt, :], y, w, None, ALU.mult).then_inc(me_y_out, 1)
                    else:
                        v.scalar_tensor_tensor(me_acc[:, tt, :], y, w, me_acc[:, tt, :], ALU.mult, ALU.add
                                               ).then_inc(me_y_out, 1)

            for e in range(EXPERTS + 1):
                for i in range(4):
                    n = 4 * e + i
                    m, c = i // 2, i % 2
                    dve.wait_ge(me_sqr, n + 1)
                    if e >= 3 and i == 0:
                        dve.wait_ge(me_y, 2 * (e - 2))
                    dst = me_us[:, m, c * 512:(c + 1) * 512] if e == 0 else me_u[:, e % 2, m, c * 512:(c + 1) * 512]
                    v.tensor_tensor(dst, bank(n % 2), me_rq[:, n % 4, :], ALU.mult).then_inc(me_u_made, 1)
                    if i % 2 == 1 and e >= 2:
                        me_add(e - 1, i // 2)
            me_add(EXPERTS, 0)
            me_add(EXPERTS, 1)
            add_and_norm(6, bias=False)

        @block.scalar
        def _(act):
            s = nc.scalar
            act.wait_ge(consts_set, 5)

            def sa_split_high(g):
                act.wait_ge(sa_lin_out, 16)
                if g >= 2:
                    for q in sa_stack:
                        act.wait_ge(q, 2 * 96 * (g - 1))
                for i, x in enumerate((sa_q, sa_k)):
                    s.copy(sa_high[g % 2][:, i, :], x[:, g, :]).then_inc(sa_high_made, 1)

            sa_split_high(0)
            for n in range(SA_JOBS + 5):
                if n < SA_JOBS:
                    b, h, t, seen = sa_unit(n)
                    act.wait_ge(sa_nm_made, n + 1)
                    if n >= 3:
                        act.wait_ge(sa_turned, n - 2)
                    s.activation(sa_p[:, n % 3, 0:seen], sa_s[:, n % 3, 0:seen], ACT.Exp, bias=sa_nm[:, n:n + 1],
                                 scale=-1.0, accum_out=sa_sum[:, n:n + 1]).then_inc(sa_p_made, 1)
                if n >= 3 and n - 3 < SA_JOBS:
                    m = n - 3
                    b, h, t, seen = sa_unit(m)
                    act.wait_ge(sa_turned, m + 1)
                    if m >= 3:
                        act.wait_ge(sa_pv, m - 2)
                    s.copy(sa_pt[:, m % 3, 0:seen], bank(3 + m % 3)[:, 0:seen]).then_inc(sa_pt_made, 1)
                if n % SA_GROUP == 1 and n // SA_GROUP + 1 < FT:
                    sa_split_high(n // SA_GROUP + 1)
                if n >= 5 and sa_unit(n - 5)[1] % 4 == 3 and sa_unit(n - 5)[2] == TB - 1:
                    b, h, t, seen = sa_unit(n - 5)
                    act.wait_ge(sa_pv, n - 4)
                    s.copy(sa_of[:, h // 4, b * SEQ:(b + 1) * SEQ], bank(6 + b)).then_inc(sa_of_made, 1)
            act_std(act, 0)
            act_copy_x(act, 0)

            for g in range(16):
                m, c = g // 4, g % 4
                act.wait_ge(qa_vl, g + 1)
                if g >= 8 and c == 0:
                    act.wait_ge(qa_v_q, m - 1)
                s.activation(qa_vf[:, m % 2, c * 512:(c + 1) * 512], bank(2 + g % 2), ACT.Identity,
                             bias=v_bias2[:, m:m + 1]).then_inc(qa_vl_out, 1)
            for t in range(KT):
                act.wait_ge(qa_vt, t + 1)
                s.copy(qa_v[:, t, :], bank(6 + t % 2).bitcast(BF16)[:, 0:D]).then_inc(qa_v_made, 1)

            turn_bank = bank(6).bitcast(BF16)
            stacks = [0]

            def stack(rows, dst):
                stacks[0] += 1
                act.wait_ge(qa_turned, stacks[0])
                s.copy(dst, turn_bank[0:rows, :]).then_inc(qa_stack, 1)

            def copy_stack(what, h):
                if what == "qa":
                    stack(3 * HD, qa_qa[:, :])
                elif what == "qb":
                    stack(KR, qa_qb2[:, h % 2, :])
                elif what < "kb":
                    stack(3 * HD, qa_ka[:, int(what[2]) * 1024:(int(what[2]) + 1) * 1024])
                else:
                    stack(KR, qa_kb2[:, h % 2, int(what[2]) * 1024:(int(what[2]) + 1) * 1024])

            def exponent(h, i):
                n = h * EU + i
                k = i % KT
                act.wait_ge(qa_st, n + 1)
                if n >= ERING:
                    act.wait_ge(qa_pv, n - ERING + 1)
                    if (n - ERING) % KT < POOLED:
                        act.wait_ge(qa_added, (n - ERING) // KT * (POOLED - 1) + max((n - ERING) % KT, 1))
                s.activation(qa_e(n), bank(2 + n % 2), ACT.Exp, bias=ln255[:, :],
                             scale=qa_sk[:, k, h:h + 1]).then_inc(qa_exp, 1)

            def out_chunk(h, c):
                o, z = qa_quadrants(h)
                act.wait_ge(qa_pv, (h * HALF + c + 1) * KT)
                if h % 4 == 0 and h > 0:
                    act.wait_ge(qa_grp, PIECES * (HALF * (h // 4 - 1) + c + 1))
                s.copy(qa_os[o, c, :], bank((5, 7)[c])[o, :]).then_inc(act_step, 1)
                s.copy(qa_zs[o, c, :], bank((5, 7)[c])[z, :]).then_inc(qa_oz, 1)

            act.wait_ge(qa_ints, 1)
            for x in qa_order[:9]:
                copy_stack(*x)
            for h in range(HEADS):
                for i in range(EU):
                    exponent(h, i)
                    if i == LAG + 1 and h > 0:
                        out_chunk(h - 1, 1)
                    if i == KT + LAG + 1:
                        out_chunk(h, 0)
                    if i in QA_STEP and (QA_STEP[i][0], h + QA_STEP[i][1]) in qa_no:
                        copy_stack(QA_STEP[i][0], h + QA_STEP[i][1])
            out_chunk(HEADS - 1, 1)
            act_std(act, 1)
            act_copy_x(act, 1)

            def ff_copy_rv(t):
                act.wait_ge(ff_turned, t + 1)
                if t >= 2:
                    act.wait_ge(y_made[2], t - 1)
                s.copy(ff_rvt[:, t % 2, 0:4, :].rearrange("p a b -> p (a b)"), bank(2)).then_inc(act_step, 1)
                s.copy(ff_rvt[:, t % 2, 4:8, :].rearrange("p a b -> p (a b)"), bank(3)).then_inc(ff_rvt_made, 1)

            for t in range(TT + 1):
                if t < TT:
                    act.wait_ge(ff_vecs, t + 1)
                    if t >= 2:
                        act.wait_ge(ff_rv_made, t - 1)
                    s.copy(ff_vec[:, t % 2, 0:32, :].rearrange("p a b -> p (a b)"), bank(0)).then_inc(act_step, 1)
                    s.copy(ff_vec[:, t % 2, 32:64, :].rearrange("p a b -> p (a b)"), bank(1)).then_inc(ff_vec_out, 1)
                if t >= 1:
                    ff_copy_rv(t - 1)
            act_std(act, 2)
            act_copy_x(act, 2)

            for c in range(HALF):
                act.wait_ge(rc_zl, c + 1)
                s.copy(rc_z[:, c * 512:(c + 1) * 512], bank(c)).then_inc(rc_z_out, 1)
            for c in range(HALF):
                act.wait_ge(rc_gl, c + 1)
                s.activation(rc_d[:, c * 512:(c + 1) * 512], bank(2 + c), ACT.Sigmoid).then_inc(rc_d_out, 1)
            act_std(act, 3)

            def ca_copy_values(t):
                act.wait_ge(ca_vg, t + 1)
                s.copy(ca_v[:, t, :, :].rearrange("p j (a d) -> p j a d", a=3)[:, :, 0:3:2, :],
                       bank(2 + t % 2).rearrange("p (j a d) -> p j a d", j=HEADS // 2, a=2)
                       ).then_inc(ca_vg_out, 1)

            for t in range(TB):
                ca_copy_values(t)
            act_std(act, 4)
            for t in range(TT):
                act.wait_ge(ca_ss_made, t + 1)
                s.activation(rc_y[:, t, :], x_tok[:, t, :], ACT.Square, scale=float(D) ** -0.5,
                             accum_out=ca_rr[:, t:t + 1]).then_inc(ca_xn_made, 1)
                if t % 2 == 0:
                    ca_copy_values(TB + t // 2)
            act.wait_ge(ca_xn_made, TT)
            s.activation(ca_ss[:, :], ca_rr[:, :], ACT.Sqrt, bias=eps_rms[:, :]).then_inc(ca_rr_made, 1)
            act_copy_x(act, 4)

            act.wait_ge(ca_set, 4)

            def ca_split_high(j):
                g, part = j // 3, j % 3
                act.wait_ge(ca_proj, j + 1)
                if g >= 2 and part == 0:
                    for q in ca_stack:
                        act.wait_ge(q, 96 * (g - 1))
                if part < 2:
                    s.copy(ca_kp[:, g % 2, 0, part * 512:(part + 1) * 512], bank(7)).then_inc(ca_high, 1)
                else:
                    s.mul(ca_qp[:, g % 2, 0, :], bank(7), SCALE).then_inc(ca_high, 1)

            def copy_mrow(u):
                act.wait_ge(ca_mt, u + 1)
                s.copy(ca_qs[MROW:KE, u % 4, :], bank(6)[0:3, :]).then_inc(ca_mrow_made, 1)

            def ca_out(u):
                h = u % HEADS
                r = slice(h % 4 * HD, h % 4 * HD + HD)
                act.wait_ge(ca_pv, CE * (u + 1))
                if u >= 4 and h % 4 == 0:
                    act.wait_ge(ca_grp, u)
                o = bank(4 + u % 2)
                a = h % 2 * HD
                s.copy(ca_os[r, :], o[a:a + HD, :]).then_inc(ca_oz, 1)
                s.copy(ca_zs[r, :], o[HD - a:2 * HD - a, :]).then_inc(ca_oz, 1)

            for j in range(3):
                ca_split_high(j)
            for b in range(BATCH):
                for t in range(TB):
                    g = b * (KB + TB) + KB + t
                    act.wait_ge(ca_vg, g + 1)
                    act.wait_ge(ca_vg_out, g)
                    if b and t == 0:
                        act.wait_ge(y_added[5], TB)
                    s.activation(ca_gate[:, t, :], bank(2 + t % 2), ACT.Sigmoid).then_inc(ca_vg_out, 1)
                if b == 0:
                    copy_mrow(0)
                for h in range(HEADS):
                    u = b * HEADS + h
                    for k in range(CE):
                        n = u * CE + k
                        act.wait_ge(ca_st, n + 1)
                        if n >= 4:
                            act.wait_ge(ca_pv, n - 3)
                        s.activation(ca_e[:, n % 4, :], bank(2 + n % 2), ACT.Exp).then_inc(ca_exp, 1)
                        if k == 1 and h > 0:
                            ca_out(u - 1)
                        if (h % 4, k) in CA_PROJ and u // 4 + 1 < UNITS // 4:
                            ca_split_high(3 * (u // 4 + 1) + CA_PROJ[h % 4, k])
                        if k == 4 and u + 1 < UNITS:
                            copy_mrow(u + 1)
                ca_out(u)
            act_std(act, 5)
            act_copy_x(act, 5)

            for c in range(HALF):
                act.wait_ge(me_l, c + 1)
                s.copy(me_xh[:, c * 512:(c + 1) * 512], bank(c)).then_inc(me_high, 1)
            act.wait_ge(me_r, 1)
            s.activation(me_pr[:, :, :].rearrange("p a b -> p (a b)"), bank(2)[:, 0:TT * EXPERTS], ACT.Sigmoid
                         ).then_inc(me_pr_made, 1)
            act.wait_ge(me_load2, 5 * 16)
            for n in range(ME_UNITS):
                if n < len(ME_HALVES):
                    w, e = ME_HALVES[n]
                    s.copy((me_wgh, me_w1h)[w][:, e, :], (me_wg, me_w1)[w][:, e, :]).then_inc(me_high, 1)
                act.wait_ge(me_h, n + 1)
                if n >= 4:
                    act.wait_ge(me_u_made, n - 3)
                s.activation(me_rl[:, n % 4, :], bank(2 + n % 2), ACT.Relu).then_inc(me_relu, 1)
                act.wait_ge(me_relu, n + 1)
                s.activation(me_rq[:, n % 4, :], me_rl[:, n % 4, :], ACT.Square).then_inc(me_sqr, 1)
            for c in range(2):
                act.wait_ge(me_at, c + 1)
                s.copy(me_acct[:, c * 4:(c + 1) * 4, :].rearrange("p a b -> p (a b)"), bank(c)).then_inc(me_at_out, 1)
            act_std(act, 6)

        @block.gpsimd
        def _(pool):
            g = nc.gpsimd
            steps = [0]

            def step(ins):
                steps[0] += 1
                ins.then_inc(pool_step, 1)
                pool.wait_ge(pool_step, steps[0])

            def add_bias(i, bias, ready, counts):
                for t in range(TT):
                    pool.wait_ge(ready, counts(t))
                    g.tensor_tensor(x_tok[:, t, :], x_tok[:, t, :], bias[:, :], ALU.add).then_inc(bias_in[i], 1)

            pool.wait_ge(consts_in, 13 * 16)
            add_bias(0, sa_ob, x_in, lambda t: 16)
            add_bias(1, qa_pb, x_turned[0], lambda t: t + 1)
            pool.wait_ge(qa_ints, 1)
            pool.wait_ge(qa_k, KT)

            def split(dst, ints, scale, t1, t2):
                step(g.tensor_tensor(t1, ints, scale, ALU.mult))
                step(g.tensor_tensor(dst[0], ints, scale, ALU.mult))
                step(g.tensor_tensor(t2, t1, dst[0], ALU.subtract))
                step(g.tensor_tensor(dst[1], t1, dst[0], ALU.subtract))
                return g.tensor_tensor(dst[2], t2, dst[1], ALU.subtract)

            pool.wait_ge(qa_qt_zero, 1)

            def split_k(h):
                if h >= 1:
                    pool.wait_ge(qa_turned, qa_no["ka1", h - 1])
                split([qa_kt[:, :, j, :] for j in range(3)], qa_kint[:, :, h, 0:HD],
                      qa_sk[:, :, h].unsqueeze(2).broadcast_to([P, KT, HD]), qa_t1[:, :, :], qa_t2[:, :, :]
                      ).then_inc(qa_kt_made, 1)

            def split_q(h):
                if h >= 1:
                    pool.wait_ge(qa_turned, qa_no["qb", h - 1])
                split([qa_qt[:, :, j, 0:HD] for j in range(3)], qa_qint[:, :, h * HD:(h + 1) * HD],
                      qa_sq[:, :, h].unsqueeze(2).broadcast_to([P, TT, HD]), qa_t3[:, :, :], qa_t4[:, :, :]
                      ).then_inc(qa_qt_made, 1)

            def sum_chunk(h, c):
                n0 = h * EU + c * KT
                dst = qa_sum[c][:, :]
                if h >= 1:
                    pool.wait_ge(qa_pv, n0 - EU + KT)
                for k in range(1, POOLED):
                    pool.wait_ge(qa_exp, n0 + k + 1)
                    if k > 1:
                        pool.wait_ge(qa_added, (h * HALF + c) * (POOLED - 1) + k - 1)
                    g.tensor_tensor(dst, qa_e(n0) if k == 1 else dst, qa_e(n0 + k), ALU.add).then_inc(qa_added, 1)

            split_k(0)
            split_q(0)
            split_k(1)
            for h in range(HEADS):
                sum_chunk(h, 0)
                if h + 2 < HEADS:
                    split_k(h + 2)
                sum_chunk(h, 1)
                if h + 1 < HEADS:
                    split_q(h + 1)
            add_bias(2, ff_bias, x_turned[1], lambda t: t + 1)
            for t in range(TT):
                pool.wait_ge(y_added[3], t + 1)
                g.tensor_tensor(x_tok[:, t, :], x_tok[:, t, :], rc_beta[:, :], ALU.add).then_inc(rc_beta_in, 1)
            for i, (w, e) in enumerate(ME_HALVES):
                x, high, low = (t[w][:, e, :] for t in ((me_wg, me_w1), (me_wgh, me_w1h), (me_wgl, me_w1l)))
                pool.wait_ge(me_high, HALF + i + 1)
                g.tensor_tensor(low, x, high.bitcast(F32), ALU.subtract).then_inc(me_low, 1)


def kernel(**inputs):
    import numpy as np
    import concourse.bacc as bacc
    from concourse.bass_utils import run_bass_kernel_spmd

    a = {k: np.asarray(v) for k, v in inputs.items()}

    def tiles(w):
        return w.reshape(-1, P, w.shape[-1]).transpose(1, 0, 2)

    x = a["x"].reshape(TOK, D)
    ctx = a["ctx_2048"].reshape(KEYS, D)
    mask = a["mask_BxS2_bk0"].reshape(KEYS)
    lanes, cols = np.arange(P)[:, None], np.arange(SEQ)[None, :]
    past = cols - (SEQ - P) - lanes
    arrays = {
        "x_tok": tiles(x), "x_feat": tiles(x.T), "ctx": tiles(ctx.T),
        "ctx0": tiles(ctx[:CTX].T), "ctx1": tiles(ctx[CTX:].T),
        "ident": np.eye(P, dtype=np.float32),
        "decay": np.where(past > 0, -MASKED, -past).astype(np.float32),
        "sa_wq": tiles(a["L0_attn_q_w"].T), "sa_wk": tiles(a["L0_attn_k_w"].T),
        "sa_wv": tiles(a["L0_attn_v_w"].T), "sa_wo": tiles(a["L0_attn_o_w"].T),
        "q_b": a["L0_attn_q_b"].reshape(FT, P).T, "k_b": a["L0_attn_k_b"].reshape(FT, P).T,
        "sa_vb": a["L0_attn_v_b"], "sa_ob": a["L0_attn_o_b"],
        "qa_wq": tiles(a["L0_xattn_Wq"]), "qa_wkv": tiles(a["L0_xattn_Wkv"]), "qa_wp": tiles(a["L0_xattn_Wp"]),
        "qa_qb": a["L0_xattn_bq"], "qa_kb": a["L0_xattn_bkv"][:D], "qa_pb": a["L0_xattn_bp"],
        "qa_vb": a["L0_xattn_bkv"][D:].reshape(FT, P).T,
        "ff_a": tiles(a["L0_ffn_A"].reshape(ARROWS * RANK, D).T),
        "ff_b": tiles(a["L0_ffn_B"].transpose(0, 2, 1).reshape(ARROWS * RANK, D)),
        "ff_w": tiles(a["L0_ffn_W"].T), "ff_bias": a["L0_ffn_bias"],
        "rc_win": tiles(a["L1_attn_W_in"]), "rc_wout": a["L1_attn_W_out"],
        "rc_wf_d": a["L1_attn_W_fwd"][:, :DI], "rc_wf_g": a["L1_attn_W_fwd"][:, DI:],
        "rc_wb_d": a["L1_attn_W_bwd"][:, :DI], "rc_wb_g": a["L1_attn_W_bwd"][:, DI:],
        "rc_gamma": a["L1_attn_gamma"], "rc_beta": a["L1_attn_beta"],
        "ca_nw": a["L1_xattn_norm_w"], "ca_wq": tiles(a["L1_xattn_wq"].T), "ca_wk": tiles(a["L1_xattn_wk"].T),
        "ca_wv": tiles(a["L1_xattn_wv"].T), "ca_wo": tiles(a["L1_xattn_wo"].T), "ca_wg": tiles(a["L1_xattn_wg"].T),
        "mask_row": mask,
        "me_s1": tiles(a["L1_ffn_sw1"].T), "me_sg": tiles(a["L1_ffn_swg"].T), "me_s2": tiles(a["L1_ffn_sw2"].T),
        "me_wd": tiles(a["L1_ffn_Wdown"].T), "me_wu": a["L1_ffn_Wup"].T, "me_wr": tiles(a["L1_ffn_Wg"].T),
        "me_w1": a["L1_ffn_rw1"].transpose(2, 0, 1), "me_wg": a["L1_ffn_rwg"].transpose(2, 0, 1),
        "me_w2": tiles(a["L1_ffn_rw2"].transpose(0, 2, 1).reshape(EXPERTS * HID, LAT)),
        "me_bias": a["L1_ffn_biases"],
    }
    arrays = {f"in_{k}": np.ascontiguousarray(v) for k, v in arrays.items()}
    nc = bacc.Bacc("TRN2", target_bir_lowering=False, num_devices=1)
    dram = {k[3:]: nc.dram_tensor(k, v.shape, mybir.dt.from_np(v.dtype), kind="ExternalInput").ap()
            for k, v in arrays.items()}
    out = nc.dram_tensor("out_x", (TOK, D), F32, kind="ExternalOutput").ap()
    decoder_program(nc, dram, out)
    r = run_bass_kernel_spmd(nc, [arrays], core_ids=[0])
    return r.results[0]["out_x"].reshape(BATCH, SEQ, D)
```
